# Optimizing a Trainium2 kernel written in Bass

```python
import numpy as np
import jax
import jax.numpy as jnp

def _softmax(x, axis=-1):
    return jax.nn.softmax(x, axis=axis)

def _gelu(x):
    return jax.nn.gelu(x, approximate=True)

def _silu(x):
    return jax.nn.silu(x)

def _sigmoid(x):
    return jax.nn.sigmoid(x)

def _layernorm(x, axis=-1, eps=1e-05):
    m = jnp.mean(x, axis=axis, keepdims=True)
    v = jnp.var(x, axis=axis, keepdims=True)
    return (x - m) / jnp.sqrt(v + eps)

def _scatter_add(tgt, idx, src, axis=0):
    return tgt.at[idx].add(src)

def _segment_sum(src, seg, n):
    return jax.ops.segment_sum(src, seg, n)
kernel_name = 'mk_vit_tower_cls_d1_tok_img768_r4_720362'

def setup_inputs(seed: int=0):
    np.random.seed(seed)
    _w = jnp.asarray

    def _rec_inputs():
        import jax
        import jax.numpy as jnp
        _rk = jax.random.key(seed)
        x = -0.00016672 + 0.999947 * jax.random.normal(jax.random.fold_in(_rk, 1), (16, 3, 96, 96), jnp.float32)
        cls_tok = 0.02 * jax.random.normal(jax.random.fold_in(_rk, 5), (1, 1, 192), jnp.float32)
        return (x, cls_tok)
    x, cls_tok = _rec_inputs()

    def _L0_tok_setup():
        import jax, jax.numpy as jnp
        import numpy as np
        IMAGE_SIZE = 96
        PATCH = 16
        EMBED = 192
        NUM_PATCHES = (IMAGE_SIZE // PATCH) ** 2
        PATCH_DIM = PATCH * PATCH * 3

        def _patchify(x, patch):
            b, c, h, w = x.shape
            nh, nw = (h // patch, w // patch)
            x = x.reshape(b, c, nh, patch, nw, patch)
            x = x.transpose(0, 2, 4, 1, 3, 5)
            return x.reshape(b, nh * nw, c * patch * patch)
        key = jax.random.key(seed)
        k1, k2, k3, k4, k5 = jax.random.split(key, 5)
        x = jax.random.normal(k1, (64, 3, IMAGE_SIZE, IMAGE_SIZE), dtype=jnp.float32)
        W_emb = jax.random.normal(k2, (PATCH_DIM, EMBED), dtype=jnp.float32) * 0.02
        b_emb = jnp.zeros((EMBED,), dtype=jnp.float32)
        pos_embedding = jax.random.normal(k3, (1, NUM_PATCHES + 1, EMBED), dtype=jnp.float32) * 0.02
        cls_token = jax.random.normal(k4, (1, 1, EMBED), dtype=jnp.float32) * 0.02
        return {'x': x, 'W_emb': W_emb, 'b_emb': b_emb, 'pos_embedding': pos_embedding, 'cls_token': cls_token}
    _L0_tok_all = _L0_tok_setup()
    _L0_tok_in = {k: v for k, v in _L0_tok_all.items() if k in ('W_emb', 'b_emb', 'pos_embedding', 'cls_token')}
    del _L0_tok_all

    def _L0_attn_setup():
        import jax, jax.numpy as jnp
        import numpy as np
        N_HEADS = 12
        WINDOW = 12
        STRIDE = 3
        N_ANCHORS = 12
        EPS = 1e-06

        def fmap(x):
            return jax.nn.elu(x) + 1.0

        def _local_band(q, k, v, window):
            B, H, S, D = q.shape
            w = min(window, S)
            half = w // 2
            k_pad = jnp.pad(k, ((0, 0), (0, 0), (half, half), (0, 0)))
            v_pad = jnp.pad(v, ((0, 0), (0, 0), (half, half), (0, 0)))
            q_f = fmap(q)
            k_f = fmap(k_pad)
            idx = jnp.arange(S)[:, None] + jnp.arange(w)[None, :]
            k_unf = k_f[:, :, idx, :]
            v_unf = v_pad[:, :, idx, :]
            qk = jnp.einsum('bhsd,bhswd->bhsw', q_f, k_unf)
            out = jnp.einsum('bhsw,bhswd->bhsd', qk, v_unf)
            norm = jnp.clip(qk.sum(-1, keepdims=True), 1e-06, None)
            return out / norm

        def _stride_band(q, k, v, stride):
            k_s = fmap(k[:, :, ::stride])
            v_s = v[:, :, ::stride]
            q_f = fmap(q)
            kv = jnp.einsum('bhsd,bhse->bhde', k_s, v_s)
            out = jnp.einsum('bhsd,bhde->bhse', q_f, kv)
            k_sum = k_s.sum(axis=2)
            norm = jnp.clip(jnp.einsum('bhsd,bhd->bhs', q_f, k_sum)[..., None], 1e-06, None)
            return out / norm

        def _global_band(q, k, v, anchor_q, n_heads, n_anchors):
            B, H, S, D = q.shape
            aq = anchor_q.reshape(1, n_heads, n_anchors, D)
            aq = jnp.broadcast_to(aq, (B, n_heads, n_anchors, D))
            aq_f = fmap(aq)
            k_f = fmap(k)
            kv = jnp.einsum('bhsd,bhse->bhde', k_f, v)
            anchor_out = jnp.einsum('bhad,bhde->bhae', aq_f, kv)
            k_sum = k_f.sum(axis=2)
            anchor_norm = jnp.clip(jnp.einsum('bhad,bhd->bha', aq_f, k_sum)[..., None], 1e-06, None)
            anchor_out = anchor_out / anchor_norm
            q_f = fmap(q)
            anchor_k = fmap(aq)
            qk = jnp.einsum('bhsd,bhad->bhsa', q_f, anchor_k)
            out = jnp.einsum('bhsa,bhae->bhse', qk, anchor_out)
            qk_sum = jnp.clip(qk.sum(-1, keepdims=True), 1e-06, None)
            return out / qk_sum
        key = jax.random.key(seed)
        ks = jax.random.split(key, 4)
        B, S, D = (4, 512, 192)
        x = jax.random.normal(ks[0], (B, S, D), dtype=jnp.float32)
        qkv_w = jax.random.normal(ks[1], (3 * D, D), dtype=jnp.float32) * 0.02
        out_w = jax.random.normal(ks[2], (D, D), dtype=jnp.float32) * 0.02
        anchor_q = jax.random.normal(ks[3], (1, N_ANCHORS, D), dtype=jnp.float32) * 0.02
        w_local = jnp.float32(1.0 / 2.0)
        w_stride = jnp.float32(1.0 / 3.0)
        w_global = jnp.float32(1.0 / 6.0)
        return {'x': x, 'qkv_w': qkv_w, 'out_w': out_w, 'anchor_q': anchor_q, 'w_local': w_local, 'w_stride': w_stride, 'w_global': w_global}
    _L0_attn_all = _L0_attn_setup()
    _L0_attn_in = {k: v for k, v in _L0_attn_all.items() if k in ('qkv_w', 'out_w', 'anchor_q', 'w_local', 'w_stride', 'w_global')}
    del _L0_attn_all

    def _L0_ffn_setup():
        import jax, jax.numpy as jnp
        import numpy as np
        B, T, DM, DF, E, K = (4, 256, 192, 768, 8, 2)
        key = jax.random.key(seed)
        k0, k1, k2, k3 = jax.random.split(key, 4)
        x = jax.random.normal(k0, (B, T, DM), jnp.float32)
        Wg = jax.random.normal(k1, (DM, E), jnp.float32) * 0.02
        W1 = jax.random.normal(k2, (E, DM, DF), jnp.float32) * 0.02
        b1 = jnp.zeros((E, DF), jnp.float32)
        W2 = jax.random.normal(k3, (E, DF, DM), jnp.float32) * 0.02
        b2 = jnp.zeros((E, DM), jnp.float32)
        return {'x': x, 'Wg': Wg, 'W1': W1, 'b1': b1, 'W2': W2, 'b2': b2}
    _L0_ffn_all = _L0_ffn_setup()
    _L0_ffn_in = {k: v for k, v in _L0_ffn_all.items() if k in ('Wg', 'W1', 'b1', 'W2', 'b2')}
    del _L0_ffn_all
    return {'x': x, 'cls_tok': cls_tok, 'L0_tok_W_emb': _L0_tok_in['W_emb'], 'L0_tok_b_emb': _L0_tok_in['b_emb'], 'L0_tok_pos_embedding': _L0_tok_in['pos_embedding'], 'L0_tok_cls_token': _L0_tok_in['cls_token'], 'L0_attn_qkv_w': _L0_attn_in['qkv_w'], 'L0_attn_out_w': _L0_attn_in['out_w'], 'L0_attn_anchor_q': _L0_attn_in['anchor_q'], 'L0_attn_w_local': _L0_attn_in['w_local'], 'L0_attn_w_stride': _L0_attn_in['w_stride'], 'L0_attn_w_global': _L0_attn_in['w_global'], 'L0_ffn_Wg': _L0_ffn_in['Wg'], 'L0_ffn_W1': _L0_ffn_in['W1'], 'L0_ffn_b1': _L0_ffn_in['b1'], 'L0_ffn_W2': _L0_ffn_in['W2'], 'L0_ffn_b2': _L0_ffn_in['b2']}

def reference(x, cls_tok, L0_tok_W_emb, L0_tok_b_emb, L0_tok_pos_embedding, L0_tok_cls_token, L0_attn_qkv_w, L0_attn_out_w, L0_attn_anchor_q, L0_attn_w_local, L0_attn_w_stride, L0_attn_w_global, L0_ffn_Wg, L0_ffn_W1, L0_ffn_b1, L0_ffn_W2, L0_ffn_b2):
    import jax
    import jax.numpy as jnp

    def _L0_tok_ref(x, W_emb, b_emb, pos_embedding, cls_token):
        import jax, jax.numpy as jnp
        import numpy as np
        IMAGE_SIZE = 96
        PATCH = 16
        EMBED = 192
        NUM_PATCHES = (IMAGE_SIZE // PATCH) ** 2
        PATCH_DIM = PATCH * PATCH * 3

        def _patchify(x, patch):
            b, c, h, w = x.shape
            nh, nw = (h // patch, w // patch)
            x = x.reshape(b, c, nh, patch, nw, patch)
            x = x.transpose(0, 2, 4, 1, 3, 5)
            return x.reshape(b, nh * nw, c * patch * patch)
        b = x.shape[0]
        patches = _patchify(x, PATCH)
        tok = jnp.einsum('bnd,de->bne', patches, W_emb) + b_emb
        cls = jnp.broadcast_to(cls_token, (b, 1, EMBED))
        tok = jnp.concatenate([cls, tok], axis=1)
        return tok + pos_embedding[:, :tok.shape[1], :]

    def _L0_attn_ref(x, qkv_w, out_w, anchor_q, w_local, w_stride, w_global):
        import jax, jax.numpy as jnp
        import numpy as np
        N_HEADS = 12
        WINDOW = 12
        STRIDE = 3
        N_ANCHORS = 12
        EPS = 1e-06

        def fmap(x):
            return jax.nn.elu(x) + 1.0

        def _local_band(q, k, v, window):
            B, H, S, D = q.shape
            w = min(window, S)
            half = w // 2
            k_pad = jnp.pad(k, ((0, 0), (0, 0), (half, half), (0, 0)))
            v_pad = jnp.pad(v, ((0, 0), (0, 0), (half, half), (0, 0)))
            q_f = fmap(q)
            k_f = fmap(k_pad)
            idx = jnp.arange(S)[:, None] + jnp.arange(w)[None, :]
            k_unf = k_f[:, :, idx, :]
            v_unf = v_pad[:, :, idx, :]
            qk = jnp.einsum('bhsd,bhswd->bhsw', q_f, k_unf)
            out = jnp.einsum('bhsw,bhswd->bhsd', qk, v_unf)
            norm = jnp.clip(qk.sum(-1, keepdims=True), 1e-06, None)
            return out / norm

        def _stride_band(q, k, v, stride):
            k_s = fmap(k[:, :, ::stride])
            v_s = v[:, :, ::stride]
            q_f = fmap(q)
            kv = jnp.einsum('bhsd,bhse->bhde', k_s, v_s)
            out = jnp.einsum('bhsd,bhde->bhse', q_f, kv)
            k_sum = k_s.sum(axis=2)
            norm = jnp.clip(jnp.einsum('bhsd,bhd->bhs', q_f, k_sum)[..., None], 1e-06, None)
            return out / norm

        def _global_band(q, k, v, anchor_q, n_heads, n_anchors):
            B, H, S, D = q.shape
            aq = anchor_q.reshape(1, n_heads, n_anchors, D)
            aq = jnp.broadcast_to(aq, (B, n_heads, n_anchors, D))
            aq_f = fmap(aq)
            k_f = fmap(k)
            kv = jnp.einsum('bhsd,bhse->bhde', k_f, v)
            anchor_out = jnp.einsum('bhad,bhde->bhae', aq_f, kv)
            k_sum = k_f.sum(axis=2)
            anchor_norm = jnp.clip(jnp.einsum('bhad,bhd->bha', aq_f, k_sum)[..., None], 1e-06, None)
            anchor_out = anchor_out / anchor_norm
            q_f = fmap(q)
            anchor_k = fmap(aq)
            qk = jnp.einsum('bhsd,bhad->bhsa', q_f, anchor_k)
            out = jnp.einsum('bhsa,bhae->bhse', qk, anchor_out)
            qk_sum = jnp.clip(qk.sum(-1, keepdims=True), 1e-06, None)
            return out / qk_sum
        B, S, D = x.shape
        H = N_HEADS
        hd = D // H
        qkv = (x @ qkv_w.T).reshape(B, S, 3, H, hd)
        qkv = jnp.transpose(qkv, (2, 0, 3, 1, 4))
        q, k, v = (qkv[0], qkv[1], qkv[2])
        wn = jax.nn.softmax(jnp.stack([w_local, w_stride, w_global]))
        wl, ws, wg = (wn[0], wn[1], wn[2])
        out_local = _local_band(q, k, v, WINDOW)
        out_stride = _stride_band(q, k, v, STRIDE)
        out_global = _global_band(q, k, v, anchor_q, H, N_ANCHORS)
        out = wl * out_local + ws * out_stride + wg * out_global
        out = jnp.transpose(out, (0, 2, 1, 3)).reshape(B, S, D)
        return out @ out_w.T

    def _L0_ffn_ref(x, Wg, W1, b1, W2, b2):
        import jax, jax.numpy as jnp
        import numpy as np
        B, T, DM, DF, E, K = (4, 256, 192, 768, 8, 2)
        m = x.shape[-1]
        xs = x.reshape(-1, m)
        S = xs.shape[0]
        n_exp = W1.shape[0]
        logits = xs @ Wg
        probs = jax.nn.softmax(logits, axis=-1)
        topv, topi = jax.lax.top_k(probs, K)
        cw = topv / jnp.sum(topv, axis=-1, keepdims=True)
        combine_weights = cw.T
        eid_flat = topi.T.reshape(-1)
        dispatch_mask = jnp.argsort(eid_flat)
        e_sorted = eid_flat[dispatch_mask]
        dispatched = xs[dispatch_mask % S]
        expert_outputs = jnp.zeros_like(dispatched)
        for e in range(n_exp):
            sel = (e_sorted == e)[:, None].astype(dispatched.dtype)
            h = jax.nn.relu(dispatched @ W1[e] + b1[e])
            expert_outputs = expert_outputs + sel * (h @ W2[e] + b2[e])
        rerouted = jnp.zeros((S * K, m), expert_outputs.dtype).at[dispatch_mask].set(expert_outputs)
        rerouted = rerouted.reshape(K, S, m)
        combined = jnp.einsum('ks,ksm->sm', combine_weights, rerouted)
        return combined.reshape(x.shape).astype(x.dtype)
    h = _L0_tok_ref(x, L0_tok_W_emb, L0_tok_b_emb, L0_tok_pos_embedding, L0_tok_cls_token)
    h = jnp.concatenate([jnp.broadcast_to(cls_tok, (h.shape[0], 1, h.shape[2])), h], axis=1)
    h = h + _L0_attn_ref(_layernorm(h, axis=-1), L0_attn_qkv_w, L0_attn_out_w, L0_attn_anchor_q, L0_attn_w_local, L0_attn_w_stride, L0_attn_w_global)
    h = h + _L0_ffn_ref(_layernorm(h, axis=-1), L0_ffn_Wg, L0_ffn_W1, L0_ffn_b1, L0_ffn_W2, L0_ffn_b2)
    return h

_drawn_inputs = setup_inputs


def setup_inputs(seed=0):
    import zlib

    import numpy as np

    out = dict(_drawn_inputs(seed))
    spreads = {'L0_tok_b_emb': (0.0, 0.1), 'L0_ffn_b1': (0.0, 0.1), 'L0_ffn_b2': (0.0, 0.1)}
    factors = {}
    for name, (base, spread) in spreads.items():
        noise = np.random.default_rng([zlib.crc32(name.encode()), seed]).standard_normal(out[name].shape)
        drawn = base * np.exp(spread * noise) if base else spread * noise
        out[name] = jnp.asarray(drawn.astype(out[name].dtype))
    for name, factor in factors.items():
        out[name] = (out[name] * factor).astype(out[name].dtype)
    return out
```

```python
from contextlib import ExitStack

import numpy as np

import concourse.bass as bass
from concourse import mybir

F32 = mybir.dt.float32
F32R = mybir.dt.float32r
ALU = mybir.AluOpType
ACT = mybir.ActivationFunctionType
AX = mybir.AxisListType

IMAGES = 16
CH, SIDE, PATCH = 3, 96, 16
GRID = SIDE // PATCH
D = 192
SEQ = GRID * GRID + 2
TOK = IMAGES * SEQ
PER = 3
GTOK = PER * SEQ
GROUPS = -(-IMAGES // PER)
HALF = D // 2
HEADS, HD = 12, 16
HH = HEADS // 2
ANCH = 12
HA = HH * ANCH
WIN, STRIDE = 12, 3
NH2 = TOK // 2
KCH = CH * PATCH * PATCH // 128
E, DF = 8, 768
FCH = DF // 128
EPS_LN = 1e-5
EPS_DEN = 1e-6
ROWS = IMAGES * GRID


def group(g):
    n = min(PER, IMAGES - PER * g)
    return g * GTOK, n * SEQ, n


CONSTS = {
    "ident": (128, 128),
    "band": (GTOK + 1, GTOK),
    "blk": (HALF, HALF),
    "ablk": (HA, HALF),
    "vmask": (GTOK, 2 * PER),
    "tri": (GTOK, E * E),
}
OFF = {}
_at = 0
for _n, (_p, _c) in CONSTS.items():
    OFF[_n] = _at
    _at += _c
CONST_COLS = _at


def constants():
    c = np.zeros((128, CONST_COLS), np.float32)

    def put(name, a):
        p, n = CONSTS[name]
        c[:p, OFF[name]:OFF[name] + n] = a.reshape(p, n)

    put("ident", np.eye(128))
    j, s = np.arange(GTOK)[:, None], np.arange(GTOK)[None, :]
    same = j // SEQ == s // SEQ
    band = same & (j >= s - WIN // 2) & (j < s + WIN - WIN // 2)
    pos = np.arange(GTOK) % SEQ
    padded = np.maximum(0, WIN // 2 - pos) + np.maximum(0, pos + (WIN - WIN // 2) - SEQ)
    put("band", np.concatenate([band, padded[None]], 0))
    h = np.arange(HALF) // HD
    put("blk", h[:, None] == h[None, :])
    put("ablk", (np.arange(HA) // ANCH)[:, None] == h[None, :])
    img = (np.arange(GTOK) // SEQ)[:, None] == np.arange(PER)[None, :]
    strided = img & ((np.arange(GTOK) % SEQ % STRIDE) == 0)[:, None]
    put("vmask", np.stack([strided, img], 1))
    e = np.arange(E)
    put("tri", np.broadcast_to((e[:, None] > e[None, :])[None], (GTOK, E, E)))
    return c


def build(nc, x, cls_tok, w_emb, b_emb, pos_emb, cls0, qkv_w, out_w, anchor_q, w_loc, w_str, w_glo,
          wg, w1, b1, w2, b2, consts, out):
    with ExitStack() as ctx:
        def pool(stack):
            def sb(name, shape, dt=F32):
                return stack.enter_context(nc.sbuf_tensor(name, shape, dt))
            return sb

        def sem(name):
            return ctx.enter_context(nc.semaphore(name))

        ps = [ctx.enter_context(nc.psum_tensor(f"ps{i}", [128, 512], F32)) for i in range(8)]

        sb = pool(ctx)
        cst = sb("cst", [128, CONST_COLS])
        h = sb("h", [GTOK, GROUPS, D])
        h2 = sb("h2", [GTOK, GROUPS, D])
        stats = sb("stats", [GTOK, GROUPS, 6])
        mv = sb("mv", [GTOK, GROUPS, 2])
        rstd = sb("rstd", [GTOK, GROUPS])
        epsv = sb("epsv", [GTOK, 1])
        xn = sb("xn", [GTOK, GROUPS, D])
        wgs = sb("wgs", [HALF, 2, E])
        b2s = sb("b2s", [E, D])
        x2T = sb("x2T", [HALF + 1, 2, TOK])
        comb = sb("comb", [GTOK, GROUPS, E])
        w1raw = [sb(f"w1raw{i}", [HALF + 1, 2, DF]) for i in range(2)]
        w2raw = [sb(f"w2raw{i}", [128, FCH, D]) for i in range(2)]

        attn = ExitStack()
        sb = pool(attn)
        wT = sb("wT", [HALF, 2, 3 * D])
        woT = sb("woT", [HALF, 2, D])
        aqT = sb("aqT", [HA, 2, HH, HD])
        aq = sb("aq", [HALF, 2, HA])
        dg = sb("dg", [HALF, 2, HALF])
        wv = sb("wv", [HALF, 4])
        wvn = sb("wvn", [HALF, 4])
        anc = [sb(f"anc{i}", [HA, 2, HD]) for i in range(4)]
        xhT = sb("xhT", [HALF, 2, TOK])
        qkf = sb("qkf", [HALF, 4, TOK])
        emb = ExitStack()
        sb = pool(emb)
        ximg = sb("ximg", [ROWS, CH, PATCH, SIDE])
        xr = sb("xr", [ROWS, GRID, CH * PATCH, PATCH])
        wemb = sb("wemb", [128, KCH, D])
        xT = sb("xT", [128, KCH, TOK])
        qkvw = sb("qkvw", [HALF, 6, D])
        outw = sb("outw", [HALF, 2, D])
        posa = sb("posa", [GTOK, D])
        posb = sb("posb", [GTOK, D])
        hbase = sb("hbase", [GTOK, D])
        emb.close()
        sb = pool(attn)
        qkmin = sb("qkmin", [HALF, 2, NH2])
        qkexp = sb("qkexp", [HALF, 2, NH2])
        vtok = sb("vtok", [GTOK, GROUPS, D])
        vexp = sb("vexp", [GTOK, 2, HEADS, HALF])
        vm = sb("vm", [GTOK, 2, 2, 2 * PER, HALF])
        ktok = sb("ktok", [GTOK + 1, GROUPS, D])
        ksum = sb("ksum", [HALF, 2, 2, IMAGES])
        prod = sb("prod", [HALF, 2, 2, TOK])
        den = sb("den", [HALF, 2, 3, TOK])
        qs = sb("qs", [HALF, 2, 3, TOK])
        dena = sb("dena", [HA, 2, IMAGES])
        qas = sb("qas", [HA, 2, TOK])
        qlb = sb("qlb", [HALF, 2, 2, HH, GTOK])
        kvb = sb("kvb", [HALF, 2, 2, 2 * PER, HALF])
        at = sb("at", [GTOK, 2, HEADS, GTOK])
        oT = sb("oT", [HALF, 2, TOK])
        attn.close()

        moe = ctx.enter_context(ExitStack())
        sb = pool(moe)
        lg = sb("lg", [GTOK, GROUPS, E])
        lmax = sb("lmax", [GTOK, GROUPS])
        rank = sb("rank", [GTOK, GROUPS, E])
        cmpa = sb("cmpa", [GTOK, GROUPS, E, E])
        cmpb = sb("cmpb", [GTOK, GROUPS, E, E])
        xhi = sb("xhi", [HALF + 1, 2, TOK], F32R)
        xlo = sb("xlo", [HALF + 1, 2, TOK], F32R)
        cT = sb("cT", [E, TOK])
        w1hi = [sb(f"w1hi{i}", [HALF + 1, 2, DF], F32R) for i in range(2)]
        w1lo = [sb(f"w1lo{i}", [HALF + 1, 2, DF], F32R) for i in range(2)]
        w2hi = [sb(f"w2hi{i}", [128, FCH, D], F32R) for i in range(2)]
        w2lo = [sb(f"w2lo{i}", [128, FCH, D], F32R) for i in range(2)]
        hhi = sb("hhi", [128, FCH, TOK], F32R)
        hlo = sb("hlo", [128, FCH, TOK], F32R)
        res = sb("res", [GTOK, GROUPS, D])

        def const(name):
            p, n = CONSTS[name]
            return cst[:p, OFF[name]:OFF[name] + n]

        ident = const("ident")
        blk = const("blk")
        ablk = const("ablk")
        band = const("band")
        vmask = const("vmask")
        tri = const("tri")

        consts_in = sem("consts_in")
        x_in = sem("x_in")
        wemb_in, qkvw_in, outw_in, pos_in, anc_in, wv_in, wg_in = (
            sem(n) for n in ("wemb_in", "qkvw_in", "outw_in", "pos_in", "anc_in", "wv_in", "wg_in"))
        w_in = [sem(f"w_in{i}") for i in range(2)]
        out_done = sem("out_done")
        pe_wt, pe_xt, pe_emb, pe_xht, pe_qk, pe_v, pe_kt, pe_kb, pe_dl, pe_an, pe_qg = (
            sem("pe_" + n) for n in ("wt", "xt", "emb", "xht", "qk", "v", "kt", "kb", "dl", "an", "qg"))
        pe_kv, pe_sc, pe_o, pe_p, pe_x2t, pe_lg, pe_ct, pe_h, pe_y, pe_b2 = (
            sem("pe_" + n) for n in ("kv", "sc", "o", "p", "x2t", "lg", "ct", "h", "y", "b2"))
        dv = sem("dv")
        dv_var, dv_xr, dv_xt, dv_h, dv_xh, dv_min, dv_f, dv_prod, dv_den, dv_q, dv_qa, dv_qg, dv_kv, dv_at, dv_h2, dv_x2, dv_c, dv_lo, dv_y, dv_w, dv_pd, dv_cl = (
            sem("dv_" + n) for n in ("var", "xr", "xt", "h", "xh", "min", "f", "prod", "den", "q", "qa", "qg", "kv", "at", "h2", "x2", "c", "lo", "y", "w", "pd", "cl"))
        ac_root, ac_wt, ac_xr, ac_xt, ac_anc, ac_w, ac_xht, ac_exp, ac_v, ac_kt, ac_qlb, ac_o, ac_x2t, ac_hi, ac_whi, ac_ex, ac_ct, ac_x0 = (
            sem("ac_" + n) for n in ("root", "wt", "xr", "xt", "anc", "w", "xht", "exp", "v", "kt", "qlb", "o", "x2t", "hi", "whi", "ex", "ct", "x0"))
        gp = sem("gp")
        gp_comb, gp_eps, gp_zero, gp_base, gp_anc, gp_v, gp_whi, gp_wlo, gp_ones = (sem("gp_" + n) for n in ("comb", "eps", "zero", "base", "anc", "v", "whi", "wlo", "ones"))

        block = ctx.enter_context(nc.Block())

        def patches_of(wh, k):
            return xT[:, k, :].rearrange("p (b s) -> p b s", s=SEQ)[:, :, 2:SEQ].rearrange(
                "p b (i w) -> p w b i", w=GRID)[:, 3 * wh:3 * wh + 3]

        def turned(u):
            return ps[u % 4][:, 0:3 * ROWS].rearrange("p (w b i) -> p w b i", w=3, b=IMAGES)

        @block.sync
        def _(sp):
            sp.dma_start(cst[:], consts).then_inc(consts_in, 16)
            sp.dma_start(qkvw[:], qkv_w.rearrange("(r p) c -> p r c", p=HALF)).then_inc(qkvw_in, 16)
            for b in range(IMAGES):
                sp.dma_start(ximg[b * GRID:(b + 1) * GRID].rearrange("p c y w -> p c (y w)"),
                             x[b].rearrange("c (i y) w -> i c (y w)", y=PATCH)).then_inc(x_in, 16)
            sp.dma_start(wemb[:], w_emb.rearrange("(k p) c -> p k c", p=128)).then_inc(wemb_in, 16)
            sp.dma_start(outw[:], out_w.rearrange("(r p) c -> p r c", p=HALF)).then_inc(outw_in, 16)
            sp.wait_ge(gp_zero, 3)
            for e in range(E):
                if e >= 2:
                    sp.wait_ge(gp_wlo, e - 1)
                    sp.wait_ge(ac_whi, e - 1)
                s = e % 2
                sp.dma_start(w1raw[s][0:HALF], w1[e].rearrange("(i p) f -> p i f", p=HALF)).then_inc(w_in[s], 16)
                sp.dma_start(w1raw[s][HALF:HALF + 1, 1, :], b1[e:e + 1, :]).then_inc(w_in[s], 16)
                sp.dma_start(w2raw[s][:], w2[e].rearrange("(k p) c -> p k c", p=128)).then_inc(w_in[s], 16)
            flat = out.rearrange("b s d -> (b s) d")
            for g in range(GROUPS):
                t0, n, _ = group(g)
                sp.wait_ge(dv_y, GROUPS * (E - 1) + g + 1)
                sp.dma_start(flat[t0:t0 + n, :], res[0:n, g, :]).then_inc(out_done, 16)
            sp.wait_ge(out_done, 16 * GROUPS)

        @block.tensor
        def _(pe):
            pe.wait_ge(consts_in, 16)
            pe.wait_ge(qkvw_in, 16)
            for i in range(2):
                for r3 in range(2):
                    for r in range(3):
                        last = pe.transpose(ps[4 + 2 * i + r3][0:HALF, r * HALF:(r + 1) * HALF],
                                            qkvw[:, 3 * r3 + r, i * HALF:(i + 1) * HALF], ident[0:HALF, 0:HALF])
                    last.then_inc(pe_wt, 1)
            for u in range(2 * KCH):
                wh, k = u // KCH, u % KCH
                pe.wait_ge(dv_xr, 2 * wh + 2)
                pe.wait_ge(ac_xr, wh + 1)
                if u >= 4:
                    pe.wait_ge(dv_xt if u % 2 == 0 else ac_xt, (u - 4) // 2 + 1)
                for w in range(3):
                    last = pe.transpose(ps[u % 4][:, w * ROWS:(w + 1) * ROWS],
                                        xr[:, 3 * wh + w, 8 * k:8 * k + 8, :].rearrange("p y x -> p (y x)"),
                                        ident[0:ROWS, 0:ROWS])
                last.then_inc(pe_xt, 1)
            pe.wait_ge(ac_wt, 2)
            pe.wait_ge(outw_in, 16)
            for i in range(2):
                for r in range(2):
                    last = pe.transpose(ps[4][0:HALF, (2 * i + r) * HALF:(2 * i + r + 1) * HALF],
                                        outw[:, r, i * HALF:(i + 1) * HALF], ident[0:HALF, 0:HALF])
            last.then_inc(pe_wt, 1)
            pe.wait_ge(gp_anc, 2)
            for i in range(2):
                pe.transpose(ps[5][0:HALF, i * HA:(i + 1) * HA],
                             aqT[:, i].rearrange("p h d -> p (h d)"), ident[0:HA, 0:HA])
            for i in range(2):
                last = pe.matmul(ps[5][0:HALF, 192 + i * HALF:192 + (i + 1) * HALF],
                                 aqT[:, i].rearrange("p h d -> p (h d)"), ablk, start=True, stop=True)
            last.then_inc(pe_wt, 1)
            pe.wait_ge(wemb_in, 16)
            pe.wait_ge(dv_xt, KCH)
            pe.wait_ge(ac_xt, KCH)
            pe.wait_ge(gp_zero, 2)
            pe.wait_ge(ac_wt, 4)

            def xhat_turn(g):
                t0, n, _ = group(g)
                pe.wait_ge(dv_xh, g + 1)
                if g >= 2:
                    pe.wait_ge(ac_xht, g - 1)
                for i in range(2):
                    last = pe.transpose(ps[g % 2][0:HALF, i * GTOK:i * GTOK + n],
                                        xn[0:n, g, i * HALF:(i + 1) * HALF], ident[0:n, 0:n])
                last.then_inc(pe_xht, 1)

            for g in range(GROUPS + 2):
                if g < GROUPS:
                    t0, n, _ = group(g)
                    if g >= 2:
                        pe.wait_ge(dv_h, g - 1)
                    for k in range(KCH):
                        last = pe.matmul(ps[6 + g % 2][0:n, 0:D], xT[:, k, t0:t0 + n], wemb[:, k, :],
                                         start=(k == 0), stop=(k == KCH - 1))
                    last.then_inc(pe_emb, 1)
                if g >= 2:
                    xhat_turn(g - 2)
            pe.wait_ge(ac_wt, 6)
            for u in range(8):
                th, r = u // 4, u % 4
                if u == 0:
                    pe.wait_ge(ac_xht, 3)
                if u == 4:
                    pe.wait_ge(ac_xht, GROUPS)
                    for g in range(3):
                        pass
                if u >= 4:
                    pe.wait_ge(dv_f, u - 3)
                for i in range(2):
                    last = pe.matmul(ps[2 + r][0:HALF, 0:NH2], wT[:, i, r * HALF:(r + 1) * HALF],
                                     xhT[:, i, th * NH2:(th + 1) * NH2], start=(i == 0), stop=(i == 1))
                last.then_inc(pe_qk, 1)
            pe.wait_ge(dv_h, GROUPS)
            for g in range(GROUPS):
                t0, n, _ = group(g)
                if g >= 2:
                    pe.wait_ge(ac_v, g - 1)
                for i in range(2):
                    last = pe.matmul(ps[6 + g % 2][0:n, 0:D], xhT[:, i, t0:t0 + n], wT[:, i, 2 * D:3 * D],
                                     start=(i == 0), stop=(i == 1))
                last.then_inc(pe_v, 1)
            pe.wait_ge(dv_f, 8)
            for g in range(GROUPS):
                t0, n, _ = group(g)
                if g >= 2:
                    pe.wait_ge(ac_kt, g - 1)
                for i in range(2):
                    last = pe.transpose(ps[g % 2][0:n, i * HALF:(i + 1) * HALF],
                                        qkf[:, 2 + i, t0:t0 + n], ident[0:HALF, 0:HALF])
                last.then_inc(pe_kt, 1)
            pe.wait_ge(dv_pd, 2)
            for i in range(2):
                for th in range(2):
                    last = pe.matmul(ps[4 + 2 * i + th][0:HA, 0:NH2], aq[:, i, :],
                                     qkf[:, i, th * NH2:(th + 1) * NH2], start=True, stop=True)
                if i == 0:
                    pe.wait_ge(ac_v, GROUPS)
                last.then_inc(pe_an, 1)
            for i in range(2):
                last = pe.matmul(ps[3][0:HA, i * IMAGES:(i + 1) * IMAGES], aq[:, i, :], ksum[:, i, 0, :],
                                 start=True, stop=True)
            last.then_inc(pe_an, 1)
            for g in range(GROUPS):
                t0, n, _ = group(g)
                pe.wait_ge(ac_kt, GROUPS)
                if g >= 2:
                    pe.wait_ge(dv_prod, g - 1)
                for i in range(2):
                    last = pe.matmul(ps[(0, 2)[g % 2]][0:HALF, i * GTOK:i * GTOK + n], ktok[:, g, i * HALF:(i + 1) * HALF],
                                     band[:, 0:n], start=True, stop=True)
                last.then_inc(pe_kb, 1)
            pe.wait_ge(dv_pd, 4)
            pe.wait_ge(dv_prod, GROUPS)
            pe.wait_ge(dv_qa, 4)
            n_ = 0
            for i in range(2):
                for kind in range(3):
                    for th in range(2):
                        if n_ >= 6:
                            pe.wait_ge(dv_den, n_ - 5)
                        src = prod[:, i, kind, th * NH2:(th + 1) * NH2] if kind < 2 else qkf[:, i, th * NH2:(th + 1) * NH2]
                        pe.matmul(ps[n_ % 6][0:HALF, 0:NH2], blk if kind < 2 else dg[:, i, :], src,
                                  start=True, stop=True).then_inc(pe_dl, 1)
                        n_ += 1
            for i in range(2):
                for th in range(2):
                    m = 2 * i + th
                    if m >= 2:
                        pe.wait_ge(dv_qg, m - 1)
                    pe.matmul(ps[6 + th][0:HALF, 0:NH2], aqT[:, i].rearrange("p h d -> p (h d)"),
                              qas[:, i, th * NH2:(th + 1) * NH2], start=True, stop=True).then_inc(pe_qg, 1)
            pe.wait_ge(dv_den, 12)
            pe.wait_ge(dv_qg, 4)

            def keys_values(g):
                t0, n, imgs = group(g)
                pe.wait_ge(gp_v, 2 * g + 2)
                for i in range(2):
                    for kind in range(2):
                        m = 4 * g + 2 * i + kind
                        if m >= 2:
                            pe.wait_ge(dv_kv, m - 1)
                        pe.matmul(ps[m % 2][0:HALF, 0:imgs * HALF], ktok[0:n, g, i * HALF:(i + 1) * HALF],
                                  vm[0:n, g % 2, i, kind * PER:kind * PER + imgs, :],
                                  start=True, stop=True).then_inc(pe_kv, 1)

            def scores(g):
                t0, n, _ = group(g)
                pe.wait_ge(ac_qlb, g + 1)
                for q in range(4):
                    m = 4 * g + q
                    if m >= 2:
                        pe.wait_ge(dv_at, m - 1)
                    i = q // 2
                    pe.matmul(ps[2 + m % 2][0:n, 0:3 * n], qkf[:, 2 + i, t0:t0 + n],
                              qlb[:, g % 2, i, 3 * (q % 2):3 * (q % 2) + 3, 0:n],
                              start=True, stop=True).then_inc(pe_sc, 1)

            def outputs(g):
                t0, n, imgs = group(g)
                pe.wait_ge(dv_kv, 4 * g + 4)
                pe.wait_ge(dv_at, 4 * g + 4)
                for i in range(2):
                    if g >= 1:
                        pe.wait_ge(ac_o, 2 * g - 1 + i)
                    o = ps[4 + i]
                    for hh in range(HH):
                        pe.matmul(o[0:HALF, 0:n], vexp[0:n, g % 2, i * HH + hh, :], at[0:n, g % 2, i * HH + hh, 0:n],
                                  start=(hh == 0), stop=False, skip_group_check=True)
                    for kind in range(2):
                        for b in range(imgs):
                            last = pe.matmul(o[0:HALF, b * SEQ:(b + 1) * SEQ], kvb[:, g % 2, i, kind * PER + b, :],
                                             qs[:, i, 1 + kind, t0 + b * SEQ:t0 + (b + 1) * SEQ],
                                             start=False, stop=(kind == 1 and b == imgs - 1), skip_group_check=True)
                    last.then_inc(pe_o, 1)

            def project(g):
                t0, n, _ = group(g)
                pe.wait_ge(ac_o, 2 * g + 2)
                if g >= 1:
                    pe.wait_ge(dv_h2, g)
                for i in range(2):
                    last = pe.matmul(ps[6][0:n, 0:D], oT[:, i, t0:t0 + n], woT[:, i, :], start=(i == 0), stop=(i == 1))
                last.then_inc(pe_p, 1)

            def x2_turn(g):
                t0, n, _ = group(g)
                pe.wait_ge(dv_x2, g + 1)
                if g >= 1:
                    pe.wait_ge(ac_x2t, g)
                    pe.wait_ge(dv_cl, g)
                for i in range(2):
                    last = pe.transpose(ps[7][0:HALF, i * GTOK:i * GTOK + n],
                                        xn[0:n, g, i * HALF:(i + 1) * HALF], ident[0:n, 0:n])
                last.then_inc(pe_x2t, 1)
                pe.wait_ge(ac_x2t, g + 1)
                for i in range(2):
                    last = pe.matmul(ps[7][0:n, 256:256 + E], x2T[0:HALF, i, t0:t0 + n], wgs[:, i, :],
                                     start=(i == 0), stop=(i == 1))
                last.then_inc(pe_lg, 1)

            pe.wait_ge(wg_in, 32)
            for g in range(GROUPS + 2):
                if g < GROUPS:
                    keys_values(g)
                    scores(g)
                if g >= 1 and g - 1 < GROUPS:
                    outputs(g - 1)
                if g >= 2:
                    project(g - 2)
                    x2_turn(g - 2)
            pe.wait_ge(dv_c, 1)
            for g in range(GROUPS):
                t0, n, _ = group(g)
                last = pe.transpose(ps[g // 4][0:E, (g % 4) * GTOK:(g % 4) * GTOK + n], comb[0:n, g, :], ident[0:n, 0:n])
            last.then_inc(pe_ct, 1)

            def hidden(e, f):
                m = e * FCH + f
                s = e % 2
                if m >= 2:
                    pe.wait_ge(dv_lo, 2 * (m - 1))
                for th in range(2):
                    o = ps[4 + 2 * (m % 2) + th]
                    first = True
                    for i in range(2):
                        p = HALF + i
                        for wt, xx in ((w1hi, xhi), (w1hi, xlo), (w1lo, xhi)):
                            last = pe.matmul(o[:, 0:NH2], wt[s][0:p, i, f * 128:(f + 1) * 128],
                                             xx[0:p, i, th * NH2:(th + 1) * NH2], start=first,
                                             stop=(i == 1 and wt is w1lo))
                            first = False
                    last.then_inc(pe_h, 1)

            def down(e, g):
                t0, n, _ = group(g)
                s = e % 2
                m = e * GROUPS + g
                if m >= 4:
                    pe.wait_ge(dv_y, m - 3)
                first = True
                for k in range(FCH):
                    for hx, wt in ((hhi, w2hi), (hlo, w2hi), (hhi, w2lo)):
                        last = pe.matmul(ps[m % 4][0:n, 0:D], hx[:, k, t0:t0 + n], wt[s][:, k, :], start=first,
                                         stop=(k == FCH - 1 and wt is w2lo))
                        first = False
                last.then_inc(pe_y, 1)

            pe.wait_ge(ac_ct, 2)
            pe.wait_ge(dv_x2, GROUPS + 1)
            for g in range(GROUPS):
                t0, n, _ = group(g)
                if g >= 2:
                    pe.wait_ge(dv_y, 0) if False else None
                pe.matmul(ps[2 + g // 2][0:n, (g % 2) * 256:(g % 2) * 256 + D], cT[:, t0:t0 + n], b2s[:],
                          start=True, stop=True).then_inc(pe_b2, 1)
            pe.wait_ge(dv_w, GROUPS)
            for e in range(E):
                pe.wait_ge(gp_wlo, e + 1)
                pe.wait_ge(ac_whi, e + 1)
                for f in range(FCH):
                    hidden(e, f)
                pe.wait_ge(dv_lo, 2 * FCH * (e + 1))
                for g in range(GROUPS):
                    down(e, g)

        @block.vector
        def _(ve):
            links = [0]

            def link(ins):
                links[0] += 1
                ins.then_inc(dv, 1)
                ve.wait_ge(dv, links[0])

            ve.wait_ge(gp_zero, 1)
            ve.wait_ge(x_in, 16 * IMAGES)
            for w in (0, 2, 4, 5):
                ve.tensor_copy(xr[:, w], ximg[:, :, :, w * PATCH:(w + 1) * PATCH].rearrange("p c y x -> p (c y) x")).then_inc(dv_xr, 1)
            for u in range(0, 2 * KCH, 2):
                wh, k = u // KCH, u % KCH
                ve.wait_ge(pe_xt, u + 1)
                ve.tensor_copy(patches_of(wh, k), turned(u)).then_inc(dv_xt, 1)
            ve.wait_ge(wv_in, 48)
            link(ve.tensor_reduce(wv[:, 3:4], wv[:, 0:3], AX.X, ALU.max))
            ve.tensor_scalar(wvn[:, 0:3], wv[:, 0:3], wv[:, 3:4], None, ALU.subtract).then_inc(dv_w, 1) if False else link(
                ve.tensor_scalar(wvn[:, 0:3], wv[:, 0:3], wv[:, 3:4], None, ALU.subtract))
            links_w = links[0]
            ve.wait_ge(ac_w, 1)
            link(ve.tensor_reduce(wv[:, 3:4], wv[:, 0:3], AX.X, ALU.add))
            link(ve.reciprocal(wvn[:, 3:4], wv[:, 3:4]))
            link(ve.tensor_scalar(wvn[:, 0:3], wv[:, 0:3], wvn[:, 3:4], None, ALU.mult))
            ve.wait_ge(anc_in, 32)
            link(ve.tensor_scalar(anc[1][:], anc[0][:], 0.0, None, ALU.min))
            ve.wait_ge(ac_anc, 1)
            ve.scalar_tensor_tensor(anc[3][:], anc[0][:], 0.0, anc[2][:], ALU.max, ALU.add).then_inc(dv_pd, 1)

            def moments(g, n, src):
                link(ve.bn_stats(stats[0:n, g, :], src))
                ve.bn_aggr(mv[0:n, g, :], stats[0:n, g, :]).then_inc(dv_var, 1)

            def normalise(g, n, src, layer):
                ve.wait_ge(ac_root, GROUPS * layer + g + 1)
                link(ve.reciprocal(rstd[0:n, g:g + 1], rstd[0:n, g:g + 1]))
                return ve.tensor_scalar(xn[0:n, g, :], src, mv[0:n, g, 0:1], rstd[0:n, g:g + 1],
                                        ALU.subtract, ALU.mult)

            ve.wait_ge(gp_base, 1)
            for g in range(GROUPS + 1):
                if g < GROUPS:
                    t0, n, _ = group(g)
                    ve.wait_ge(pe_emb, g + 1)
                    ve.tensor_tensor(h[0:n, g, :], ps[6 + g % 2][0:n, 0:D], hbase[0:n, :], ALU.add).then_inc(dv_h, 1)
                    ve.wait_ge(dv_h, g + 1)
                    moments(g, n, h[0:n, g, :])
                if g >= 1:
                    t0, n, _ = group(g - 1)
                    normalise(g - 1, n, h[0:n, g - 1, :], 0).then_inc(dv_xh, 1)
            for u in range(8):
                th, r = u // 4, u % 4
                src = ps[2 + r][0:HALF, 0:NH2]
                ve.wait_ge(pe_qk, u + 1)
                if u >= 2:
                    ve.wait_ge(ac_exp, u - 1)
                ve.tensor_scalar(qkmin[:, u % 2, :], src, 0.0, None, ALU.min).then_inc(dv_min, 1)
                ve.wait_ge(ac_exp, u + 1)
                ve.scalar_tensor_tensor(qkf[:, r, th * NH2:(th + 1) * NH2], src, 0.0, qkexp[:, u % 2, :],
                                        ALU.max, ALU.add).then_inc(dv_f, 1)
            ve.wait_ge(dv_f, 8)
            for i in range(2):
                kk = qkf[:, 2 + i, :].rearrange("p (b s) -> p b s", s=SEQ)
                ve.tensor_reduce(ksum[:, i, 1, :], kk[:, :, 0:SEQ:STRIDE], AX.X, ALU.add).then_inc(dv, 1)
                links[0] += 1
                ins = ve.tensor_reduce(ksum[:, i, 0, :], kk, AX.X, ALU.add)
                ins.then_inc(dv_pd, 1) if i == 1 else link(ins)
            ve.wait_ge(dv, links[0])
            for i in range(2):
                ve.tensor_tensor(prod[:, i, 1, :].rearrange("p (b s) -> p b s", s=SEQ),
                                 qkf[:, i, :].rearrange("p (b s) -> p b s", s=SEQ),
                                 ksum[:, i, 1, :].unsqueeze(2).broadcast_to([HALF, IMAGES, SEQ]),
                                 ALU.mult).then_inc(dv_pd, 1)
            ve.wait_ge(pe_an, 3)
            link(ve.tensor_scalar(dena[:].rearrange("p a b -> p (a b)"), ps[3][0:HA, 0:2 * IMAGES], EPS_DEN, None, ALU.max))
            link(ve.reciprocal(dena[:], dena[:]))
            for i in range(2):
                for th in range(2):
                    nb = IMAGES // 2
                    ve.tensor_tensor(qas[:, i, th * NH2:(th + 1) * NH2].rearrange("p (b s) -> p b s", s=SEQ),
                                     ps[4 + 2 * i + th][0:HA, 0:NH2].rearrange("p (b s) -> p b s", s=SEQ),
                                     dena[:, i, th * nb:(th + 1) * nb].unsqueeze(2).broadcast_to([HA, nb, SEQ]),
                                     ALU.mult).then_inc(dv_qa, 1)
            for g in range(GROUPS):
                t0, n, _ = group(g)
                ve.wait_ge(pe_kb, g + 1)
                ve.tensor_tensor(prod[:, :, 0, t0:t0 + n],
                                 ps[(0, 2)[g % 2]][0:HALF, 0:2 * GTOK].rearrange("p (i t) -> p i t", i=2)[:, :, 0:n],
                                 qkf[:, 0:2, t0:t0 + n], ALU.mult).then_inc(dv_prod, 1)
            m = 0
            for i in range(2):
                for kind in range(3):
                    for th in range(2):
                        ve.wait_ge(pe_dl, m + 1)
                        ve.tensor_scalar(den[:, i, kind, th * NH2:(th + 1) * NH2], ps[m % 6][0:HALF, 0:NH2],
                                         EPS_DEN, None, ALU.max).then_inc(dv_den, 1)
                        m += 1
            for i in range(2):
                ve.wait_ge(dv_den, 6 * i + 6)
                link(ve.reciprocal(den[:, i], den[:, i]))
                for kind in range(2):
                    ve.scalar_tensor_tensor(qs[:, i, kind, :], den[:, i, kind, :], wvn[:, kind:kind + 1],
                                            qkf[:, i, :], ALU.mult, ALU.mult).then_inc(dv_q, 1)
            for i in range(2):
                for th in range(2):
                    sl = slice(th * NH2, (th + 1) * NH2)
                    ve.wait_ge(pe_qg, 2 * i + th + 1)
                    ve.scalar_tensor_tensor(qs[:, i, 2, sl], den[:, i, 2, sl], wvn[:, 2:3],
                                            ps[6 + th][0:HALF, 0:NH2], ALU.mult, ALU.mult).then_inc(dv_qg, 1)

            def keys_values(g):
                t0, n, imgs = group(g)
                if g >= 2:
                    ve.wait_ge(pe_o, 2 * (g - 1))
                for i in range(2):
                    for kind in range(2):
                        m = 4 * g + 2 * i + kind
                        ve.wait_ge(pe_kv, m + 1)
                        ve.tensor_tensor(kvb[:, g % 2, i, kind * PER:kind * PER + imgs, :],
                                         ps[m % 2][0:HALF, 0:imgs * HALF].rearrange("p (b c) -> p b c", c=HALF),
                                         blk.unsqueeze(1).broadcast_to([HALF, imgs, HALF]), ALU.mult).then_inc(dv_kv, 1)

            def scores(g):
                t0, n, _ = group(g)
                for q in range(4):
                    m = 4 * g + q
                    ve.wait_ge(pe_sc, m + 1)
                    ve.tensor_tensor(at[0:n, g % 2, 3 * q:3 * q + 3, 0:n],
                                     ps[2 + m % 2][0:n, 0:3 * n].rearrange("p (a s) -> p a s", a=3),
                                     band[0:n, 0:n].unsqueeze(1).broadcast_to([n, 3, n]), ALU.mult).then_inc(dv_at, 1)

            def residual(g):
                t0, n, _ = group(g)
                ve.wait_ge(pe_p, g + 1)
                ve.tensor_tensor(h2[0:n, g, :], ps[6][0:n, 0:D], h[0:n, g, :], ALU.add).then_inc(dv_h2, 1)
                ve.wait_ge(dv_h2, g + 1)
                moments(g, n, h2[0:n, g, :])
                normalise(g, n, h2[0:n, g, :], 1).then_inc(dv_x2, 1)

            def logits(g):
                t0, n, _ = group(g)
                ve.wait_ge(pe_lg, g + 1)
                if g == 0:
                    ve.wait_ge(gp_comb, 1)
                ve.tensor_copy(comb[0:n, g, :], ps[7][0:n, 256:256 + E]).then_inc(dv_cl, 1)

            for g in range(GROUPS + 2):
                if g < GROUPS:
                    keys_values(g)
                    scores(g)
                if g >= 2:
                    residual(g - 2)
                    logits(g - 2)
            ve.wait_ge(gp_comb, 1)
            ve.wait_ge(dv_cl, GROUPS)
            ve.wait_ge(pe_p, GROUPS)
            link(ve.tensor_copy(lg[:], comb[:]))
            mine = lg[:].unsqueeze(3).broadcast_to([GTOK, GROUPS, E, E])
            other = lg[:].unsqueeze(2).broadcast_to([GTOK, GROUPS, E, E])
            link(ve.tensor_tensor(cmpa[:], other, mine, ALU.is_equal))
            link(ve.tensor_tensor(cmpb[:], cmpa[:], tri.rearrange("p (a b) -> p a b", a=E).unsqueeze(1).broadcast_to(
                [GTOK, GROUPS, E, E]), ALU.mult))
            link(ve.tensor_tensor(cmpa[:], other, mine, ALU.is_gt))
            link(ve.tensor_tensor(cmpb[:], cmpb[:], cmpa[:], ALU.add))
            link(ve.tensor_reduce(rank[:], cmpb[:], AX.X, ALU.add))
            link(ve.tensor_reduce(lmax[:], lg[:], AX.X, ALU.max))
            link(ve.tensor_tensor(lg[:], lg[:], lmax[:].unsqueeze(2).broadcast_to([GTOK, GROUPS, E]), ALU.subtract))
            ve.wait_ge(dv_c, 0) if False else None
            ve.tensor_scalar(rank[:], rank[:], 2.0, None, ALU.is_lt).then_inc(dv_pd, 1)
            ve.wait_ge(dv_pd, 5)
            ve.wait_ge(ac_ex, 1)
            link(ve.tensor_tensor(comb[:], comb[:], rank[:], ALU.mult))
            link(ve.tensor_reduce(lmax[:], comb[:], AX.X, ALU.add))
            link(ve.reciprocal(lmax[:], lmax[:]))
            ve.tensor_tensor(comb[:], comb[:], lmax[:].unsqueeze(2).broadcast_to([GTOK, GROUPS, E]), ALU.mult).then_inc(dv_c, 1)
            ve.wait_ge(dv_c, 1)
            ve.wait_ge(ac_x0, 1)
            for i in range(2):
                p = HALF + i
                ins = ve.tensor_tensor(xlo[0:p, i, :], x2T[0:p, i, :], xhi[0:p, i, :].bitcast(F32), ALU.subtract)
                ins.then_inc(dv_x2, 1) if i == 1 else link(ins)
            for g in range(GROUPS):
                t0, n, _ = group(g)
                ve.wait_ge(pe_b2, 2 * (g // 2) + 2)
                ve.tensor_tensor(res[0:n, g, :], ps[2 + g // 2][0:n, (g % 2) * 256:(g % 2) * 256 + D],
                                 h2[0:n, g, :], ALU.add).then_inc(dv_w, 1)

            def low(m):
                f = m % FCH
                if f == 0 and m:
                    ve.wait_ge(pe_y, GROUPS * (m // FCH))
                for th in range(2):
                    sl = slice(th * NH2, (th + 1) * NH2)
                    ve.wait_ge(ac_hi, 2 * m + th + 1)
                    ve.scalar_tensor_tensor(hlo[:, f, sl], ps[4 + 2 * (m % 2) + th][:, 0:NH2], 0.0,
                                            hhi[:, f, sl].bitcast(F32), ALU.max, ALU.subtract).then_inc(dv_lo, 1)

            for e in range(E):
                for f in range(FCH):
                    low(e * FCH + f)
                for g in range(GROUPS):
                    t0, n, _ = group(g)
                    m = e * GROUPS + g
                    ve.wait_ge(pe_y, m + 1)
                    if e == 0:
                        ve.wait_ge(dv_w, GROUPS)
                    else:
                        ve.wait_ge(dv_y, m - GROUPS + 1)
                    ve.scalar_tensor_tensor(res[0:n, g, :], ps[m % 4][0:n, 0:D], comb[0:n, g, e:e + 1],
                                            res[0:n, g, :], ALU.mult, ALU.add).then_inc(dv_y, 1)
            for g in range(GROUPS):
                ve.wait_ge(dv_y, GROUPS * (E - 1) + g + 1)
                ve.nop().then_inc(dv_y, 1) if False else None
            ve.wait_ge(dv_y, GROUPS * E)

        @block.scalar
        def _(ac):
            for k, w in enumerate((w_loc, w_str, w_glo)):
                ac.dma_start(wv[:, k:k + 1], w.partition_broadcast(HALF)).then_inc(wv_in, 16)
            for i in range(2):
                ac.dma_start(anc[0][:, i, :], anchor_q.rearrange("o a (b d) -> (o a b) d", d=HD)[i * HA:(i + 1) * HA, :]).then_inc(anc_in, 16)
            ac.wait_ge(gp_base, 0) if False else None
            for b in range(PER):
                ac.dma_start(posa[b * SEQ:b * SEQ + 1, :], cls_tok.rearrange("a b d -> (a b) d")).then_inc(pos_in, 16)
                ac.dma_start(posa[b * SEQ + 1:(b + 1) * SEQ, :], pos_emb[0]).then_inc(pos_in, 16)
            ac.wait_ge(gp_zero, 4)
            for b in range(PER):
                ac.dma_start(posb[b * SEQ + 1:b * SEQ + 2, :], cls0.rearrange("a b d -> (a b) d")).then_inc(pos_in, 16)
                ac.dma_start(posb[b * SEQ + 2:(b + 1) * SEQ, :], b_emb.partition_broadcast(SEQ - 2)).then_inc(pos_in, 16)
            ac.dma_start(wgs[:], wg.rearrange("(i p) e -> p i e", p=HALF)).then_inc(wg_in, 16)
            ac.dma_start(b2s[:], b2).then_inc(wg_in, 16)
            ac.wait_ge(x_in, 16 * IMAGES)
            for w in (1, 3):
                ac.activation(xr[:, w], ximg[:, :, :, w * PATCH:(w + 1) * PATCH].rearrange("p c y x -> p (c y) x"),
                              ACT.Copy).then_inc(ac_xr, 1)
            for m in range(4):
                i, r3 = m // 2, m % 2
                ac.wait_ge(pe_wt, m + 1)
                ac.activation(wT[:, i, 288 * r3:288 * (r3 + 1)], ps[4 + m][0:HALF, 0:288], ACT.Copy).then_inc(ac_wt, 1)
            ac.wait_ge(gp_zero, 1)
            for u in range(1, 2 * KCH, 2):
                wh, k = u // KCH, u % KCH
                ac.wait_ge(pe_xt, u + 1)
                ac.activation(patches_of(wh, k), turned(u), ACT.Copy).then_inc(ac_xt, 1)
            ac.wait_ge(dv, 2)
            ac.activation(wv[:, 0:3], wvn[:, 0:3], ACT.Exp).then_inc(ac_w, 1)
            ac.wait_ge(dv, 6)
            ac.activation(anc[2][:], anc[1][:], ACT.Exp).then_inc(ac_anc, 1)
            ac.wait_ge(pe_wt, 5)
            ac.activation(woT[:].rearrange("p i c -> p (i c)"), ps[4][0:HALF, 0:2 * D], ACT.Copy).then_inc(ac_wt, 1)
            ac.wait_ge(pe_wt, 6)
            ac.activation(aq[:].rearrange("p i c -> p (i c)"), ps[5][0:HALF, 0:2 * HA], ACT.Copy).then_inc(ac_ct, 1)
            ac.activation(dg[:].rearrange("p i c -> p (i c)"), ps[5][0:HALF, 192:192 + 2 * HALF], ACT.Copy).then_inc(ac_wt, 1)

            ac.wait_ge(gp_eps, 1)

            def root(g, layer):
                t0, n, _ = group(g)
                ac.wait_ge(dv_var, GROUPS * layer + g + 1)
                ac.activation(rstd[0:n, g:g + 1], mv[0:n, g, 1:2], ACT.Sqrt, bias=epsv[0:n, :]).then_inc(ac_root, 1)

            for g in range(GROUPS + 1):
                if g < GROUPS:
                    root(g, 0)
                if g == 0:
                    continue
                g -= 1
                t0, n, _ = group(g)
                ac.wait_ge(pe_xht, g + 1)
                ac.activation(xhT[:, :, t0:t0 + n],
                              ps[g % 2][0:HALF, 0:2 * GTOK].rearrange("p (i t) -> p i t", i=2)[:, :, 0:n],
                              ACT.Copy).then_inc(ac_xht, 1)
            for u in range(8):
                ac.wait_ge(dv_min, u + 1)
                if u >= 2:
                    ac.wait_ge(dv_f, u - 1)
                ac.activation(qkexp[:, u % 2, :], qkmin[:, u % 2, :], ACT.Exp).then_inc(ac_exp, 1)
            for g in range(GROUPS):
                t0, n, _ = group(g)
                ac.wait_ge(pe_v, g + 1)
                ac.activation(vtok[0:n, g, :], ps[6 + g % 2][0:n, 0:D], ACT.Copy).then_inc(ac_v, 1)
            ac.wait_ge(gp_zero, 6)
            for g in range(GROUPS):
                t0, n, _ = group(g)
                ac.wait_ge(pe_kt, g + 1)
                ac.activation(ktok[0:n, g, :], ps[g % 2][0:n, 0:D], ACT.Copy).then_inc(ac_kt, 1)

            def spread(g):
                t0, n, _ = group(g)
                ac.wait_ge(dv_q, 4)
                if g >= 2:
                    ac.wait_ge(pe_sc, 4 * (g - 1))
                for i in range(2):
                    for hh in range(HH):
                        ins = ac.activation(qlb[:, g % 2, i, hh, 0:n], qs[:, i, 0, t0:t0 + n], ACT.Copy,
                                            scale=blk[:, hh * HD:hh * HD + 1])
                ins.then_inc(ac_qlb, 1)

            def heads_out(g):
                t0, n, _ = group(g)
                for i in range(2):
                    ac.wait_ge(pe_o, 2 * g + i + 1)
                    ac.activation(oT[:, i, t0:t0 + n], ps[4 + i][0:HALF, 0:n], ACT.Copy).then_inc(ac_o, 1)

            def x2_out(g):
                t0, n, _ = group(g)
                ac.wait_ge(pe_x2t, g + 1)
                ac.activation(x2T[0:HALF, :, t0:t0 + n],
                              ps[7][0:HALF, 0:2 * GTOK].rearrange("p (i t) -> p i t", i=2)[:, :, 0:n],
                              ACT.Copy).then_inc(ac_x2t, 1)

            for g in range(GROUPS + 2):
                if g < GROUPS:
                    spread(g)
                if g >= 1 and g - 1 < GROUPS:
                    heads_out(g - 1)
                if g >= 2:
                    root(g - 2, 1)
                    x2_out(g - 2)
            ac.wait_ge(dv_pd, 5)
            ac.activation(comb[:], lg[:], ACT.Exp).then_inc(ac_ex, 1)
            ac.wait_ge(ac_x2t, GROUPS)
            ac.wait_ge(gp_ones, 2)
            for i in range(2):
                p = HALF + i
                last = ac.activation(xhi[0:p, i, :], x2T[0:p, i, :], ACT.Copy)
                if i == 1:
                    last.then_inc(ac_x0, 1)
                else:
                    last.then_inc(ac_w, 1)
                    ac.wait_ge(ac_w, 2)
            ac.wait_ge(pe_ct, 1)
            ac.activation(cT[:, 0:4 * GTOK], ps[0][0:E, 0:4 * GTOK], ACT.Copy).then_inc(ac_w, 1)
            ac.wait_ge(ac_w, 3)
            ac.activation(cT[:, 4 * GTOK:TOK], ps[1][0:E, 0:TOK - 4 * GTOK], ACT.Copy).then_inc(ac_ct, 1)

            def weights_high(e):
                s = e % 2
                ac.wait_ge(w_in[s], 48 * (e // 2 + 1))
                if e >= 2:
                    ac.wait_ge(pe_y, GROUPS * (e - 1))
                for f in range(FCH):
                    ins = ac.activation(w2hi[s][:, f, :], w2raw[s][:, f, :], ACT.Copy)
                ac.activation(w1hi[s][:], w1raw[s][:], ACT.Copy).then_inc(ac_whi, 1)

            weights_high(0)
            for e in range(E):
                for f in range(FCH):
                    m = e * FCH + f
                    if f == 0 and m:
                        ac.wait_ge(pe_y, GROUPS * e)
                    for th in range(2):
                        ac.wait_ge(pe_h, 2 * m + th + 1)
                        ac.activation(hhi[:, f, th * NH2:(th + 1) * NH2], ps[4 + 2 * (m % 2) + th][:, 0:NH2],
                                      ACT.Relu).then_inc(ac_hi, 1)
                    if f == 0 and e + 1 < E:
                        weights_high(e + 1)

        @block.gpsimd
        def _(po):
            counts = {}

            def link(ins, signal=gp):
                counts[id(signal)] = counts.get(id(signal), 0) + 1
                ins.then_inc(signal, 1)
                po.wait_ge(signal, counts[id(signal)])

            link(po.memset(xT[:].rearrange("p k (b s) -> p k b s", s=SEQ)[:, :, :, 0:2], 0.0), gp_zero)
            link(po.memset(posb[:], 0.0), gp_zero)
            link(po.memset(epsv[:], EPS_LN), gp_eps)
            link(po.memset(comb[:], 0.0), gp_comb)
            for s in range(2):
                link(po.memset(w1raw[s][HALF:HALF + 1, 0, :], 0.0), gp_zero)
            po.wait_ge(pos_in, 16 * 12)
            link(po.tensor_tensor(hbase[:], posa[:], posb[:], ALU.add), gp_base)
            po.wait_ge(dv_pd, 1)
            po.wait_ge(consts_in, 16)
            for i in range(2):
                link(po.tensor_tensor(aqT[:, i], anc[3][:, i, :].unsqueeze(1).broadcast_to([HA, HH, HD]),
                                      ablk.rearrange("p (a d) -> p a d", d=HD), ALU.mult), gp_anc)
            po.wait_ge(pe_emb, GROUPS)
            po.wait_ge(dv_h, GROUPS)
            link(po.memset(ktok[:], 1.0), gp_zero)
            link(po.memset(vexp[:], 0.0), gp_zero)
            for g in range(GROUPS):
                t0, n, imgs = group(g)
                po.wait_ge(ac_v, g + 1)
                if g >= 2:
                    po.wait_ge(pe_o, 2 * (g - 1))
                for hh in range(HH):
                    link(po.tensor_copy(
                        vexp[0:n, g % 2].rearrange("p (i a) c -> p i a c", i=2)[:, :, hh, hh * HD:(hh + 1) * HD],
                        vtok[0:n, g].rearrange("p (i c) -> p i c", i=2)[:, :, hh * HD:(hh + 1) * HD]))
                for i in range(2):
                    v = vtok[0:n, g, i * HALF:(i + 1) * HALF]
                    link(po.tensor_tensor(vm[0:n, g % 2, i], v.unsqueeze(1).broadcast_to([n, 2 * PER, HALF]),
                                          vmask[0:n, :].unsqueeze(2).broadcast_to([n, 2 * PER, HALF]), ALU.mult), gp_v)
            for i in range(2):
                link(po.memset(x2T[HALF:HALF + 1, i, :], 1.0), gp_ones)
            for e in range(E):
                s = e % 2
                po.wait_ge(ac_whi, e + 1)
                if e >= 2:
                    po.wait_ge(pe_y, GROUPS * (e - 1))
                link(po.tensor_tensor(w2lo[s][:], w2raw[s][:], w2hi[s][:].bitcast(F32), ALU.subtract))
                link(po.tensor_tensor(w1lo[s][:], w1raw[s][:], w1hi[s][:].bitcast(F32), ALU.subtract), gp_wlo)


_INS = ["x", "cls_tok", "L0_tok_W_emb", "L0_tok_b_emb", "L0_tok_pos_embedding", "L0_tok_cls_token",
        "L0_attn_qkv_w", "L0_attn_out_w", "L0_attn_anchor_q", "L0_attn_w_local", "L0_attn_w_stride",
        "L0_attn_w_global", "L0_ffn_Wg", "L0_ffn_W1", "L0_ffn_b1", "L0_ffn_W2", "L0_ffn_b2"]


def kernel(**inputs):
    import concourse.bacc as bacc
    from concourse.bass_utils import run_bass_kernel_spmd

    nc = bacc.Bacc("TRN2", target_bir_lowering=False, num_devices=1)
    arrays, args = {}, []
    for name in _INS:
        a = np.ascontiguousarray(inputs[name])
        arrays[f"in_{name}"] = a
        args.append(nc.dram_tensor(f"in_{name}", a.shape, mybir.dt.from_np(a.dtype), kind="ExternalInput").ap())
    arrays["in_constants"] = constants()
    args.append(nc.dram_tensor("in_constants", (128, CONST_COLS), F32, kind="ExternalInput").ap())
    args.append(nc.dram_tensor("out", (IMAGES, SEQ, D), F32, kind="ExternalOutput").ap())
    build(nc, *args)
    r = run_bass_kernel_spmd(nc, [arrays], core_ids=[0])
    return r.results[0]["out"]
```

```python
from contextlib import ExitStack

import numpy as np

import concourse.bass as bass
from concourse import mybir

F32 = mybir.dt.float32
F32R = mybir.dt.float32r
I32 = mybir.dt.int32
U32 = mybir.dt.uint32
ALU = mybir.AluOpType
ACT = mybir.ActivationFunctionType
AX = mybir.AxisListType

IMAGES = 16
CH, SIDE, PATCH = 3, 96, 16
GRID = SIDE // PATCH
D = 192
SEQ = GRID * GRID + 2
TOK = IMAGES * SEQ
PER = 3
GTOK = PER * SEQ
GROUPS = -(-IMAGES // PER)
HALF = D // 2
HEADS, HD = 12, 16
HH = HEADS // 2
ANCH = 12
HA = HH * ANCH
WIN, STRIDE = 12, 3
NH2 = TOK // 2
KS = 4
KCH = CH * PATCH * PATCH // 128
E, DF = 8, 768
FCH = DF // 128
TOP = 2
SLOTS = 128
REGION = -(-TOK // SLOTS)
TILES = (TOP * TOK - E) // SLOTS + E
EMPTY = E * REGION
ROW = D + 2
PASS = DF // 2
AHEAD = 4
POOL_W1 = 3
NS = 6
EPS_LN = 1e-5
EPS_DEN = 1e-6
ROWS = IMAGES * GRID


def group(g):
    n = min(PER, IMAGES - PER * g)
    return g * GTOK, n * SEQ, n


CONSTS = {
    "ident": (128, 128),
    "band": (GTOK + 1, GTOK),
    "blk": (HALF, HALF),
    "ablk": (HA, HALF),
    "vmask": (GTOK, 2 * PER),
    "strided": (GTOK, GTOK),
    "tri": (GTOK, E * E),
    "before": (GTOK, GTOK),
    "region": (GTOK, E),
    "number": (128, GROUPS + 1),
    "repeat": (SEQ, GTOK),
    "full": (1, E * REGION),
    "tile": (1, TILES * E),
}
OFF = {}
_at = 0
for _n, (_p, _c) in CONSTS.items():
    OFF[_n] = _at
    _at += _c
CONST_COLS = _at


def constants():
    c = np.zeros((128, CONST_COLS), np.float32)

    def put(name, a):
        p, n = CONSTS[name]
        c[:p, OFF[name]:OFF[name] + n] = a.reshape(p, n)

    put("ident", np.eye(128))
    j, s = np.arange(GTOK)[:, None], np.arange(GTOK)[None, :]
    same = j // SEQ == s // SEQ
    band = same & (j >= s - WIN // 2) & (j < s + WIN - WIN // 2)
    pos = np.arange(GTOK) % SEQ
    padded = np.maximum(0, WIN // 2 - pos) + np.maximum(0, pos + (WIN - WIN // 2) - SEQ)
    put("band", np.concatenate([band, padded[None]], 0))
    h = np.arange(HALF) // HD
    put("blk", h[:, None] == h[None, :])
    put("ablk", (np.arange(HA) // ANCH)[:, None] == h[None, :])
    img = (np.arange(GTOK) // SEQ)[:, None] == np.arange(PER)[None, :]
    strided = img & ((np.arange(GTOK) % SEQ % STRIDE) == 0)[:, None]
    put("vmask", np.stack([strided, img], 1))
    put("strided", same & ((np.arange(GTOK) % SEQ % STRIDE) == 0)[:, None])
    e = np.arange(E)
    put("tri", np.broadcast_to((e[:, None] > e[None, :])[None], (GTOK, E, E)))
    put("before", j < s)
    put("region", np.broadcast_to(e * REGION * SLOTS, (GTOK, E)))
    put("number", np.concatenate([np.arange(128)[:, None] + np.arange(GROUPS) * GTOK,
                                  np.arange(128)[:, None] + TOK], 1))
    put("repeat", np.arange(SEQ)[:, None] == (np.arange(GTOK) % SEQ)[None, :])
    put("full", np.broadcast_to(np.arange(REGION) * SLOTS, (E, REGION)))
    put("tile", np.broadcast_to(np.arange(TILES)[:, None], (TILES, E)))
    return c


def build(nc, x, cls_tok, w_emb, b_emb, pos_emb, cls0, qkv_w, out_w, anchor_q, w_loc, w_str, w_glo,
          wg, w1, b1, w2, b2, consts, out):
    sent = nc.dram_tensor("sent", (EMPTY + 1, SLOTS, ROW), F32).ap()
    sums = nc.dram_tensor("sums", (TOK + SLOTS, D), F32).ap()
    with ExitStack() as ctx:
        def pool(stack):
            def sb(name, shape, dt=F32):
                return stack.enter_context(nc.sbuf_tensor(name, shape, dt))
            return sb

        def sem(name):
            return ctx.enter_context(nc.semaphore(name))

        ps = [ctx.enter_context(nc.psum_tensor(f"ps{i}", [128, 512], F32)) for i in range(8)]

        sb = pool(ctx)
        cst = sb("cst", [128, CONST_COLS])
        h = sb("h", [GTOK, GROUPS, D])
        stats = sb("stats", [GTOK, GROUPS, 6])
        mv = sb("mv", [GTOK, GROUPS, 2])
        rstd = sb("rstd", [GTOK, GROUPS])
        epsv = sb("epsv", [GTOK, 1])
        ones = sb("ones", [GTOK, 128])
        row = sb("row", [GTOK, GROUPS, TOP, ROW])
        blank = sb("blank", [SLOTS, ROW])
        wgs = sb("wgs", [HALF, 2, E])
        b2s = sb("b2s", [E, D])
        x2T = sb("x2T", [HALF, 2, 2, GTOK])
        woT = sb("woT", [HALF, 2, D])
        oT = sb("oT", [HALF, 2, 2, GTOK])
        comb = sb("comb", [GTOK, GROUPS, E])
        pair = sb("pair", [GTOK, GROUPS, TOP, E])
        rank = sb("rank", [GTOK, E])
        cmpa = sb("cmpa", [GTOK, E, E])
        cmpb = sb("cmpb", [GTOK, E, E])
        sel = sb("sel", [GTOK, GROUPS, TOP, E])
        both = sb("both", [GTOK, GROUPS, E])
        run = sb("run", [GTOK, GROUPS + 1, E])
        pick = sb("pick", [GTOK, TOP, E])
        best = sb("best", [GTOK, GROUPS, TOP])
        place = sb("place", [GTOK, TOP])
        index = sb("index", [GTOK, GROUPS, TOP], U32)
        diff = sb("diff", [GTOK, GROUPS, 3])
        w1s = sb("w1s", [HALF + 1, E, 2, DF])
        w2_ahead = ctx.enter_context(ExitStack())
        pool(w2_ahead)("w2_ahead", [128, AHEAD, FCH, D])

        attn = ExitStack()
        sb = pool(attn)
        wT = sb("wT", [HALF, 2, 3 * D])
        aqT = sb("aqT", [HA, 2, HH, HD])
        aq = sb("aq", [HALF, 2, HA])
        aqs = sb("aqs", [GTOK, D])
        wv = sb("wv", [GTOK, 4])
        wvn = sb("wvn", [GTOK, 4])
        anc = [sb(f"anc{i}", [HA, 2, HD]) for i in range(4)]
        hbase = sb("hbase", [GTOK, D])
        ktok = sb("ktok", [GTOK + 1, KS, D])
        XW = PER * (GTOK + SEQ)
        qx = sb("qx", [HALF, 2, 2, 2, XW])
        xhT = sb("xhT", [HALF, 2, TOK])
        emb = ExitStack()
        sb = pool(emb)
        ximg = sb("ximg", [ROWS, CH, PATCH, SIDE])
        xr = sb("xr", [ROWS, GRID, CH * PATCH, PATCH])
        wemb = sb("wemb", [128, KCH, D])
        xT = sb("xT", [128, KCH, TOK])
        qkvw = sb("qkvw", [HALF, 6, D])
        outw = sb("outw", [HALF, 2, D])
        posa = sb("posa", [SEQ, D])
        posb = sb("posb", [SEQ, D])
        xn = sb("xn", [GTOK, GROUPS, D])
        emb.close()
        sb = pool(attn)
        qkmin = sb("qkmin", [GTOK, 2 * D])
        qkexp = sb("qkexp", [GTOK, 2 * D])
        qtok = sb("qtok", [GTOK, 2, D])
        vtok = sb("vtok", [GTOK, 3, D])
        vexp = sb("vexp", [GTOK, 2, HEADS, HALF])
        vm = sb("vm", [GTOK, 2, 2, 2 * PER, HALF])
        kT = sb("kT", [HALF, 3, 2, GTOK])
        ksum = sb("ksum", [HALF, GROUPS, 2, PER])
        prod = sb("prod", [GTOK, 3, D])
        den = sb("den", [GTOK, 3, HEADS])
        qsc = sb("qsc", [GTOK, 2, 3, D])
        reca = sb("reca", [HA, 2, 2, PER])
        qgT = sb("qgT", [HALF, 2, 2, GTOK])
        qas = sb("qas", [HA, 2, 2, GTOK])
        qlb = sb("qlb", [HALF, 2, 2, HH, GTOK])
        kvb = sb("kvb", [HALF, 2, 2, 2 * PER, HALF])
        at = sb("at", [GTOK, 2, HEADS, GTOK])
        attn.close()
        w2_ahead.close()

        moe = ctx.enter_context(ExitStack())
        sb = pool(moe)
        w2s = sb("w2s", [128, E, FCH, D])
        w1hi = sb("w1hi", [HALF + 1, E, 2, DF], F32R)
        cT = sb("cT", [E, TOK])
        first = sb("first", [GTOK, GROUPS, D])
        full = sb("full", [1, E, REGION])
        tiles = sb("tiles", [1, 4, E])
        ge = sb("ge", [1, 2, TILES, E])
        tabf = sb("tabf", [1, 2, TILES])
        tab = sb("tab", [1, 2, TILES], I32)
        xs = sb("xs", [SLOTS, NS, ROW])
        xhi = sb("xhi", [HALF + 1, 2, 2, SLOTS], F32R)
        xlo = sb("xlo", [HALF + 1, 2, 2, SLOTS], F32R)
        hid = sb("hid", [SLOTS, DF])
        hidT = sb("hidT", [128, FCH, SLOTS])
        ys = sb("ys", [SLOTS, 2, D])

        def const(name):
            p, n = CONSTS[name]
            return cst[:p, OFF[name]:OFF[name] + n]

        ident = const("ident")
        blk = const("blk")
        ablk = const("ablk")
        band = const("band")
        vmask = const("vmask")
        tri = const("tri")
        strided = const("strided")
        before = const("before")

        ident_in = sem("ident_in")
        consts_in = sem("consts_in")
        x_in = sem("x_in")
        wemb_in, qkvw_in, outw_in, pos_in, anc_in, wv_in, wg_in = (
            sem(n) for n in ("wemb_in", "qkvw_in", "outw_in", "pos_in", "anc_in", "wv_in", "wg_in"))
        w1_in, w2_in, sent_blank, sent_in, sums_in, out_done = (
            sem(n) for n in ("w1_in", "w2_in", "sent_blank", "sent_in", "sums_in", "out_done"))
        added = sem("added")
        xs_in = [sem(f"xs_in{i}") for i in range(NS)]
        pe_wt, pe_xt, pe_emb, pe_xht, pe_qk, pe_v, pe_kt, pe_kb, pe_qt, pe_qa, pe_qg = (
            sem("pe_" + n) for n in ("wt", "xt", "emb", "xht", "qk", "v", "kt", "kb", "qt", "qa", "qg"))
        pe_kv, pe_sc, pe_o, pe_p, pe_x2t, pe_lg, pe_ct, pe_h, pe_y, pe_b2 = (
            sem("pe_" + n) for n in ("kv", "sc", "o", "p", "x2t", "lg", "ct", "h", "y", "b2"))
        pe_cnt, pe_tx, pe_th = (sem("pe_" + n) for n in ("cnt", "tx", "th"))
        dv = sem("dv")
        dv_wv, dv_anc, dv_var, dv_xr, dv_xt, dv_h, dv_xh = (
            sem("dv_" + n) for n in ("wv", "anc", "var", "xr", "xt", "h", "xh"))
        dv_min, dv_f, dv_ks, dv_kb, dv_da, dv_q, dv_qa, dv_kv, dv_at, dv_h2, dv_x2 = (
            sem("dv_" + n) for n in ("min", "f", "ks", "kb", "da", "q", "qa", "kv", "at", "h2", "x2"))
        dv_cl, dv_both, dv_diff, dv_row, dv_idx, dv_c, dv_first, dv_tab, dv_wlo, dv_xlo, dv_hid, dv_ht = (
            sem("dv_" + n) for n in ("cl", "both", "diff", "row", "idx", "c", "first", "tab", "wlo", "xlo", "hid", "ht"))
        ac_wt, ac_xr, ac_xt, ac_anc, ac_w, ac_root, ac_xht, ac_base = (
            sem("ac_" + n) for n in ("wt", "xr", "xt", "anc", "w", "root", "xht", "base"))
        ac_exp, ac_v, ac_kt, ac_qlb, ac_qx, ac_gt, ac_qg, ac_o, ac_x2t, ac_whi, ac_ex, ac_ct = (
            sem("ac_" + n) for n in ("exp", "v", "kt", "qlb", "qx", "gt", "qg", "o", "x2t", "whi", "ex", "ct"))
        ac_xhi, ac_hid, ac_ht, ac_y = (sem("ac_" + n) for n in ("xhi", "hid", "ht", "y"))
        gp = sem("gp")
        gp_sel, gp_eps, gp_zero, gp_base, gp_anc, gp_one, gp_att, gp_vx, gp_v, gp_blank, gp_row, gp_wlo = (
            sem("gp_" + n) for n in ("sel", "eps", "zero", "base", "anc", "one", "att", "vx", "v", "blank", "row", "wlo"))

        block = ctx.enter_context(nc.Block())

        def patches_of(wh, k):
            return xT[:, k, :].rearrange("p (b s) -> p b s", s=SEQ)[:, :, 2:SEQ].rearrange(
                "p b (i w) -> p w i b", w=GRID)[:, 3 * wh:3 * wh + 3]

        def turned(u):
            return ps[u % 4][:, 0:3 * ROWS].rearrange("p (w i b) -> p w i b", w=3, b=IMAGES)

        def own_columns(g, kind, imgs):
            return qx[:, g % 2, kind].rearrange("p i (b x) -> p i b x", x=GTOK + SEQ)[:, :, 0:imgs, 0:SEQ]

        def by_image(bank, n, imgs):
            return bank.rearrange("p (i t) -> p i t", i=2)[:, :, 0:n].rearrange("p i (b s) -> p i b s", s=SEQ)

        w1lo = w1s[:].bitcast(F32R)

        def embedding_over(engine):
            engine.wait_ge(pe_emb, GROUPS)
            engine.wait_ge(pe_xht, GROUPS)

        def attention_over(engine):
            engine.wait_ge(pe_o, GROUPS)

        @block.sync
        def _(sp):
            for i in range(GRID):
                sp.dma_start(ximg[i * IMAGES:(i + 1) * IMAGES].rearrange("p c y w -> p c (y w)"),
                             x.rearrange("b c (i y) w -> i b c (y w)", y=PATCH)[i]).then_inc(x_in, 16)
            sp.dma_start(wemb[:], w_emb.rearrange("(k p) c -> p k c", p=128)).then_inc(wemb_in, 16)
            sp.wait_ge(gp_zero, 2)
            sp.dma_start(posa[0:1, :], cls_tok.rearrange("a b d -> (a b) d")).then_inc(pos_in, 16)
            sp.dma_start(posa[1:SEQ, :], pos_emb[0]).then_inc(pos_in, 16)
            sp.dma_start(posb[1:2, :], cls0.rearrange("a b d -> (a b) d")).then_inc(pos_in, 16)
            sp.dma_start(posb[2:SEQ, :], b_emb.partition_broadcast(SEQ - 2)).then_inc(pos_in, 16)
            sp.dma_start(outw[:], out_w.rearrange("(r p) c -> p r c", p=HALF)).then_inc(outw_in, 16)
            sp.dma_start(wgs[:], wg.rearrange("(i p) e -> p i e", p=HALF)).then_inc(wg_in, 16)
            sp.dma_start(b2s[:], b2).then_inc(wg_in, 16)
            sp.wait_ge(x_in, 16 * GRID)
            sp.wait_ge(wemb_in, 16)
            for e in range(E):
                sp.dma_start(w1s[0:HALF, e], w1[e].rearrange("(i p) f -> p i f", p=HALF)).then_inc(w1_in, 16)
            sp.dma_start(w1s[HALF:HALF + 1, :, 1, :], b1.unsqueeze(0)).then_inc(w1_in, 16)
            sp.wait_ge(gp_blank, 1)
            sp.dma_start(sent.rearrange("r p c -> p r c"),
                         blank[:].unsqueeze(1).broadcast_to([SLOTS, EMPTY + 1, ROW])).then_inc(sent_blank, 16)
            sp.dma_start(sums[TOK:], blank[:, 0:D]).then_inc(sums_in, 16)

            def load_w2(e):
                sp.dma_start(w2s[:, e], w2[e].rearrange("(k p) c -> p k c", p=128)).then_inc(w2_in, 16)

            for e in range(AHEAD):
                load_w2(e)
            attention_over(sp)
            for e in range(AHEAD, E):
                load_w2(e)
            sp.wait_ge(dv_tab, 1)
            sp.wait_ge(sent_in, 16 * TOP * GROUPS)

            def load_tile(j):
                place_of = sp.value_load(tab[0:1, 1, j:j + 1], min_val=0, max_val=EMPTY)
                sp.dma_start(xs[:, j % NS, :], sent[bass.ds(place_of, 1)].rearrange("r p c -> p (r c)")).then_inc(xs_in[j % NS], 16)

            for j in range(NS):
                load_tile(j)
            for g in range(GROUPS):
                t0, n, _ = group(g)
                sp.wait_ge(dv_first, g + 1)
                sp.dma_start(sums[t0:t0 + n, :], first[0:n, g, :]).then_inc(sums_in, 16)
            for j in range(NS, TILES):
                sp.wait_ge(pe_tx, j - NS + 1)
                sp.wait_ge(added, 16 * (j - NS + 1))
                load_tile(j)
            sp.wait_ge(added, 16 * TILES)
            flat = out.rearrange("b s d -> (b s) d")
            sp.dma_start(flat.rearrange("(q r) c -> q (r c)", q=IMAGES),
                         sums[0:TOK].rearrange("(q r) c -> q (r c)", q=IMAGES)).then_inc(out_done, 16)
            sp.wait_ge(out_done, 16)

        @block.tensor
        def _(pe):
            pe.wait_ge(ident_in, 16)
            for u in range(2 * KCH):
                wh, k = u // KCH, u % KCH
                pe.wait_ge(dv_xr, 2 * wh + 2)
                pe.wait_ge(ac_xr, wh + 1)
                if u >= 4:
                    pe.wait_ge(dv_xt if u % 2 == 0 else ac_xt, (u - 4) // 2 + 1)
                for w in range(3):
                    last = pe.transpose(ps[u % 4][:, w * ROWS:(w + 1) * ROWS],
                                        xr[:, 3 * wh + w, 8 * k:8 * k + 8, :].rearrange("p y x -> p (y x)"),
                                        ident[0:ROWS, 0:ROWS])
                last.then_inc(pe_xt, 1)
            pe.wait_ge(qkvw_in, 16)
            for i in range(2):
                for r3 in range(2):
                    for r in range(3):
                        last = pe.transpose(ps[4 + 2 * i + r3][0:HALF, r * HALF:(r + 1) * HALF],
                                            qkvw[:, 3 * r3 + r, i * HALF:(i + 1) * HALF], ident[0:HALF, 0:HALF])
                    last.then_inc(pe_wt, 1)
            pe.wait_ge(consts_in, 16)
            pe.wait_ge(ac_wt, 4)
            pe.wait_ge(outw_in, 16)
            for i in range(2):
                for r in range(2):
                    last = pe.transpose(ps[4][0:HALF, (2 * i + r) * HALF:(2 * i + r + 1) * HALF],
                                        outw[:, r, i * HALF:(i + 1) * HALF], ident[0:HALF, 0:HALF])
            last.then_inc(pe_wt, 1)
            pe.wait_ge(gp_anc, 2)
            for i in range(2):
                last = pe.transpose(ps[5][0:HALF, i * HA:(i + 1) * HA],
                             aqT[:, i].rearrange("p h d -> p (h d)"), ident[0:HA, 0:HA])
            pe.wait_ge(pos_in, 64)
            for k, part in enumerate((posa, posb)):
                last = pe.matmul(ps[5][0:GTOK, 192:192 + D], const("repeat"), part[:], start=(k == 0), stop=(k == 1),
                                 skip_group_check=True)
            last.then_inc(pe_wt, 1)
            pe.wait_ge(gp_one, 1)
            for i in range(2):
                last = pe.matmul(ps[6][0:GTOK, i * HALF:(i + 1) * HALF], ones[0:HA, 0:GTOK],
                                 aqT[:, i].rearrange("p h d -> p (h d)"), start=True, stop=True)
            last.then_inc(pe_wt, 1)
            pe.wait_ge(wemb_in, 16)
            pe.wait_ge(dv_xt, KCH)
            pe.wait_ge(ac_xt, KCH)
            pe.wait_ge(gp_zero, 2)
            pe.wait_ge(ac_wt, 7)

            def xhat_turn(g):
                t0, n, _ = group(g)
                pe.wait_ge(dv_xh, g + 1)
                if g >= 2:
                    pe.wait_ge(ac_xht, g - 1)
                for i in range(2):
                    last = pe.transpose(ps[g % 2][0:HALF, i * GTOK:i * GTOK + n],
                                        xn[0:n, g, i * HALF:(i + 1) * HALF], ident[0:n, 0:n])
                last.then_inc(pe_xht, 1)

            for g in range(GROUPS + 2):
                if g < GROUPS:
                    t0, n, _ = group(g)
                    if g >= 2:
                        pe.wait_ge(dv_h, g - 1)
                    for k in range(KCH):
                        last = pe.matmul(ps[6 + g % 2][0:n, 0:D], xT[:, k, t0:t0 + n], wemb[:, k, :],
                                         start=(k == 0), stop=(k == KCH - 1))
                    last.then_inc(pe_emb, 1)
                if g >= 2:
                    xhat_turn(g - 2)

            def project_qkv(g):
                t0, n, _ = group(g)
                if g == 0:
                    pe.wait_ge(ac_xht, GROUPS)
                if g >= 2:
                    pe.wait_ge(ac_qx, g - 1)
                elif g == 1:
                    pe.wait_ge(dv_f, 1)
                if g >= 1:
                    pe.wait_ge(ac_kt, g)
                for i in range(2):
                    last = pe.matmul(ps[2][0:n, 0:2 * D], xhT[:, i, t0:t0 + n], wT[:, i, 0:2 * D],
                                     start=(i == 0), stop=(i == 1))
                last.then_inc(pe_qk, 1)
                for i in range(2):
                    last = pe.matmul(ps[3][0:n, 0:D], xhT[:, i, t0:t0 + n], wT[:, i, 2 * D:3 * D],
                                     start=(i == 0), stop=(i == 1))
                last.then_inc(pe_v, 1)

            def project_out(g):
                t0, n, _ = group(g)
                pe.wait_ge(ac_o, g + 1)
                pe.wait_ge(ac_qg, min(g + 2, GROUPS))
                for i in range(2):
                    last = pe.matmul(ps[0][0:n, 0:D], oT[:, g % 2, i, 0:n], woT[:, i, :], start=(i == 0), stop=(i == 1))
                last.then_inc(pe_p, 1)

            def outputs(g, i):
                t0, n, imgs = group(g)
                w = max(n, HALF)
                pe.wait_ge(dv_kv, 4 * g + 4)
                pe.wait_ge(dv_at, 4 * g + 4)
                pe.wait_ge(gp_vx, HH * (g + 1))
                pe.wait_ge(ac_qg, g + 1)
                if g >= 1:
                    pe.wait_ge(ac_o, g)
                o = ps[7][0:HALF, i * GTOK:i * GTOK + w]
                for hh in range(HH):
                    pe.matmul(o, vexp[0:n, g % 2, i * HH + hh, :], at[0:n, g % 2, i * HH + hh, 0:w],
                              start=(hh == 0), stop=False, skip_group_check=True)
                for kind in range(2):
                    for b in range(imgs):
                        last = pe.matmul(o, kvb[:, g % 2, i, kind * PER + b, :],
                                         qx[:, g % 2, kind, i, b * GTOK:b * GTOK + w],
                                         start=False, stop=(kind == 1 and b == imgs - 1), skip_group_check=True)
                if i == 1:
                    last.then_inc(pe_o, 1)

            def key_sums(g):
                t0, n, _ = group(g)
                pe.wait_ge(dv_f, g + 1)
                if g >= 1:
                    pe.wait_ge(dv_kb, g)
                pe.matmul(ps[4][0:n, 0:D], band[:, 0:n], ktok[:, g % KS, :], start=True, stop=True)
                pe.matmul(ps[4][0:n, D:2 * D], strided[0:n, 0:n], ktok[0:n, g % KS, :], start=True, stop=True).then_inc(pe_kb, 1)

            def turn_keys(g):
                t0, n, _ = group(g)
                pe.wait_ge(ac_v, g + 1)
                for i in range(2):
                    last = pe.transpose(ps[3][0:HALF, i * GTOK:i * GTOK + n], ktok[0:n, g % KS, i * HALF:(i + 1) * HALF],
                                        ident[0:n, 0:n])
                last.then_inc(pe_kt, 1)

            def turn_queries(g):
                t0, n, imgs = group(g)
                pe.wait_ge(dv_q, g + 1)
                pe.wait_ge(dv_f, min(g + 2, GROUPS))
                for kind in range(2):
                    for i in range(2):
                        c = (2 * kind + i) * GTOK
                        last = pe.transpose(ps[2][0:HALF, c:c + n], qsc[0:n, g % 2, kind, i * HALF:(i + 1) * HALF],
                                            ident[0:n, 0:n])
                last.then_inc(pe_qt, 1)
                if g >= 4:
                    pe.wait_ge(dv_cl, g - 3)
                for i in range(2):
                    last = pe.transpose(ps[1][0:HALF, i * GTOK:i * GTOK + n], qsc[0:n, g % 2, 2, i * HALF:(i + 1) * HALF],
                                        ident[0:n, 0:n])
                last.then_inc(pe_qt, 1)

            def through_anchors(g):
                t0, n, imgs = group(g)
                pe.wait_ge(ac_gt, g + 1)
                pe.wait_ge(dv_ks, g + 1)
                if g >= 1:
                    pe.wait_ge(ac_qg, g)
                if g >= 2:
                    pe.wait_ge(dv_h2, g - 1)
                for i in range(2):
                    pe.matmul(ps[0][0:HA, i * GTOK:i * GTOK + n], aq[:, i, :], qgT[:, g % 2, i, 0:n],
                              start=True, stop=True)
                for i in range(2):
                    last = pe.matmul(ps[0][0:HA, 256 + i * PER:256 + i * PER + imgs], aq[:, i, :], ksum[:, g, i, 0:imgs],
                                     start=True, stop=True)
                last.then_inc(pe_qa, 1)

            def keys_values(g, m):
                t0, n, imgs = group(g)
                i, kind = m // 2, m % 2
                pe.wait_ge(gp_v, 2 * g + i + 1)
                if 4 * g + m >= 1:
                    pe.wait_ge(dv_kv, 4 * g + m)
                pe.matmul(ps[5][0:HALF, 0:imgs * HALF], ktok[0:n, g % KS, i * HALF:(i + 1) * HALF],
                          vm[0:n, g % 2, i, kind * PER:kind * PER + imgs, :],
                          start=True, stop=True).then_inc(pe_kv, 1)

            def scores(g, m):
                t0, n, _ = group(g)
                i = m // 2
                pe.wait_ge(ac_kt, g + 1)
                pe.wait_ge(ac_qlb, g + 1)
                if 4 * g + m >= 1:
                    pe.wait_ge(dv_at, 4 * g + m)
                pe.matmul(ps[6][0:n, 0:3 * n], kT[:, g % 3, i, 0:n],
                          qlb[:, g % 2, i, 3 * (m % 2):3 * (m % 2) + 3, 0:n],
                          start=True, stop=True).then_inc(pe_sc, 1)

            def from_anchors(g):
                t0, n, _ = group(g)
                pe.wait_ge(dv_qa, 2 * (g + 1))
                for i in range(2):
                    last = pe.matmul(ps[0][0:HALF, i * GTOK:i * GTOK + n], aqT[:, i].rearrange("p h d -> p (h d)"),
                                     qas[:, g % 2, i, 0:n], start=True, stop=True)
                last.then_inc(pe_qg, 1)

            def x2_turn(g):
                t0, n, _ = group(g)
                pe.wait_ge(dv_x2, g + 1)
                pe.wait_ge(ac_gt, min(g + 4, GROUPS))
                if g >= 1:
                    pe.wait_ge(dv_cl, g)
                for i in range(2):
                    last = pe.transpose(ps[1][0:HALF, i * GTOK:i * GTOK + n],
                                        row[0:n, g, 0, i * HALF:(i + 1) * HALF], ident[0:n, 0:n])
                last.then_inc(pe_x2t, 1)

            def logits(g):
                t0, n, _ = group(g)
                pe.wait_ge(ac_x2t, g + 1)
                for i in range(2):
                    last = pe.matmul(ps[1][0:n, 256:256 + E], x2T[:, g % 2, i, 0:n], wgs[:, i, :],
                                     start=(i == 0), stop=(i == 1))
                if g == 0:
                    last.then_inc(pe_lg, 1)
                else:
                    places(g - 1)

            def places(g):
                t0, n, _ = group(g)
                if g == GROUPS - 1:
                    pe.wait_ge(dv_cl, GROUPS)
                pe.wait_ge(dv_both, 2 * g + 2)
                pe.matmul(ps[1][0:n, 256 + E:256 + 2 * E], before[0:n, 0:n], both[0:n, g, :], start=True, stop=False)
                pe.matmul(ps[1][0:n, 256 + E:256 + 2 * E], ones[:, 0:n], run[:, g, :],
                          start=False, stop=True).then_inc(pe_lg, 1)

            pe.wait_ge(wg_in, 32)
            for t in range(GROUPS + 5):
                if 0 <= t - 3 < GROUPS:
                    through_anchors(t - 3)
                for m in range(4):
                    if 0 <= t - 3 < GROUPS:
                        keys_values(t - 3, m)
                        scores(t - 3, m)
                    if m == 0 and 0 <= t - 1 < GROUPS:
                        key_sums(t - 1)
                        turn_keys(t - 1)
                    if m == 1 and 0 <= t - 2 < GROUPS:
                        turn_queries(t - 2)
                    if m < 2 and 0 <= t - 4 < GROUPS:
                        outputs(t - 4, m)
                    if m == 1 and 0 <= t - 5 < GROUPS:
                        x2_turn(t - 5)
                    if m == 2:
                        if 0 <= t - 3 < GROUPS:
                            from_anchors(t - 3)
                        if 0 <= t - 5 < GROUPS:
                            logits(t - 5)
                if 0 <= t - 4 < GROUPS:
                    project_out(t - 4)
                if t < GROUPS:
                    project_qkv(t)
            places(GROUPS - 1)
            pe.matmul(ps[0][0:1, 0:E], ones[:, 0:1], run[:, GROUPS, :], start=True, stop=True).then_inc(pe_cnt, 1)
            pe.wait_ge(dv_c, GROUPS)
            for g in range(GROUPS):
                t0, n, _ = group(g)
                last = pe.transpose(ps[4 + g // 4][0:E, (g % 4) * GTOK:(g % 4) * GTOK + n], comb[0:n, g, :], ident[0:n, 0:n])
            last.then_inc(pe_ct, 1)
            pe.wait_ge(ac_ct, 2)
            for g in range(GROUPS):
                t0, n, _ = group(g)
                pe.matmul(ps[(6, 7, 4)[g // 2]][0:n, (g % 2) * 256:(g % 2) * 256 + D], cT[:, t0:t0 + n], b2s[:],
                          start=True, stop=True).then_inc(pe_b2, 1)

            def turn_tokens(j):
                pe.wait_ge(xs_in[j % NS], 16 * (j // NS + 1))
                if j >= 2:
                    pe.wait_ge(dv_xlo, j - 1)
                for i in range(2):
                    last = pe.transpose(ps[j % 2][0:HALF, i * SLOTS:(i + 1) * SLOTS],
                                        xs[:, j % NS, i * HALF:(i + 1) * HALF], ident)
                last.then_inc(pe_tx, 1)

            def hidden(j, expert):
                pe.wait_ge(ac_xhi, j + 1)
                pe.wait_ge(dv_xlo, j + 1)
                for c in range(2):
                    if j >= 1:
                        pe.wait_ge(dv_hid if c else ac_hid, j)
                    first_product = True
                    for i in range(2):
                        p = HALF + i
                        for xx, ww in ((xhi, w1hi), (xlo, w1hi), (xhi, w1lo)):
                            last = pe.matmul(ps[2 + c][:, 0:PASS], xx[0:p, j % 2, i, :],
                                             ww[0:p, bass.ds(expert, 1), i, c * PASS:(c + 1) * PASS].rearrange("p e f -> p (e f)"),
                                             start=first_product, stop=(i == 1 and ww is w1lo))
                            first_product = False
                    last.then_inc(pe_h, 1)

            def turn_hidden(j):
                if j >= 1:
                    pe.wait_ge(ac_ht, j)
                    pe.wait_ge(dv_ht, j)
                for c in range(2):
                    pe.wait_ge(dv_hid if c else ac_hid, j + 1)
                    for k in range(3):
                        last = pe.transpose(ps[4 + c][:, k * 128:(k + 1) * 128],
                                            hid[:, (3 * c + k) * 128:(3 * c + k + 1) * 128], ident)
                    last.then_inc(pe_th, 1)

            def answers(j, expert):
                if j >= 2:
                    pe.wait_ge(ac_y, j - 1)
                pe.wait_ge(ac_ht, j + 1)
                pe.wait_ge(dv_ht, j + 1)
                for k in range(FCH):
                    last = pe.matmul(ps[6 + j % 2][:, 0:D], hidT[:, k, :],
                                     w2s[:, bass.ds(expert, 1), k, :].rearrange("p e c -> p (e c)"),
                                     start=(k == 0), stop=(k == FCH - 1))
                last.then_inc(pe_y, 1)

            pe.wait_ge(dv_tab, 1)
            turn_tokens(0)
            turn_tokens(1)
            pe.wait_ge(ac_whi, E)
            pe.wait_ge(dv_wlo, E - POOL_W1)
            pe.wait_ge(gp_wlo, POOL_W1)
            pe.wait_ge(w1_in, 16 * (E + 1))
            experts = {}
            for j in range(TILES + 1):
                if j < TILES:
                    experts[j] = pe.value_load(tab[0:1, 0, j:j + 1], min_val=0, max_val=E - 1)
                    hidden(j, experts[j])
                if j == 1:
                    pe.wait_ge(w2_in, 16 * E)
                if j >= 1:
                    answers(j - 1, experts[j - 1])
                if j + 2 < TILES:
                    turn_tokens(j + 2)
                if j == 0:
                    pe.wait_ge(dv_first, GROUPS)
                if j < TILES:
                    turn_hidden(j)

        @block.vector
        def _(ve):
            links = [0]

            def link(ins):
                links[0] += 1
                ins.then_inc(dv, 1)
                ve.wait_ge(dv, links[0])

            ve.wait_ge(wv_in, 48)
            link(ve.tensor_reduce(wv[:, 3:4], wv[:, 0:3], AX.X, ALU.max))
            ve.tensor_scalar(wvn[:, 0:3], wv[:, 0:3], wv[:, 3:4], None, ALU.subtract).then_inc(dv_wv, 1)
            ve.wait_ge(ac_w, 1)
            link(ve.tensor_reduce(wv[:, 3:4], wv[:, 0:3], AX.X, ALU.add))
            link(ve.reciprocal(wvn[:, 3:4], wv[:, 3:4]))
            link(ve.tensor_scalar(wvn[:, 0:3], wv[:, 0:3], wvn[:, 3:4], None, ALU.mult))
            ve.wait_ge(anc_in, 32)
            ve.tensor_scalar(anc[1][:], anc[0][:], 0.0, None, ALU.min).then_inc(dv_anc, 1)
            ve.wait_ge(ac_anc, 1)
            ve.scalar_tensor_tensor(anc[3][:], anc[0][:], 0.0, anc[2][:], ALU.max, ALU.add).then_inc(dv_anc, 1)
            ve.wait_ge(gp_zero, 1)
            ve.wait_ge(x_in, 16 * GRID)
            for w in (0, 2, 4, 5):
                ve.tensor_copy(xr[:, w], ximg[:, :, :, w * PATCH:(w + 1) * PATCH].rearrange("p c y x -> p (c y) x")).then_inc(dv_xr, 1)
            for u in range(0, 2 * KCH, 2):
                wh, k = u // KCH, u % KCH
                ve.wait_ge(pe_xt, u + 1)
                ve.tensor_copy(patches_of(wh, k), turned(u)).then_inc(dv_xt, 1)

            def moments(g, n, src):
                link(ve.bn_stats(stats[0:n, g, :], src))
                ve.bn_aggr(mv[0:n, g, :], stats[0:n, g, :]).then_inc(dv_var, 1)

            def normalise(g, n, src, dst, layer):
                ve.wait_ge(ac_root, GROUPS * layer + g + 1)
                link(ve.reciprocal(rstd[0:n, g:g + 1], rstd[0:n, g:g + 1]))
                return ve.tensor_scalar(dst, src, mv[0:n, g, 0:1], rstd[0:n, g:g + 1],
                                        ALU.subtract, ALU.mult)

            ve.wait_ge(ac_base, 1)
            for g in range(GROUPS + 1):
                if g < GROUPS:
                    t0, n, _ = group(g)
                    ve.wait_ge(pe_emb, g + 1)
                    ve.tensor_tensor(h[0:n, g, :], ps[6 + g % 2][0:n, 0:D], hbase[0:n, :], ALU.add).then_inc(dv_h, 1)
                    ve.wait_ge(dv_h, g + 1)
                    moments(g, n, h[0:n, g, :])
                if g >= 1:
                    t0, n, _ = group(g - 1)
                    normalise(g - 1, n, h[0:n, g - 1, :], xn[0:n, g - 1, :], 0).then_inc(dv_xh, 1)

            def features(g):
                t0, n, _ = group(g)
                src = ps[2][0:n, 0:2 * D]
                ve.wait_ge(pe_qk, g + 1)
                if g >= 1:
                    ve.wait_ge(ac_exp, g)
                ve.tensor_scalar(qkmin[0:n, :], src, 0.0, None, ALU.min).then_inc(dv_min, 1)
                ve.wait_ge(ac_exp, g + 1)
                if g >= 2:
                    ve.wait_ge(dv_q, g - 1)
                if g >= KS:
                    ve.wait_ge(pe_kv, 4 * (g - KS + 1))
                link(ve.scalar_tensor_tensor(qtok[0:n, g % 2, :], src[:, 0:D], 0.0, qkexp[0:n, 0:D], ALU.max, ALU.add))
                ve.scalar_tensor_tensor(ktok[0:n, g % KS, :], src[:, D:2 * D], 0.0, qkexp[0:n, D:2 * D],
                                        ALU.max, ALU.add).then_inc(dv_f, 1)

            def scaled_queries(g):
                t0, n, _ = group(g)
                ve.tensor_tensor(prod[0:n, 2, :], qtok[0:n, g % 2, :], aqs[0:n, :], ALU.mult).then_inc(dv, 1)
                links[0] += 1
                ve.wait_ge(pe_kb, g + 1)
                ve.tensor_tensor(prod[0:n, 0:2, :], ps[4][0:n, 0:2 * D].rearrange("p (a c) -> p a c", a=2),
                                 qtok[0:n, g % 2, :].unsqueeze(1).broadcast_to([n, 2, D]), ALU.mult).then_inc(dv_kb, 1)
                ve.wait_ge(dv, links[0])
                ve.wait_ge(dv_kb, g + 1)
                link(ve.tensor_reduce(den[0:n], prod[0:n].rearrange("p a (h d) -> p a h d", d=HD), AX.X, ALU.add))
                link(ve.tensor_scalar(den[0:n], den[0:n], EPS_DEN, None, ALU.max))
                link(ve.reciprocal(den[0:n], den[0:n]))
                link(ve.tensor_tensor(den[0:n], den[0:n], wvn[0:n, 0:3].unsqueeze(2).broadcast_to([n, 3, HEADS]), ALU.mult))
                if g >= 2:
                    ve.wait_ge(pe_qt, 2 * (g - 1))
                ve.tensor_tensor(qsc[0:n, g % 2].rearrange("p a (h d) -> p a h d", d=HD),
                                 qtok[0:n, g % 2, :].rearrange("p (h d) -> p h d", d=HD).unsqueeze(1).broadcast_to([n, 3, HEADS, HD]),
                                 den[0:n].unsqueeze(3).broadcast_to([n, 3, HEADS, HD]), ALU.mult).then_inc(dv_q, 1)

            def image_key_sums(g):
                t0, n, imgs = group(g)
                ve.wait_ge(ac_kt, g + 1)
                ve.tensor_reduce(ksum[:, g, :, 0:imgs], kT[:, g % 3, :, 0:n].rearrange("p i (b s) -> p i b s", s=SEQ),
                                 AX.X, ALU.add).then_inc(dv_ks, 1)

            def over_anchors(g):
                t0, n, imgs = group(g)
                r = reca[:, g % 2, :, 0:imgs]
                ve.wait_ge(pe_qa, g + 1)
                link(ve.tensor_scalar(r, ps[0][0:HA, 256:256 + 2 * PER].rearrange("p (i b) -> p i b", i=2)[:, :, 0:imgs],
                                      EPS_DEN, None, ALU.max))
                link(ve.reciprocal(r, r))
                if g >= 2:
                    ve.wait_ge(pe_qg, g - 1)
                for i in range(2):
                    ve.tensor_tensor(qas[:, g % 2, i, 0:n].rearrange("p (b s) -> p b s", s=SEQ),
                                     ps[0][0:HA, i * GTOK:i * GTOK + n].rearrange("p (b s) -> p b s", s=SEQ),
                                     r[:, i, :].unsqueeze(2).broadcast_to([HA, imgs, SEQ]), ALU.mult).then_inc(dv_qa, 1)

            def own_blocks(g, m):
                t0, n, imgs = group(g)
                if g >= 2:
                    ve.wait_ge(pe_o, g - 1)
                ve.wait_ge(pe_kv, 4 * g + m + 1)
                i, kind = m // 2, m % 2
                ve.tensor_tensor(kvb[:, g % 2, i, kind * PER:kind * PER + imgs, :],
                                 ps[5][0:HALF, 0:imgs * HALF].rearrange("p (b c) -> p b c", c=HALF),
                                 blk.unsqueeze(1).broadcast_to([HALF, imgs, HALF]), ALU.mult).then_inc(dv_kv, 1)

            def windows(g, m):
                t0, n, _ = group(g)
                ve.wait_ge(pe_sc, 4 * g + m + 1)
                ve.tensor_tensor(at[0:n, g % 2, 3 * m:3 * m + 3, 0:n],
                                 ps[6][0:n, 0:3 * n].rearrange("p (a s) -> p a s", a=3),
                                 band[0:n, 0:n].unsqueeze(1).broadcast_to([n, 3, n]), ALU.mult).then_inc(dv_at, 1)

            def residual(g):
                t0, n, _ = group(g)
                ve.wait_ge(pe_p, g + 1)
                ve.tensor_tensor(h[0:n, g, :], ps[0][0:n, 0:D], h[0:n, g, :], ALU.add).then_inc(dv_h2, 1)
                ve.wait_ge(dv_h2, g + 1)
                moments(g, n, h[0:n, g, :])

            def take_logits(g):
                if g < GROUPS:
                    t0, n, _ = group(g)
                    ve.wait_ge(pe_lg, g + 1)
                    ins = ve.tensor_copy(pair[0:n, g, 0, :], ps[1][0:n, 256:256 + E])
                if g >= 1:
                    if g < GROUPS:
                        link(ins)
                    n1 = group(g - 1)[1]
                    ve.wait_ge(pe_lg, g + 1)
                    ins = ve.tensor_tensor(pair[0:n1, g - 1, 1, :], ps[1][0:n1, 256 + E:256 + 2 * E],
                                           const("region")[0:n1, :], ALU.add)
                ins.then_inc(dv_cl, 1)

            def route(g):
                ve.wait_ge(dv_cl, g + 1)
                if g < GROUPS:
                    t0, n, _ = group(g)
                    mine = pair[0:n, g, 0, :].unsqueeze(2).broadcast_to([n, E, E])
                    other = pair[0:n, g, 0, :].unsqueeze(1).broadcast_to([n, E, E])
                    link(ve.tensor_tensor(cmpa[0:n], other, mine, ALU.is_equal))
                    link(ve.tensor_tensor(cmpb[0:n], cmpa[0:n], tri[0:n].rearrange("p (a b) -> p a b", a=E), ALU.mult))
                    link(ve.tensor_tensor(cmpa[0:n], other, mine, ALU.is_gt))
                    link(ve.tensor_tensor(cmpb[0:n], cmpb[0:n], cmpa[0:n], ALU.add))
                    link(ve.tensor_reduce(rank[0:n], cmpb[0:n], AX.X, ALU.add))
                    ve.tensor_scalar(both[0:n, g, :], rank[0:n], float(TOP), None, ALU.is_lt).then_inc(dv_both, 1)
                    for k in range(TOP):
                        link(ve.tensor_scalar(sel[0:n, g, k, :], rank[0:n], float(k), None, ALU.is_equal))
                    ve.wait_ge(dv_both, 2 * g + 1)
                    ve.tensor_tensor(run[:, g + 1, :], run[:, g, :], both[:, g, :], ALU.add).then_inc(dv_both, 1)
                    ve.wait_ge(dv_both, 2 * g + 2)
                    link(ve.tensor_tensor(pick[0:n], sel[0:n, g], pair[0:n, g, 0:1, :].broadcast_to([n, TOP, E]), ALU.mult))
                    link(ve.tensor_reduce(best[0:n, g, :], pick[0:n], AX.X, ALU.add))
                    ve.tensor_tensor(diff[0:n, g, 0:1], best[0:n, g, 1:2], best[0:n, g, 0:1], ALU.subtract).then_inc(dv_diff, 1)
                    ve.wait_ge(dv_diff, g + 1)
                if g >= 1:
                    send(g - 1)

            def send(g):
                t0, n, _ = group(g)
                link(ve.tensor_tensor(pick[0:n], sel[0:n, g], pair[0:n, g, 1:2, :].broadcast_to([n, TOP, E]), ALU.mult))
                link(ve.tensor_reduce(place[0:n, :], pick[0:n], AX.X, ALU.add))
                link(ve.tensor_copy(index[0:n, g, :], place[0:n, :]))
                ve.wait_ge(ac_ex, g + 1)
                link(ve.tensor_scalar(diff[0:n, g, 2:3], diff[0:n, g, 1:2], 1.0, None, ALU.add))
                link(ve.reciprocal(row[0:n, g, 0, D:D + 1], diff[0:n, g, 2:3]))
                ve.wait_ge(gp_row, g + 1)
                link(ve.tensor_tensor(row[0:n, g, 1, D:D + 1], row[0:n, g, 0, D:D + 1], diff[0:n, g, 1:2], ALU.mult))
                ve.tensor_copy(row[0:n, g, :, D + 1].bitcast(U32),
                               const("number")[0:n, g:g + 1].broadcast_to([n, TOP])).then_inc(dv_row, 1)
                ve.wait_ge(dv_row, g + 1)
                link(ve.tensor_scalar(pick[0:n, 0, :], sel[0:n, g, 0, :], row[0:n, g, 0, D:D + 1], None, ALU.mult))
                ve.scalar_tensor_tensor(comb[0:n, g, :], sel[0:n, g, 1, :], row[0:n, g, 1, D:D + 1], pick[0:n, 0, :],
                                        ALU.mult, ALU.add).then_inc(dv_c, 1)
                ve.wait_ge(dv_c, g + 1)

            ve.wait_ge(gp_sel, 2)
            ve.wait_ge(consts_in, 16)
            ve.wait_ge(gp_att, 1)
            embedding_over(ve)
            for t in range(GROUPS + 5):
                for m in range(4):
                    if 0 <= t - 3 < GROUPS:
                        own_blocks(t - 3, m)
                        windows(t - 3, m)
                    if m == 0:
                        if 0 <= t - 3 < GROUPS:
                            over_anchors(t - 3)
                        if 0 <= t - 5 < GROUPS:
                            g = t - 5
                            n = group(g)[1]
                            normalise(g, n, h[0:n, g, :], row[0:n, g, 0, 0:D], 1).then_inc(dv_x2, 1)
                        if 0 <= t - 1 < GROUPS:
                            scaled_queries(t - 1)
                            image_key_sums(t - 1)
                    if m == 1 and 0 <= t - 6 < GROUPS:
                        route(t - 6)
                if 0 <= t - 4 < GROUPS:
                    residual(t - 4)
                if 0 <= t - 5 < GROUPS:
                    take_logits(t - 5)
                if t < GROUPS:
                    features(t)
            route(GROUPS - 1)
            take_logits(GROUPS)
            route(GROUPS)
            ve.wait_ge(pe_cnt, 1)
            attention_over(ve)
            count, start, end, rest = (tiles[:, k, :] for k in range(4))
            link(ve.tensor_tensor(full[:], ps[0][0:1, 0:E].unsqueeze(2).broadcast_to([1, E, REGION]),
                                  const("full").rearrange("p (e r) -> p e r", e=E), ALU.is_gt))
            link(ve.tensor_reduce(count, full[:], AX.X, ALU.add))
            link(ve.tensor_tensor(ge[:, 0, 0:E, :], count.unsqueeze(1).broadcast_to([1, E, E]),
                                  tri[0:1].rearrange("p (a b) -> p a b", a=E), ALU.mult))
            link(ve.tensor_reduce(start, ge[:, 0, 0:E, :], AX.X, ALU.add))
            link(ve.tensor_tensor(end, start, count, ALU.add))
            link(ve.tensor_scalar(rest, count, -1.0, float(REGION), ALU.mult, ALU.add))
            number = const("tile").rearrange("p (j e) -> p j e", e=E)
            link(ve.tensor_tensor(ge[:, 0], number, end.unsqueeze(1).broadcast_to([1, TILES, E]), ALU.is_ge))
            link(ve.tensor_tensor(ge[:, 1], ge[:, 0], rest.unsqueeze(1).broadcast_to([1, TILES, E]), ALU.mult))
            link(ve.tensor_reduce(tabf[:], ge[:], AX.X, ALU.add))
            link(ve.tensor_tensor(tabf[:, 1, :], tabf[:, 1, :], number[:, :, 0], ALU.add))
            link(ve.tensor_scalar(tabf[:, 0, :], tabf[:, 0, :], float(E - 1), None, ALU.min))
            link(ve.tensor_scalar(tabf[:, 1, :], tabf[:, 1, :], float(EMPTY), None, ALU.min))
            ve.tensor_copy(tab[:], tabf[:]).then_inc(dv_tab, 1)
            for s in range(2):
                link(ve.tensor_copy(xhi[HALF:HALF + 1, s, 1, :], ones[HALF:HALF + 1, :]))
                link(ve.tensor_scalar(xlo[HALF:HALF + 1, s, 1, :], ones[HALF:HALF + 1, :], 0.0, None, ALU.mult))
            for e in range(E - POOL_W1):
                ve.wait_ge(ac_whi, POOL_W1 + e + 1)
                e += POOL_W1
                ve.tensor_tensor(w1lo[:, e], w1s[:, e], w1hi[:, e].bitcast(F32), ALU.subtract).then_inc(dv_wlo, 1)

            def tokens_low(j):
                ve.wait_ge(ac_xhi, j + 1)
                if j >= 2:
                    ve.wait_ge(pe_h, 2 * (j - 1))
                ve.tensor_tensor(xlo[0:HALF, j % 2], ps[j % 2][0:HALF, 0:2 * SLOTS].rearrange("p (i t) -> p i t", i=2),
                                 xhi[0:HALF, j % 2].bitcast(F32), ALU.subtract).then_inc(dv_xlo, 1)

            tokens_low(0)
            tokens_low(1)
            for g in range(GROUPS):
                t0, n, _ = group(g)
                ve.wait_ge(pe_b2, 2 * (g // 2) + 2)
                ve.tensor_tensor(first[0:n, g, :], ps[(6, 7, 4)[g // 2]][0:n, (g % 2) * 256:(g % 2) * 256 + D],
                                 h[0:n, g, :], ALU.add).then_inc(dv_first, 1)
            for j in range(TILES):
                ve.wait_ge(pe_h, 2 * j + 2)
                if j >= 1:
                    ve.wait_ge(pe_th, 2 * j)
                ve.tensor_scalar(hid[:, PASS:DF], ps[3][:, 0:PASS], 0.0, None, ALU.max).then_inc(dv_hid, 1)
                if j + 2 < TILES:
                    tokens_low(j + 2)
                ve.wait_ge(pe_th, 2 * j + 2)
                if j >= 1:
                    ve.wait_ge(pe_y, j)
                ve.tensor_copy(hidT[:, 3:6, :].rearrange("p k t -> p (k t)"), ps[5][:, 0:PASS]).then_inc(dv_ht, 1)

        @block.scalar
        def _(ac):
            ac.dma_start(cst[:, 0:128], consts[:, 0:128]).then_inc(ident_in, 16)
            for k, w in enumerate((w_loc, w_str, w_glo)):
                ac.dma_start(wv[:, k:k + 1], w.partition_broadcast(GTOK)).then_inc(wv_in, 16)
            for i in range(2):
                ac.dma_start(anc[0][:, i, :], anchor_q.rearrange("o a (b d) -> (o a b) d", d=HD)[i * HA:(i + 1) * HA, :]).then_inc(anc_in, 16)
            ac.dma_start(cst[:, 128:], consts[:, 128:]).then_inc(consts_in, 16)
            ac.dma_start(qkvw[:], qkv_w.rearrange("(r p) c -> p r c", p=HALF)).then_inc(qkvw_in, 16)
            ac.wait_ge(dv_wv, 1)
            ac.activation(wv[:, 0:3], wvn[:, 0:3], ACT.Exp).then_inc(ac_w, 1)
            ac.wait_ge(dv_anc, 1)
            ac.activation(anc[2][:], anc[1][:], ACT.Exp).then_inc(ac_anc, 1)
            ac.wait_ge(x_in, 16 * GRID)
            for w in (1, 3):
                ac.activation(xr[:, w], ximg[:, :, :, w * PATCH:(w + 1) * PATCH].rearrange("p c y x -> p (c y) x"),
                              ACT.Copy).then_inc(ac_xr, 1)
            ac.wait_ge(gp_zero, 1)
            for u in range(1, 2 * KCH, 2):
                wh, k = u // KCH, u % KCH
                ac.wait_ge(pe_xt, u + 1)
                ac.activation(patches_of(wh, k), turned(u), ACT.Copy).then_inc(ac_xt, 1)
            for m in range(4):
                i, r3 = m // 2, m % 2
                ac.wait_ge(pe_wt, m + 1)
                ac.activation(wT[:, i, 288 * r3:288 * (r3 + 1)], ps[4 + m][0:HALF, 0:288], ACT.Copy).then_inc(ac_wt, 1)
            ac.wait_ge(pe_wt, 5)
            ac.activation(woT[:].rearrange("p i c -> p (i c)"), ps[4][0:HALF, 0:2 * D], ACT.Copy).then_inc(ac_wt, 1)
            ac.wait_ge(pe_wt, 6)
            ac.activation(aq[:].rearrange("p i c -> p (i c)"), ps[5][0:HALF, 0:2 * HA], ACT.Copy).then_inc(ac_wt, 1)
            ac.activation(hbase[:], ps[5][0:GTOK, 192:192 + D], ACT.Copy).then_inc(ac_base, 1)
            ac.wait_ge(pe_wt, 7)
            ac.activation(aqs[:], ps[6][0:GTOK, 0:D], ACT.Copy).then_inc(ac_wt, 1)
            ac.wait_ge(gp_eps, 1)

            def root(g, layer):
                t0, n, _ = group(g)
                ac.wait_ge(dv_var, GROUPS * layer + g + 1)
                ac.activation(rstd[0:n, g:g + 1], mv[0:n, g, 1:2], ACT.Sqrt, bias=epsv[0:n, :]).then_inc(ac_root, 1)

            for g in range(GROUPS + 1):
                if g < GROUPS:
                    root(g, 0)
                if g == 0:
                    continue
                g -= 1
                t0, n, _ = group(g)
                ac.wait_ge(pe_xht, g + 1)
                ac.activation(xhT[:, :, t0:t0 + n],
                              ps[g % 2][0:HALF, 0:2 * GTOK].rearrange("p (i t) -> p i t", i=2)[:, :, 0:n],
                              ACT.Copy).then_inc(ac_xht, 1)

            def heads_out(g):
                t0, n, _ = group(g)
                ac.wait_ge(pe_o, g + 1)
                if g >= 2:
                    ac.wait_ge(pe_p, g - 1)
                ac.activation(oT[:, g % 2, :, 0:n],
                              ps[7][0:HALF, 0:2 * GTOK].rearrange("p (i t) -> p i t", i=2)[:, :, 0:n], ACT.Copy).then_inc(ac_o, 1)

            def spread(g):
                t0, n, imgs = group(g)
                ac.wait_ge(pe_qt, 2 * g + 1)
                if g >= 2:
                    ac.wait_ge(pe_sc, 4 * (g - 1))
                for i in range(2):
                    for hh in range(HH):
                        ins = ac.activation(qlb[:, g % 2, i, hh, 0:n], ps[2][0:HALF, i * GTOK:i * GTOK + n], ACT.Copy,
                                            scale=blk[:, hh * HD:hh * HD + 1])
                ins.then_inc(ac_qlb, 1)
                if g >= 2:
                    ac.wait_ge(pe_o, g - 1)
                ac.activation(own_columns(g, 0, imgs), by_image(ps[2][0:HALF, 2 * GTOK:4 * GTOK], n, imgs), ACT.Copy).then_inc(ac_qx, 1)
                ac.wait_ge(pe_qt, 2 * g + 2)
                if g >= 2:
                    ac.wait_ge(pe_qa, g - 1)
                ac.activation(qgT[:, g % 2, :, 0:n],
                              ps[1][0:HALF, 0:2 * GTOK].rearrange("p (i t) -> p i t", i=2)[:, :, 0:n], ACT.Copy).then_inc(ac_gt, 1)

            def weight(g):
                t0, n, _ = group(g)
                ac.wait_ge(dv_diff, g + 1)
                ac.activation(diff[0:n, g, 1:2], diff[0:n, g, 0:1], ACT.Exp).then_inc(ac_ex, 1)

            def x2_out(g):
                t0, n, _ = group(g)
                ac.wait_ge(pe_x2t, g + 1)
                if g >= 2:
                    ac.wait_ge(pe_lg, g - 1)
                ac.activation(x2T[:, g % 2, :, 0:n],
                              ps[1][0:HALF, 0:2 * GTOK].rearrange("p (i t) -> p i t", i=2)[:, :, 0:n],
                              ACT.Copy).then_inc(ac_x2t, 1)

            ac.wait_ge(gp_att, 2)
            embedding_over(ac)
            def weights_high(e):
                ac.activation(w1hi[:, e], w1s[:, e], ACT.Copy).then_inc(ac_whi, 1)

            for t in range(GROUPS + 5):
                if 0 <= t - 1 < GROUPS:
                    t0, n, _ = group(t - 1)
                    ac.wait_ge(pe_kt, t)
                    if t - 1 >= 3:
                        ac.wait_ge(pe_sc, 4 * (t - 3))
                    ac.activation(kT[:, (t - 1) % 3, :, 0:n],
                                  ps[3][0:HALF, 0:2 * GTOK].rearrange("p (i t) -> p i t", i=2)[:, :, 0:n], ACT.Copy).then_inc(ac_kt, 1)
                if 0 <= t - 2 < GROUPS:
                    spread(t - 2)
                if 0 <= t - 4 < GROUPS:
                    heads_out(t - 4)
                if t == GROUPS + 3:
                    attention_over(ac)
                    ac.wait_ge(w1_in, 16 * (E + 1))
                    ac.wait_ge(gp_zero, 3)
                    weights_high(0)
                if 0 <= t - 5 < GROUPS:
                    x2_out(t - 5)
                if 0 <= t - 3 < GROUPS:
                    g = t - 3
                    t0, n, imgs = group(g)
                    ac.wait_ge(pe_qg, g + 1)
                    if g >= 2:
                        ac.wait_ge(pe_o, g - 1)
                    ac.activation(own_columns(g, 1, imgs), by_image(ps[0][0:HALF, 0:2 * GTOK], n, imgs), ACT.Copy).then_inc(ac_qg, 1)
                if 0 <= t - 6 < GROUPS:
                    weight(t - 6)
                if t < GROUPS:
                    t0, n, _ = group(t)
                    ac.wait_ge(dv_min, t + 1)
                    if t >= 1:
                        ac.wait_ge(dv_f, t)
                    ac.activation(qkexp[0:n, :], qkmin[0:n, :], ACT.Exp).then_inc(ac_exp, 1)
                    ac.wait_ge(pe_v, t + 1)
                    if t >= 3:
                        ac.wait_ge(gp_vx, HH * (t - 2))
                    ac.activation(vtok[0:n, t % 3, :], ps[3][0:n, 0:D], ACT.Copy).then_inc(ac_v, 1)
                if 0 <= t - 4 < GROUPS:
                    root(t - 4, 1)
                if t >= GROUPS + 3:
                    weights_high(t - GROUPS - 2)
            weight(GROUPS - 1)
            for e in range(3, E):
                weights_high(e)
            for c in range(2):
                lo, hi = 4 * c * GTOK, (4 * GTOK, TOK)[c]
                ac.wait_ge(pe_ct, 1)
                ac.activation(cT[:, lo:hi], ps[4 + c][0:E, 0:hi - lo], ACT.Copy).then_inc(ac_ct, 1)

            def tokens_high(j):
                ac.wait_ge(pe_tx, j + 1)
                if j >= 2:
                    ac.wait_ge(pe_h, 2 * (j - 1))
                ac.activation(xhi[0:HALF, j % 2], ps[j % 2][0:HALF, 0:2 * SLOTS].rearrange("p (i t) -> p i t", i=2),
                              ACT.Copy).then_inc(ac_xhi, 1)

            def weigh(j):
                ac.wait_ge(pe_y, j + 1)
                if j >= 2:
                    ac.wait_ge(added, 16 * (j - 1))
                ac.activation(ys[:, j % 2, :], ps[6 + j % 2][:, 0:D], ACT.Copy,
                              scale=xs[:, j % NS, D:D + 1]).then_inc(ac_y, 1)

            tokens_high(0)
            tokens_high(1)
            for j in range(TILES):
                ac.wait_ge(pe_h, 2 * j + 1)
                if j >= 1:
                    ac.wait_ge(pe_th, 2 * j - 1)
                ac.activation(hid[:, 0:PASS], ps[2][:, 0:PASS], ACT.Relu).then_inc(ac_hid, 1)
                if j >= 1:
                    weigh(j - 1)
                if j + 2 < TILES:
                    tokens_high(j + 2)
                ac.wait_ge(pe_th, 2 * j + 1)
                if j >= 1:
                    ac.wait_ge(pe_y, j)
                ac.activation(hidT[:, 0:3, :].rearrange("p k t -> p (k t)"), ps[4][:, 0:PASS], ACT.Copy).then_inc(ac_ht, 1)
            weigh(TILES - 1)

        @block.gpsimd
        def _(po):
            counts = {}

            def link(ins, signal=gp):
                counts[id(signal)] = counts.get(id(signal), 0) + 1
                ins.then_inc(signal, 1)
                po.wait_ge(signal, counts[id(signal)])

            link(po.memset(ones[:], 1.0), gp_one)
            link(po.memset(xT[:].rearrange("p k (b s) -> p k b s", s=SEQ)[:, :, :, 0:2], 0.0), gp_zero)
            link(po.memset(posb[0:1, :], 0.0), gp_zero)
            link(po.memset(epsv[:], EPS_LN), gp_eps)
            po.wait_ge(dv_anc, 2)
            po.wait_ge(consts_in, 16)
            for i in range(2):
                link(po.tensor_tensor(aqT[:, i], anc[3][:, i, :].unsqueeze(1).broadcast_to([HA, HH, HD]),
                                      ablk.rearrange("p (a d) -> p a d", d=HD), ALU.mult), gp_anc)
            link(po.memset(ktok[96:GTOK + 1], 1.0), gp_att)
            link(po.memset(blank[:, 0:D + 1], 0.0))
            link(po.tensor_copy(blank[:, D + 1:ROW].bitcast(U32), const("number")[:, GROUPS:GROUPS + 1]), gp_blank)
            link(po.memset(qx[:], 0.0), gp_att)
            link(po.memset(both[:], 0.0), gp_sel)
            link(po.memset(run[:, 0, :], 0.0), gp_sel)
            link(po.memset(w1s[HALF:HALF + 1, :, 0, :], 0.0), gp_zero)

            def copy_row(g):
                n = group(g)[1]
                po.wait_ge(dv_x2, g + 1)
                link(po.tensor_copy(row[0:n, g, 1, 0:D], row[0:n, g, 0, 0:D]), gp_row)

            def weights_low(e):
                po.wait_ge(ac_whi, e + 1)
                link(po.tensor_tensor(w1lo[:, e], w1s[:, e], w1hi[:, e].bitcast(F32), ALU.subtract), gp_wlo)

            def scatter(g):
                n = group(g)[1]
                po.wait_ge(dv_row, g + 1)
                for k in range(TOP):
                    po.indirect_dma_start(sent.rearrange("r p c -> (r p) c"),
                                          bass.IndirectOffsetOnAxis(ap=index[0:n, g, k:k + 1], axis=0),
                                          row[0:n, g, k, :], None).then_inc(sent_in, 16)

            embedding_over(po)
            link(po.memset(vexp[:], 0.0), gp_att)
            for g in range(GROUPS):
                t0, n, imgs = group(g)
                if g >= 4:
                    copy_row(g - 4)
                po.wait_ge(ac_v, g + 1)
                if g >= 2:
                    po.wait_ge(pe_kv, 4 * (g - 1))
                for i in range(2):
                    v = vtok[0:n, g % 3, i * HALF:(i + 1) * HALF]
                    link(po.tensor_tensor(vm[0:n, g % 2, i], v.unsqueeze(1).broadcast_to([n, 2 * PER, HALF]),
                                          vmask[0:n, :].unsqueeze(2).broadcast_to([n, 2 * PER, HALF]), ALU.mult), gp_v)
                if g >= 2:
                    po.wait_ge(pe_o, g - 1)
                for hh in range(HH):
                    link(po.tensor_copy(
                        vexp[0:n, g % 2].rearrange("p (i a) c -> p i a c", i=2)[:, :, hh, hh * HD:(hh + 1) * HD],
                        vtok[0:n, g % 3].rearrange("p (i c) -> p i c", i=2)[:, :, hh * HD:(hh + 1) * HD]), gp_vx)
            po.wait_ge(sent_blank, 16)
            for g in range(GROUPS - 4, GROUPS + 2):
                if g < GROUPS:
                    copy_row(g)
                if g == GROUPS:
                    weights_low(0)
                    weights_low(1)
                scatter(g - 2)
            weights_low(2)
            po.wait_ge(sums_in, 16 * (GROUPS + 1))
            for j in range(TILES):
                po.wait_ge(ac_y, j + 1)
                if j >= 1:
                    po.wait_ge(added, 16 * j)
                po.indirect_dma_start(sums, bass.IndirectOffsetOnAxis(ap=xs[:, j % NS, D + 1:ROW].bitcast(U32), axis=0),
                                      ys[:, j % 2, :], None, compute_op=ALU.add).then_inc(added, 16)
            po.wait_ge(added, 16 * TILES)


_INS = ["x", "cls_tok", "L0_tok_W_emb", "L0_tok_b_emb", "L0_tok_pos_embedding", "L0_tok_cls_token",
        "L0_attn_qkv_w", "L0_attn_out_w", "L0_attn_anchor_q", "L0_attn_w_local", "L0_attn_w_stride",
        "L0_attn_w_global", "L0_ffn_Wg", "L0_ffn_W1", "L0_ffn_b1", "L0_ffn_W2", "L0_ffn_b2"]


def kernel(**inputs):
    import concourse.bacc as bacc
    from concourse.bass_utils import run_bass_kernel_spmd

    nc = bacc.Bacc("TRN2", target_bir_lowering=False, num_devices=1)
    arrays, args = {}, []
    for name in _INS:
        a = np.ascontiguousarray(inputs[name])
        arrays[f"in_{name}"] = a
        args.append(nc.dram_tensor(f"in_{name}", a.shape, mybir.dt.from_np(a.dtype), kind="ExternalInput").ap())
    arrays["in_constants"] = constants()
    args.append(nc.dram_tensor("in_constants", (128, CONST_COLS), F32, kind="ExternalInput").ap())
    args.append(nc.dram_tensor("out", (IMAGES, SEQ, D), F32, kind="ExternalOutput").ap())
    build(nc, *args)
    r = run_bass_kernel_spmd(nc, [arrays], core_ids=[0])
    return r.results[0]["out"]
```

```python
from contextlib import ExitStack

import numpy as np

import concourse.bass as bass
from concourse import mybir

F32 = mybir.dt.float32
F32R = mybir.dt.float32r
I32 = mybir.dt.int32
U32 = mybir.dt.uint32
ALU = mybir.AluOpType
ACT = mybir.ActivationFunctionType
AX = mybir.AxisListType

IMAGES = 16
CH, SIDE, PATCH = 3, 96, 16
GRID = SIDE // PATCH
D = 192
SEQ = GRID * GRID + 2
TOK = IMAGES * SEQ
PER = 3
GTOK = PER * SEQ
GROUPS = -(-IMAGES // PER)
HALF = D // 2
HEADS, HD = 12, 16
HH = HEADS // 2
ANCH = 12
HA = HH * ANCH
WIN, STRIDE = 12, 3
KS = 4
KCH = CH * PATCH * PATCH // 128
E, DF = 8, 768
FCH = DF // 128
TOP = 2
SLOTS = 128
REGION = -(-TOK // SLOTS)
EXTRA = (TOP * TOK - 1) // SLOTS
TILES = E + EXTRA
EMPTY = E * REGION
ROW = D + 2
PASS = DF // 2
AHEAD = 4
GP_SPLITS = (0, 2, 3, 4, 5)
DV_SPLITS = (1, 6, 7)
NS = 6
EPS_LN = 1e-5
EPS_DEN = 1e-6
ROWS = IMAGES * GRID


def group(g):
    n = min(PER, IMAGES - PER * g)
    return g * GTOK, n * SEQ, n


CONSTS = {
    "ident": (128, 128),
    "band": (GTOK + 1, GTOK),
    "blk": (HALF, HALF),
    "ablk": (HA, HALF),
    "vmask": (GTOK, 2 * PER),
    "strided": (GTOK, GTOK),
    "tri": (GTOK, E * E),
    "before": (GTOK, GTOK),
    "region": (GTOK, E),
    "number": (128, GROUPS + 1),
    "repeat": (SEQ, GTOK),
    "expert": (1, E),
    "full": (1, E * (REGION - 1)),
    "tile": (1, EXTRA * E),
}
OFF = {}
_at = 0
for _n, (_p, _c) in CONSTS.items():
    OFF[_n] = _at
    _at += _c
CONST_COLS = _at


def constants():
    c = np.zeros((128, CONST_COLS), np.float32)

    def put(name, a):
        p, n = CONSTS[name]
        c[:p, OFF[name]:OFF[name] + n] = a.reshape(p, n)

    put("ident", np.eye(128))
    j, s = np.arange(GTOK)[:, None], np.arange(GTOK)[None, :]
    same = j // SEQ == s // SEQ
    band = same & (j >= s - WIN // 2) & (j < s + WIN - WIN // 2)
    pos = np.arange(GTOK) % SEQ
    padded = np.maximum(0, WIN // 2 - pos) + np.maximum(0, pos + (WIN - WIN // 2) - SEQ)
    put("band", np.concatenate([band, padded[None]], 0))
    h = np.arange(HALF) // HD
    put("blk", h[:, None] == h[None, :])
    put("ablk", (np.arange(HA) // ANCH)[:, None] == h[None, :])
    img = (np.arange(GTOK) // SEQ)[:, None] == np.arange(PER)[None, :]
    strided = img & ((np.arange(GTOK) % SEQ % STRIDE) == 0)[:, None]
    put("vmask", np.stack([strided, img], 1))
    put("strided", same & ((np.arange(GTOK) % SEQ % STRIDE) == 0)[:, None])
    e = np.arange(E)
    put("tri", np.broadcast_to((e[:, None] > e[None, :])[None], (GTOK, E, E)))
    put("before", j < s)
    put("region", np.broadcast_to(e * REGION * SLOTS, (GTOK, E)))
    put("number", np.concatenate([np.arange(128)[:, None] + np.arange(GROUPS) * GTOK,
                                  np.arange(128)[:, None] + TOK], 1))
    put("repeat", np.arange(SEQ)[:, None] == (np.arange(GTOK) % SEQ)[None, :])
    put("expert", e)
    put("full", np.broadcast_to(np.arange(1, REGION) * SLOTS, (E, REGION - 1)))
    put("tile", np.broadcast_to(np.arange(EXTRA)[:, None], (EXTRA, E)))
    return c


def build(nc, x, cls_tok, w_emb, b_emb, pos_emb, cls0, qkv_w, out_w, anchor_q, w_loc, w_str, w_glo,
          wg, w1, b1, w2, b2, consts, out):
    sent = nc.dram_tensor("sent", (EMPTY + 1, SLOTS, ROW), F32).ap()
    sums = nc.dram_tensor("sums", (TOK + SLOTS, D), F32).ap()
    with ExitStack() as ctx:
        def pool(stack):
            def sb(name, shape, dt=F32):
                return stack.enter_context(nc.sbuf_tensor(name, shape, dt))
            return sb

        def sem(name):
            return ctx.enter_context(nc.semaphore(name))

        ps = [ctx.enter_context(nc.psum_tensor(f"ps{i}", [128, 512], F32)) for i in range(8)]

        sb = pool(ctx)
        cst = sb("cst", [128, CONST_COLS])
        h = sb("h", [GTOK, GROUPS, D])
        stats = sb("stats", [GTOK, GROUPS, 6])
        mv = sb("mv", [GTOK, GROUPS, 2])
        rstd = sb("rstd", [GTOK, GROUPS])
        epsv = sb("epsv", [GTOK, 1])
        ones = sb("ones", [GTOK, 128])
        row = sb("row", [GTOK, GROUPS, TOP, ROW])
        blank = sb("blank", [SLOTS, ROW])
        wgs = sb("wgs", [HALF, 2, E])
        b2s = sb("b2s", [E, D])
        x2T = sb("x2T", [HALF, 2, 2, GTOK])
        own = sb("own", [1, E], I32)
        woT = sb("woT", [HALF, 2, D])
        oT = sb("oT", [HALF, 2, 2, GTOK])
        comb = sb("comb", [GTOK, GROUPS, E])
        pair = sb("pair", [GTOK, GROUPS, TOP, E])
        rank = sb("rank", [GTOK, E])
        cmpa = sb("cmpa", [GTOK, E, E])
        cmpb = sb("cmpb", [GTOK, E, E])
        sel = sb("sel", [GTOK, GROUPS, TOP, E])
        both = sb("both", [GTOK, GROUPS, E])
        run = sb("run", [GTOK, GROUPS + 1, E])
        pick = sb("pick", [GTOK, TOP, E])
        best = sb("best", [GTOK, GROUPS, TOP])
        place = sb("place", [GTOK, TOP])
        index = sb("index", [GTOK, GROUPS, TOP], U32)
        diff = sb("diff", [GTOK, GROUPS, 3])
        w1s = sb("w1s", [HALF + 1, E, 2, DF])
        w2_ahead = ctx.enter_context(ExitStack())
        pool(w2_ahead)("w2_ahead", [128, AHEAD, FCH, D])

        attn = ExitStack()
        sb = pool(attn)
        wT = sb("wT", [HALF, 2, 3 * D])
        aqT = sb("aqT", [HA, 2, HH, HD])
        aq = sb("aq", [HALF, 2, HA])
        aqs = sb("aqs", [GTOK, D])
        wv = sb("wv", [GTOK, 4])
        wvn = sb("wvn", [GTOK, 4])
        anc = [sb(f"anc{i}", [HA, 2, HD]) for i in range(4)]
        hbase = sb("hbase", [GTOK, D])
        ktok = sb("ktok", [GTOK + 1, KS, D])
        XW = PER * (GTOK + SEQ)
        qx = sb("qx", [HALF, 2, 2, 2, XW])
        xhT = sb("xhT", [HALF, 2, TOK])
        xn = sb("xn", [GTOK, GROUPS, D])
        emb = ExitStack()
        sb = pool(emb)
        ximg = sb("ximg", [ROWS, CH, PATCH, SIDE])
        xr = sb("xr", [ROWS, GRID, CH * PATCH, PATCH])
        qkvw = sb("qkvw", [HALF, 6, D])
        outw = sb("outw", [HALF, 2, D])
        posa = sb("posa", [SEQ, D])
        posb = sb("posb", [SEQ, D])
        xT = sb("xT", [128, KCH, TOK])
        wemb = sb("wemb", [128, KCH, D])
        emb.close()
        sb = pool(attn)
        qkmin = sb("qkmin", [GTOK, 2 * D])
        qkexp = sb("qkexp", [GTOK, 2 * D])
        qtok = sb("qtok", [GTOK, 2, D])
        vtok = sb("vtok", [GTOK, 3, D])
        vm = sb("vm", [GTOK, 2, 2, 2 * PER, HALF])
        kT = sb("kT", [HALF, 3, 2, GTOK])
        ksum = sb("ksum", [HALF, GROUPS, 2, PER])
        prod = sb("prod", [GTOK, 3, D])
        den = sb("den", [GTOK, 3, HEADS])
        qsc = sb("qsc", [GTOK, 2, 3, D])
        qgT = sb("qgT", [HALF, 2, 2, GTOK])
        qlb = sb("qlb", [HALF, 2, 2, HH, GTOK])
        kvb = sb("kvb", [HALF, 2, 2, 2 * PER, HALF])
        at = sb("at", [GTOK, 2, HEADS, GTOK])
        vexp = sb("vexp", [GTOK, 2, HEADS, HALF])
        qas = sb("qas", [HA, 2, 2, GTOK])
        reca = sb("reca", [HA, 2, 2, PER])
        attn.close()
        w2_ahead.close()

        moe = ctx.enter_context(ExitStack())
        sb = pool(moe)
        w2s = sb("w2s", [128, E, FCH, D])
        w1hi = sb("w1hi", [HALF + 1, E, 2, DF], F32R)
        cT = sb("cT", [E, TOK])
        first = sb("first", [GTOK, GROUPS, D])
        counts = sb("counts", [1, E])
        full = sb("full", [1, E, REGION - 1])
        tiles = sb("tiles", [1, 4, E])
        ge = sb("ge", [1, 2, EXTRA, E])
        tabf = sb("tabf", [1, 2, EXTRA])
        tab = sb("tab", [1, 2, EXTRA], I32)
        xs = sb("xs", [SLOTS, NS, ROW])
        xhi = sb("xhi", [HALF + 1, 2, 2, SLOTS], F32R)
        xlo = sb("xlo", [HALF + 1, 2, 2, SLOTS], F32R)
        hid = sb("hid", [SLOTS, DF])
        hidT = sb("hidT", [128, FCH, SLOTS])
        ys = sb("ys", [SLOTS, 2, D])

        def const(name):
            p, n = CONSTS[name]
            return cst[:p, OFF[name]:OFF[name] + n]

        ident = const("ident")
        blk = const("blk")
        ablk = const("ablk")
        band = const("band")
        vmask = const("vmask")
        tri = const("tri")
        strided = const("strided")
        before = const("before")

        ident_in = sem("ident_in")
        consts_in = sem("consts_in")
        x_in = [sem(f"x_in{c}") for c in range(CH)]
        wemb_in = sem("wemb_in")
        qkvw_in = sem("qkvw_in")
        outw_in = sem("outw_in")
        pos_in = sem("pos_in")
        anc_in = sem("anc_in")
        wv_in = sem("wv_in")
        wg_in = sem("wg_in")
        w1_in = sem("w1_in")
        w2_in = sem("w2_in")
        sent_blank = sem("sent_blank")
        sent_in = sem("sent_in")
        sums_in = sem("sums_in")
        added = sem("added")
        xs_in = [sem(f"xs_in{i}") for i in range(NS)]
        out_done = sem("out_done")
        pe_patch_turned = sem("pe_patch_turned")
        pe_base = sem("pe_base")
        pe_weights_turned = sem("pe_weights_turned")
        pe_embedded = sem("pe_embedded")
        pe_xhat_turned = sem("pe_xhat_turned")
        pe_qk = sem("pe_qk")
        pe_v = sem("pe_v")
        pe_key_sums = sem("pe_key_sums")
        pe_keys_turned = sem("pe_keys_turned")
        pe_queries_turned = sem("pe_queries_turned")
        pe_on_anchors = sem("pe_on_anchors")
        pe_keys_values = sem("pe_keys_values")
        pe_scores = sem("pe_scores")
        pe_from_anchors = sem("pe_from_anchors")
        pe_heads = sem("pe_heads")
        pe_projected = sem("pe_projected")
        pe_x2_turned = sem("pe_x2_turned")
        pe_logits = sem("pe_logits")
        pe_places = sem("pe_places")
        pe_counts = sem("pe_counts")
        pe_combine_turned = sem("pe_combine_turned")
        pe_out_bias = sem("pe_out_bias")
        pe_tile_turned = sem("pe_tile_turned")
        pe_hidden = sem("pe_hidden")
        pe_hidden_turned = sem("pe_hidden_turned")
        pe_answers = sem("pe_answers")
        dv = sem("dv")
        dv_patch_rows = sem("dv_patch_rows")
        dv_patches = sem("dv_patches")
        dv_band_diff = sem("dv_band_diff")
        dv_anchors = sem("dv_anchors")
        dv_embedded = sem("dv_embedded")
        dv_moments = sem("dv_moments")
        dv_xhat = sem("dv_xhat")
        dv_min = sem("dv_min")
        dv_features = sem("dv_features")
        dv_key_sums = sem("dv_key_sums")
        dv_image_sums = sem("dv_image_sums")
        dv_queries = sem("dv_queries")
        dv_anchored = sem("dv_anchored")
        dv_keys_values = sem("dv_keys_values")
        dv_windows = sem("dv_windows")
        dv_h2 = sem("dv_h2")
        dv_x2 = sem("dv_x2")
        dv_logits = sem("dv_logits")
        dv_places = sem("dv_places")
        dv_both = sem("dv_both")
        dv_diff = sem("dv_diff")
        dv_row = sem("dv_row")
        dv_combine = sem("dv_combine")
        dv_count = sem("dv_count")
        dv_tab = sem("dv_tab")
        dv_first = sem("dv_first")
        dv_w1_low = sem("dv_w1_low")
        dv_x_low = sem("dv_x_low")
        dv_hidden = sem("dv_hidden")
        dv_hidden_turned = sem("dv_hidden_turned")
        ac_patch_rows = sem("ac_patch_rows")
        ac_patches = sem("ac_patches")
        ac_band_exp = sem("ac_band_exp")
        ac_anchor_exp = sem("ac_anchor_exp")
        ac_base = sem("ac_base")
        ac_root = sem("ac_root")
        ac_weights = sem("ac_weights")
        ac_anchor_sum = sem("ac_anchor_sum")
        ac_xhat_turned = sem("ac_xhat_turned")
        ac_exp = sem("ac_exp")
        ac_v = sem("ac_v")
        ac_keys_turned = sem("ac_keys_turned")
        ac_local_queries = sem("ac_local_queries")
        ac_strided_queries = sem("ac_strided_queries")
        ac_global_queries = sem("ac_global_queries")
        ac_from_anchors = sem("ac_from_anchors")
        ac_heads = sem("ac_heads")
        ac_x2_turned = sem("ac_x2_turned")
        ac_weight_exp = sem("ac_weight_exp")
        ac_combine_turned = sem("ac_combine_turned")
        ac_w1_high = sem("ac_w1_high")
        ac_x_high = sem("ac_x_high")
        ac_hidden = sem("ac_hidden")
        ac_hidden_turned = sem("ac_hidden_turned")
        ac_answers = sem("ac_answers")
        gp = sem("gp")
        gp_one = sem("gp_one")
        gp_class_zero = sem("gp_class_zero")
        gp_posb_zero = sem("gp_posb_zero")
        gp_eps = sem("gp_eps")
        gp_anchors = sem("gp_anchors")
        gp_ktok_one = sem("gp_ktok_one")
        gp_blank = sem("gp_blank")
        gp_qx_zero = sem("gp_qx_zero")
        gp_own = sem("gp_own")
        gp_route_zero = sem("gp_route_zero")
        gp_bias_zero = sem("gp_bias_zero")
        gp_vexp_zero = sem("gp_vexp_zero")
        gp_masked_values = sem("gp_masked_values")
        gp_head_values = sem("gp_head_values")
        gp_row = sem("gp_row")
        gp_w1_low = sem("gp_w1_low")

        block = ctx.enter_context(nc.Block())

        def patches_of(wh, k):
            return xT[:, k, :].rearrange("p (b s) -> p b s", s=SEQ)[:, :, 2:SEQ].rearrange(
                "p b (i w) -> p w i b", w=GRID)[:, 3 * wh:3 * wh + 3]

        def patch_rows(c, wh):
            return xr[:, 3 * wh:3 * wh + 3, c * PATCH:(c + 1) * PATCH, :]

        def image_rows(c, wh):
            return ximg[:, c, :, 3 * PATCH * wh:3 * PATCH * (wh + 1)].rearrange("p y (w x) -> p w y x", x=PATCH)

        def turned(u):
            return ps[u % 4][:, 0:3 * ROWS].rearrange("p (w i b) -> p w i b", w=3, b=IMAGES)

        def own_columns(g, kind, imgs):
            return qx[:, g % 2, kind].rearrange("p i (b x) -> p i b x", x=GTOK + SEQ)[:, :, 0:imgs, 0:SEQ]

        def xhat_bank(g):
            return ps[7] if g >= 4 else ps[g % 2]

        def by_image(bank, n, imgs):
            return bank.rearrange("p (i t) -> p i t", i=2)[:, :, 0:n].rearrange("p i (b s) -> p i b s", s=SEQ)

        w1lo = w1s[:].bitcast(F32R)

        def turning_over(engine):
            engine.wait_ge(pe_patch_turned, 2 * KCH)
            engine.wait_ge(pe_weights_turned, 6)
            engine.wait_ge(pe_base, 1)

        def embedding_over(engine):
            engine.wait_ge(pe_embedded, GROUPS)

        def attention_over(engine):
            engine.wait_ge(pe_heads, GROUPS)

        @block.sync
        def _(sp):
            for c in range(CH):
                for i in range(GRID):
                    sp.dma_start(ximg[i * IMAGES:(i + 1) * IMAGES, c].rearrange("p y w -> p (y w)"),
                                 x.rearrange("b c (i y) w -> c i b (y w)", y=PATCH)[c, i]).then_inc(x_in[c], 16)
            sp.dma_start(cst[:, 128:], consts[:, 128:]).then_inc(consts_in, 16)
            sp.dma_start(wemb[:], w_emb.rearrange("(k p) c -> p k c", p=128)).then_inc(wemb_in, 16)
            sp.wait_ge(gp_posb_zero, 1)
            sp.dma_start(posa[0:1, :], cls_tok.rearrange("a b d -> (a b) d")).then_inc(pos_in, 16)
            sp.dma_start(posa[1:SEQ, :], pos_emb[0]).then_inc(pos_in, 16)
            sp.dma_start(posb[1:2, :], cls0.rearrange("a b d -> (a b) d")).then_inc(pos_in, 16)
            sp.dma_start(posb[2:SEQ, :], b_emb.partition_broadcast(SEQ - 2)).then_inc(pos_in, 16)
            sp.dma_start(qkvw[:], qkv_w.rearrange("(r p) c -> p r c", p=HALF)).then_inc(qkvw_in, 16)
            sp.dma_start(outw[:], out_w.rearrange("(r p) c -> p r c", p=HALF)).then_inc(outw_in, 16)
            sp.dma_start(wgs[:], wg.rearrange("(i p) e -> p i e", p=HALF)).then_inc(wg_in, 16)
            sp.dma_start(b2s[:], b2).then_inc(wg_in, 16)
            sp.wait_ge(x_in[CH - 1], 16 * GRID)
            sp.wait_ge(wemb_in, 16)
            for e in range(E):
                sp.dma_start(w1s[0:HALF, e], w1[e].rearrange("(i p) f -> p i f", p=HALF)).then_inc(w1_in, 16)
            sp.dma_start(w1s[HALF:HALF + 1, :, 1, :], b1.unsqueeze(0)).then_inc(w1_in, 16)
            sp.wait_ge(gp_blank, 1)
            sp.dma_start(sent.rearrange("r p c -> p r c"),
                         blank[:].unsqueeze(1).broadcast_to([SLOTS, EMPTY + 1, ROW])).then_inc(sent_blank, 16)
            sp.dma_start(sums[TOK:], blank[:, 0:D]).then_inc(sums_in, 16)

            def load_w2(e):
                sp.dma_start(w2s[:, e], w2[e].rearrange("(k p) c -> p k c", p=128)).then_inc(w2_in, 16)

            for e in range(AHEAD):
                load_w2(e)
            attention_over(sp)
            for e in range(AHEAD, E):
                load_w2(e)
            sp.wait_ge(sent_in, 16 * TOP * GROUPS)

            def load_tile(j):
                if j < E:
                    source = sent[j * REGION]
                else:
                    place_of = sp.value_load(tab[0:1, 1, j - E:j - E + 1], min_val=0, max_val=EMPTY)
                    source = sent[bass.ds(place_of, 1)].rearrange("r p c -> p (r c)")
                sp.dma_start(xs[:, j % NS, :], source).then_inc(xs_in[j % NS], 16)

            for j in range(NS):
                load_tile(j)
            for g in range(GROUPS):
                t0, n, _ = group(g)
                sp.wait_ge(dv_first, g + 1)
                sp.dma_start(sums[t0:t0 + n, :], first[0:n, g, :]).then_inc(sums_in, 16)
            sp.wait_ge(dv_tab, 1)
            for j in range(NS, TILES):
                sp.wait_ge(pe_tile_turned, j - NS + 1)
                sp.wait_ge(added, 16 * (j - NS + 1))
                load_tile(j)
            sp.wait_ge(added, 16 * TILES)
            flat = out.rearrange("b s d -> (b s) d")
            sp.dma_start(flat.rearrange("(q r) c -> q (r c)", q=IMAGES),
                         sums[0:TOK].rearrange("(q r) c -> q (r c)", q=IMAGES)).then_inc(out_done, 16)
            sp.wait_ge(out_done, 16)

        @block.tensor
        def _(pe):
            pe.wait_ge(ident_in, 16)
            for u in range(2 * KCH):
                k, wh = u // 2, u % 2
                if wh:
                    pe.wait_ge(ac_patch_rows, k // 2 + 1)
                else:
                    pe.wait_ge(dv_patch_rows, k // 2 + 1)
                if u >= 4:
                    pe.wait_ge(ac_patches if wh else dv_patches, k - 1)
                for w in range(3):
                    last = pe.transpose(ps[u % 4][:, w * ROWS:(w + 1) * ROWS],
                                        xr[:, 3 * wh + w, 8 * k:8 * k + 8, :].rearrange("p y x -> p (y x)"),
                                        ident[0:ROWS, 0:ROWS])
                last.then_inc(pe_patch_turned, 1)
            pe.wait_ge(consts_in, 16)
            pe.wait_ge(pos_in, 64)
            for k, part in enumerate((posa, posb)):
                last = pe.matmul(ps[5][0:GTOK, 0:D], const("repeat"), part[:], start=(k == 0), stop=(k == 1))
            last.then_inc(pe_base, 1)

            def turn_projections():
                pe.wait_ge(qkvw_in, 16)
                pe.wait_ge(ac_base, 1)
                for i in range(2):
                    for r3 in range(2):
                        for r in range(3):
                            last = pe.transpose(ps[2 + 2 * i + r3][0:HALF, r * HALF:(r + 1) * HALF],
                                                qkvw[:, 3 * r3 + r, i * HALF:(i + 1) * HALF], ident[0:HALF, 0:HALF])
                        last.then_inc(pe_weights_turned, 1)

            def turn_anchors():
                pe.wait_ge(outw_in, 16)
                pe.wait_ge(ac_weights, 3)
                for i in range(2):
                    for r in range(2):
                        last = pe.transpose(ps[4][0:HALF, (2 * i + r) * HALF:(2 * i + r + 1) * HALF],
                                            outw[:, r, i * HALF:(i + 1) * HALF], ident[0:HALF, 0:HALF])
                last.then_inc(pe_weights_turned, 1)
                pe.wait_ge(gp_anchors, 2)
                pe.wait_ge(gp_one, 1)
                pe.wait_ge(ac_weights, 4)
                for i in range(2):
                    anchors = aqT[:, i].rearrange("p h d -> p (h d)")
                    pe.transpose(ps[5][0:HALF, i * HA:(i + 1) * HA], anchors, ident[0:HA, 0:HA])
                    last = pe.matmul(ps[5][0:GTOK, 160 + i * HALF:160 + (i + 1) * HALF], ones[0:HA, 0:GTOK], anchors,
                                     start=True, stop=True)
                last.then_inc(pe_weights_turned, 1)

            pe.wait_ge(wemb_in, 16)
            pe.wait_ge(dv_patches, KCH)
            pe.wait_ge(ac_patches, KCH)
            pe.wait_ge(gp_class_zero, 1)

            def embed(g):
                t0, n, _ = group(g)
                if g >= 2:
                    pe.wait_ge(dv_embedded, g - 1)
                for k in range(KCH):
                    last = pe.matmul(ps[6 + g % 2][0:n, 0:D], xT[:, k, t0:t0 + n], wemb[:, k, :],
                                     start=(k == 0), stop=(k == KCH - 1))
                last.then_inc(pe_embedded, 1)

            def xhat_turn(g):
                t0, n, _ = group(g)
                pe.wait_ge(dv_xhat, g + 1)
                if g >= 4:
                    pe.wait_ge(dv_embedded, GROUPS)
                    pe.wait_ge(ac_xhat_turned, g)
                elif g >= 2:
                    pe.wait_ge(ac_xhat_turned, g - 1)
                for i in range(2):
                    last = pe.transpose(xhat_bank(g)[0:HALF, i * GTOK:i * GTOK + n],
                                        xn[0:n, g, i * HALF:(i + 1) * HALF], ident[0:n, 0:n])
                last.then_inc(pe_xhat_turned, 1)

            embed(0)
            embed(1)
            turn_projections()
            xhat_turn(0)
            embed(2)
            turn_anchors()
            xhat_turn(1)

            def project_qkv(g):
                t0, n, _ = group(g)
                if g == 0:
                    pe.wait_ge(ac_weights, 6)
                pe.wait_ge(ac_xhat_turned, g + 1)
                if g >= 2:
                    pe.wait_ge(ac_strided_queries, g - 1)
                elif g == 1:
                    pe.wait_ge(dv_features, 1)
                if g >= 1:
                    pe.wait_ge(ac_keys_turned, g)
                for i in range(2):
                    last = pe.matmul(ps[2][0:n, 0:2 * D], xhT[:, i, t0:t0 + n], wT[:, i, 0:2 * D],
                                     start=(i == 0), stop=(i == 1))
                last.then_inc(pe_qk, 1)
                for i in range(2):
                    last = pe.matmul(ps[3][0:n, 0:D], xhT[:, i, t0:t0 + n], wT[:, i, 2 * D:3 * D],
                                     start=(i == 0), stop=(i == 1))
                last.then_inc(pe_v, 1)

            def project_out(g):
                t0, n, _ = group(g)
                pe.wait_ge(ac_heads, g + 1)
                pe.wait_ge(ac_from_anchors, min(g + 2, GROUPS))
                for i in range(2):
                    last = pe.matmul(ps[0][0:n, 0:D], oT[:, g % 2, i, 0:n], woT[:, i, :], start=(i == 0), stop=(i == 1))
                last.then_inc(pe_projected, 1)

            def outputs(g, i):
                t0, n, imgs = group(g)
                w = max(n, HALF)
                pe.wait_ge(dv_keys_values, 4 * g + 4)
                pe.wait_ge(dv_windows, 4 * g + 4)
                pe.wait_ge(gp_head_values, HH * (g + 1))
                pe.wait_ge(ac_from_anchors, g + 1)
                if g >= 1:
                    pe.wait_ge(ac_heads, g)
                else:
                    pe.wait_ge(ac_xhat_turned, GROUPS)
                o = ps[7][0:HALF, i * GTOK:i * GTOK + w]
                for hh in range(HH):
                    pe.matmul(o, vexp[0:n, g % 2, i * HH + hh, :], at[0:n, g % 2, i * HH + hh, 0:w],
                              start=(hh == 0), stop=False, skip_group_check=True)
                for kind in range(2):
                    for b in range(imgs):
                        last = pe.matmul(o, kvb[:, g % 2, i, kind * PER + b, :],
                                         qx[:, g % 2, kind, i, b * GTOK:b * GTOK + w],
                                         start=False, stop=(kind == 1 and b == imgs - 1), skip_group_check=True)
                if i == 1:
                    last.then_inc(pe_heads, 1)

            def key_sums(g):
                t0, n, _ = group(g)
                pe.wait_ge(dv_features, g + 1)
                if g >= 1:
                    pe.wait_ge(dv_key_sums, g)
                pe.matmul(ps[4][0:n, 0:D], band[:, 0:n], ktok[:, g % KS, :], start=True, stop=True)
                pe.matmul(ps[4][0:n, D:2 * D], strided[0:n, 0:n], ktok[0:n, g % KS, :], start=True, stop=True).then_inc(pe_key_sums, 1)

            def turn_keys(g):
                t0, n, _ = group(g)
                pe.wait_ge(ac_v, g + 1)
                for i in range(2):
                    last = pe.transpose(ps[3][0:HALF, i * GTOK:i * GTOK + n], ktok[0:n, g % KS, i * HALF:(i + 1) * HALF],
                                        ident[0:n, 0:n])
                last.then_inc(pe_keys_turned, 1)

            def turn_queries(g):
                t0, n, imgs = group(g)
                pe.wait_ge(dv_queries, g + 1)
                pe.wait_ge(dv_features, min(g + 2, GROUPS))
                for kind in range(2):
                    for i in range(2):
                        c = (2 * kind + i) * GTOK
                        last = pe.transpose(ps[2][0:HALF, c:c + n], qsc[0:n, g % 2, kind, i * HALF:(i + 1) * HALF],
                                            ident[0:n, 0:n])
                last.then_inc(pe_queries_turned, 1)
                if g == 0:
                    pe.wait_ge(ac_xhat_turned, 4)
                if g >= 4:
                    pe.wait_ge(dv_logits, g - 3)
                for i in range(2):
                    last = pe.transpose(ps[1][0:HALF, i * GTOK:i * GTOK + n], qsc[0:n, g % 2, 2, i * HALF:(i + 1) * HALF],
                                        ident[0:n, 0:n])
                last.then_inc(pe_queries_turned, 1)

            def through_anchors(g):
                t0, n, imgs = group(g)
                pe.wait_ge(ac_global_queries, g + 1)
                pe.wait_ge(dv_image_sums, g + 1)
                if g == 0:
                    pe.wait_ge(ac_xhat_turned, 3)
                if g >= 1:
                    pe.wait_ge(ac_from_anchors, g)
                if g >= 2:
                    pe.wait_ge(dv_h2, g - 1)
                for i in range(2):
                    pe.matmul(ps[0][0:HA, i * GTOK:i * GTOK + n], aq[:, i, :], qgT[:, g % 2, i, 0:n],
                              start=True, stop=True)
                for i in range(2):
                    last = pe.matmul(ps[0][0:HA, 256 + i * PER:256 + i * PER + imgs], aq[:, i, :], ksum[:, g, i, 0:imgs],
                                     start=True, stop=True)
                last.then_inc(pe_on_anchors, 1)

            def keys_values(g, m):
                t0, n, imgs = group(g)
                i, kind = m // 2, m % 2
                pe.wait_ge(gp_masked_values, 2 * g + i + 1)
                if 4 * g + m >= 1:
                    pe.wait_ge(dv_keys_values, 4 * g + m)
                pe.matmul(ps[5][0:HALF, 0:imgs * HALF], ktok[0:n, g % KS, i * HALF:(i + 1) * HALF],
                          vm[0:n, g % 2, i, kind * PER:kind * PER + imgs, :],
                          start=True, stop=True).then_inc(pe_keys_values, 1)

            def scores(g, m):
                t0, n, _ = group(g)
                i = m // 2
                pe.wait_ge(ac_keys_turned, g + 1)
                pe.wait_ge(ac_local_queries, g + 1)
                if 4 * g + m >= 1:
                    pe.wait_ge(dv_windows, 4 * g + m)
                else:
                    pe.wait_ge(dv_embedded, GROUPS)
                pe.matmul(ps[6][0:n, 0:3 * n], kT[:, g % 3, i, 0:n],
                          qlb[:, g % 2, i, 3 * (m % 2):3 * (m % 2) + 3, 0:n],
                          start=True, stop=True).then_inc(pe_scores, 1)

            def from_anchors(g):
                t0, n, _ = group(g)
                pe.wait_ge(dv_anchored, 2 * (g + 1))
                for i in range(2):
                    last = pe.matmul(ps[0][0:HALF, i * GTOK:i * GTOK + n], aqT[:, i].rearrange("p h d -> p (h d)"),
                                     qas[:, g % 2, i, 0:n], start=True, stop=True)
                last.then_inc(pe_from_anchors, 1)

            def x2_turn(g):
                t0, n, _ = group(g)
                pe.wait_ge(dv_x2, g + 1)
                pe.wait_ge(ac_global_queries, min(g + 4, GROUPS))
                if g >= 1:
                    pe.wait_ge(dv_logits, g)
                for i in range(2):
                    last = pe.transpose(ps[1][0:HALF, i * GTOK:i * GTOK + n],
                                        row[0:n, g, 0, i * HALF:(i + 1) * HALF], ident[0:n, 0:n])
                last.then_inc(pe_x2_turned, 1)

            def logits(g):
                t0, n, _ = group(g)
                pe.wait_ge(ac_x2_turned, g + 1)
                for i in range(2):
                    last = pe.matmul(ps[1][0:n, 256:256 + E], x2T[:, g % 2, i, 0:n], wgs[:, i, :],
                                     start=(i == 0), stop=(i == 1))
                last.then_inc(pe_logits, 1)

            def places(g):
                t0, n, _ = group(g)
                pe.wait_ge(dv_both, 2 * g + 2)
                pe.wait_ge(dv_key_sums, GROUPS)
                if g >= 1:
                    pe.wait_ge(dv_places, g)
                pe.matmul(ps[4][0:n, 0:E], before[0:n, 0:n], both[0:n, g, :], start=True, stop=False)
                pe.matmul(ps[4][0:n, 0:E], ones[:, 0:n], run[:, g, :], start=False, stop=True).then_inc(pe_places, 1)

            def turn_combine(gs):
                pe.wait_ge(dv_combine, gs[-1] + 1)
                if gs[0] == 0:
                    pe.wait_ge(dv_keys_values, 4 * GROUPS)
                else:
                    pe.wait_ge(ac_combine_turned, 1)
                for g in gs:
                    n = group(g)[1]
                    last = pe.transpose(ps[5][0:E, (g - gs[0]) * GTOK:(g - gs[0]) * GTOK + n], comb[0:n, g, :], ident[0:n, 0:n])
                last.then_inc(pe_combine_turned, 1)

            def output_biases(gs):
                pe.wait_ge(ac_combine_turned, 1 if gs[0] == 0 else 2)
                if gs[0] == 0:
                    pe.wait_ge(dv_windows, 4 * GROUPS)
                    pe.wait_ge(ac_heads, GROUPS)
                else:
                    pe.wait_ge(dv_places, GROUPS)
                for g in gs:
                    t0, n, _ = group(g)
                    pe.matmul(ps[(6, 7, 4)[g // 2]][0:n, (g % 2) * 256:(g % 2) * 256 + D], cT[:, t0:t0 + n], b2s[:],
                              start=True, stop=True).then_inc(pe_out_bias, 1)

            pe.wait_ge(wg_in, 32)
            for t in range(GROUPS + 5):
                if 0 <= t - 3 < GROUPS:
                    through_anchors(t - 3)
                for m in range(4):
                    if 0 <= t - 3 < GROUPS:
                        keys_values(t - 3, m)
                        scores(t - 3, m)
                    if m == 0 and 0 <= t - 1 < GROUPS:
                        key_sums(t - 1)
                        turn_keys(t - 1)
                    if m == 0 and 1 <= t < 4:
                        xhat_turn(t + 1)
                    if m == 1 and 0 <= t - 2 < GROUPS:
                        turn_queries(t - 2)
                    if m == 1 and t == 3:
                        xhat_turn(5)
                    if m < 2 and 0 <= t - 4 < GROUPS:
                        outputs(t - 4, m)
                    if m == 0 and t == GROUPS + 3:
                        x2_turn(GROUPS - 2)
                        places(GROUPS - 3)
                    if m == 2:
                        if 0 <= t - 3 < GROUPS:
                            from_anchors(t - 3)
                        if t - 5 == GROUPS - 1 or 0 <= t - 5 < GROUPS - 2:
                            x2_turn(t - 5)
                if 0 <= t - 5 < GROUPS:
                    logits(t - 5)
                if t - 5 == GROUPS - 1:
                    places(GROUPS - 2)
                    output_biases(range(4))
                if 0 <= t - 6 < GROUPS - 3:
                    places(t - 6)
                if 0 <= t - 4 < GROUPS:
                    project_out(t - 4)
                if t == GROUPS + 3:
                    turn_combine(range(4))
                if 1 <= t < GROUPS - 3:
                    embed(t + 3)
                if t < GROUPS:
                    project_qkv(t)
                if t == 0:
                    embed(3)
            places(GROUPS - 1)
            pe.matmul(ps[0][0:1, 0:E], ones[:, 0:1], run[:, GROUPS, :], start=True, stop=True).then_inc(pe_counts, 1)
            turn_combine(range(4, GROUPS))
            output_biases(range(4, GROUPS))

            def turn_tokens(j):
                pe.wait_ge(xs_in[j % NS], 16 * (j // NS + 1))
                if j >= 2:
                    pe.wait_ge(dv_x_low, j - 1)
                for i in range(2):
                    last = pe.transpose(ps[j % 2][0:HALF, i * SLOTS:(i + 1) * SLOTS],
                                        xs[:, j % NS, i * HALF:(i + 1) * HALF], ident)
                last.then_inc(pe_tile_turned, 1)

            def of_expert(weights, expert):
                return weights[:, bass.ds(expert, 1)].rearrange("p e f -> p (e f)")

            def hidden(j, expert):
                pe.wait_ge(ac_x_high, j + 1)
                pe.wait_ge(dv_x_low, j + 1)
                for c in range(2):
                    if j >= 1:
                        pe.wait_ge(dv_hidden if c else ac_hidden, j)
                    first_product = True
                    for i in range(2):
                        p = HALF + i
                        for xx, ww in ((xhi, w1hi), (xlo, w1hi), (xhi, w1lo)):
                            last = pe.matmul(ps[2 + c][:, 0:PASS], xx[0:p, j % 2, i, :],
                                             of_expert(ww[0:p, :, i, c * PASS:(c + 1) * PASS], expert),
                                             start=first_product, stop=(i == 1 and ww is w1lo))
                            first_product = False
                    last.then_inc(pe_hidden, 1)

            def turn_hidden(j):
                if j >= 1:
                    pe.wait_ge(ac_hidden_turned, j)
                    pe.wait_ge(dv_hidden_turned, j)
                for c in range(2):
                    pe.wait_ge(dv_hidden if c else ac_hidden, j + 1)
                    for k in range(3):
                        last = pe.transpose(ps[4 + c][:, k * 128:(k + 1) * 128],
                                            hid[:, (3 * c + k) * 128:(3 * c + k + 1) * 128], ident)
                    last.then_inc(pe_hidden_turned, 1)

            def answers(j, expert):
                if j >= 2:
                    pe.wait_ge(ac_answers, j - 1)
                pe.wait_ge(ac_hidden_turned, j + 1)
                pe.wait_ge(dv_hidden_turned, j + 1)
                for k in range(FCH):
                    last = pe.matmul(ps[6 + j % 2][:, 0:D], hidT[:, k, :],
                                     of_expert(w2s[:, :, k, :], expert),
                                     start=(k == 0), stop=(k == FCH - 1))
                last.then_inc(pe_answers, 1)

            pe.wait_ge(dv_count, 1)
            turn_tokens(0)
            turn_tokens(1)
            pe.wait_ge(gp_own, 1)
            experts = {}
            for j in range(TILES + 1):
                if j < E:
                    pe.wait_ge(ac_w1_high, j + 1)
                    if j in GP_SPLITS:
                        pe.wait_ge(gp_w1_low, GP_SPLITS.index(j) + 1)
                    else:
                        pe.wait_ge(dv_w1_low, DV_SPLITS.index(j) + 1)
                    experts[j] = pe.value_load(own[0:1, j:j + 1], min_val=0, max_val=E - 1)
                elif j < TILES:
                    if j == E:
                        pe.wait_ge(dv_tab, 1)
                    experts[j] = pe.value_load(tab[0:1, 0, j - E:j - E + 1], min_val=0, max_val=E - 1)
                if j < TILES:
                    hidden(j, experts[j])
                if j == 1:
                    pe.wait_ge(w2_in, 16 * E)
                if j >= 1:
                    answers(j - 1, experts[j - 1])
                if j + 2 < TILES:
                    turn_tokens(j + 2)
                if j == 0:
                    pe.wait_ge(dv_first, GROUPS)
                if j < TILES:
                    turn_hidden(j)

        @block.vector
        def _(ve):
            links = [0]

            def link(ins):
                links[0] += 1
                ins.then_inc(dv, 1)
                ve.wait_ge(dv, links[0])

            ve.wait_ge(gp_class_zero, 1)
            for c in range(CH):
                ve.wait_ge(x_in[c], 16 * GRID)
                ve.tensor_copy(patch_rows(c, 0), image_rows(c, 0)).then_inc(dv_patch_rows, 1)
                for k in (2 * c, 2 * c + 1):
                    ve.wait_ge(pe_patch_turned, 2 * k + 1)
                    ve.tensor_copy(patches_of(0, k), turned(2 * k)).then_inc(dv_patches, 1)

            ve.wait_ge(wv_in, 48)
            link(ve.tensor_reduce(wv[:, 3:4], wv[:, 0:3], AX.X, ALU.max))
            ve.tensor_scalar(wvn[:, 0:3], wv[:, 0:3], wv[:, 3:4], None, ALU.subtract).then_inc(dv_band_diff, 1)
            ve.wait_ge(ac_band_exp, 1)
            link(ve.tensor_reduce(wv[:, 3:4], wv[:, 0:3], AX.X, ALU.add))
            link(ve.reciprocal(wvn[:, 3:4], wv[:, 3:4]))
            link(ve.tensor_scalar(wvn[:, 0:3], wv[:, 0:3], wvn[:, 3:4], None, ALU.mult))
            ve.wait_ge(anc_in, 32)
            ve.tensor_scalar(anc[1][:], anc[0][:], 0.0, None, ALU.min).then_inc(dv_anchors, 1)
            ve.wait_ge(ac_anchor_exp, 1)
            ve.scalar_tensor_tensor(anc[3][:], anc[0][:], 0.0, anc[2][:], ALU.max, ALU.add).then_inc(dv_anchors, 1)

            def moments(g, n, src):
                link(ve.bn_stats(stats[0:n, g, :], src))
                ve.bn_aggr(mv[0:n, g, :], stats[0:n, g, :]).then_inc(dv_moments, 1)

            def normalise(g, n, src, dst, layer):
                ve.wait_ge(ac_root, GROUPS * layer + g + 1)
                link(ve.reciprocal(rstd[0:n, g:g + 1], rstd[0:n, g:g + 1]))
                return ve.tensor_scalar(dst, src, mv[0:n, g, 0:1], rstd[0:n, g:g + 1],
                                        ALU.subtract, ALU.mult)

            ve.wait_ge(ac_base, 1)
            def embedded(g):
                n = group(g)[1]
                ve.wait_ge(pe_embedded, g + 1)
                ve.tensor_tensor(h[0:n, g, :], ps[6 + g % 2][0:n, 0:D], hbase[0:n, :], ALU.add).then_inc(dv_embedded, 1)
                ve.wait_ge(dv_embedded, g + 1)
                moments(g, n, h[0:n, g, :])

            def xhat(g):
                n = group(g)[1]
                normalise(g, n, h[0:n, g, :], xn[0:n, g, :], 0).then_inc(dv_xhat, 1)

            embedded(0)
            embedded(1)
            xhat(0)
            embedded(2)
            xhat(1)

            def features(g):
                t0, n, _ = group(g)
                src = ps[2][0:n, 0:2 * D]
                ve.wait_ge(pe_qk, g + 1)
                if g >= 1:
                    ve.wait_ge(ac_exp, g)
                ve.tensor_scalar(qkmin[0:n, :], src, 0.0, None, ALU.min).then_inc(dv_min, 1)
                ve.wait_ge(ac_exp, g + 1)
                if g >= 2:
                    ve.wait_ge(dv_queries, g - 1)
                if g >= KS:
                    ve.wait_ge(pe_keys_values, 4 * (g - KS + 1))
                link(ve.scalar_tensor_tensor(qtok[0:n, g % 2, :], src[:, 0:D], 0.0, qkexp[0:n, 0:D], ALU.max, ALU.add))
                ve.scalar_tensor_tensor(ktok[0:n, g % KS, :], src[:, D:2 * D], 0.0, qkexp[0:n, D:2 * D],
                                        ALU.max, ALU.add).then_inc(dv_features, 1)

            def scaled_queries(g):
                t0, n, _ = group(g)
                ve.tensor_tensor(prod[0:n, 2, :], qtok[0:n, g % 2, :], aqs[0:n, :], ALU.mult).then_inc(dv, 1)
                links[0] += 1
                ve.wait_ge(pe_key_sums, g + 1)
                ve.tensor_tensor(prod[0:n, 0:2, :], ps[4][0:n, 0:2 * D].rearrange("p (a c) -> p a c", a=2),
                                 qtok[0:n, g % 2, :].unsqueeze(1).broadcast_to([n, 2, D]), ALU.mult).then_inc(dv_key_sums, 1)
                ve.wait_ge(dv, links[0])
                ve.wait_ge(dv_key_sums, g + 1)
                link(ve.tensor_reduce(den[0:n], prod[0:n].rearrange("p a (h d) -> p a h d", d=HD), AX.X, ALU.add))
                link(ve.tensor_scalar(den[0:n], den[0:n], EPS_DEN, None, ALU.max))
                link(ve.reciprocal(den[0:n], den[0:n]))
                link(ve.tensor_tensor(den[0:n], den[0:n], wvn[0:n, 0:3].unsqueeze(2).broadcast_to([n, 3, HEADS]), ALU.mult))
                if g >= 2:
                    ve.wait_ge(pe_queries_turned, 2 * (g - 1))
                ve.tensor_tensor(qsc[0:n, g % 2].rearrange("p a (h d) -> p a h d", d=HD),
                                 qtok[0:n, g % 2, :].rearrange("p (h d) -> p h d", d=HD).unsqueeze(1).broadcast_to([n, 3, HEADS, HD]),
                                 den[0:n].unsqueeze(3).broadcast_to([n, 3, HEADS, HD]), ALU.mult).then_inc(dv_queries, 1)

            def image_key_sums(g):
                t0, n, imgs = group(g)
                ve.wait_ge(ac_keys_turned, g + 1)
                ve.tensor_reduce(ksum[:, g, :, 0:imgs], kT[:, g % 3, :, 0:n].rearrange("p i (b s) -> p i b s", s=SEQ),
                                 AX.X, ALU.add).then_inc(dv_image_sums, 1)

            def over_anchors(g):
                t0, n, imgs = group(g)
                r = reca[:, g % 2, :, 0:imgs]
                ve.wait_ge(pe_on_anchors, g + 1)
                link(ve.tensor_scalar(r, ps[0][0:HA, 256:256 + 2 * PER].rearrange("p (i b) -> p i b", i=2)[:, :, 0:imgs],
                                      EPS_DEN, None, ALU.max))
                link(ve.reciprocal(r, r))
                if g >= 2:
                    ve.wait_ge(pe_from_anchors, g - 1)
                for i in range(2):
                    ve.tensor_tensor(qas[:, g % 2, i, 0:n].rearrange("p (b s) -> p b s", s=SEQ),
                                     ps[0][0:HA, i * GTOK:i * GTOK + n].rearrange("p (b s) -> p b s", s=SEQ),
                                     r[:, i, :].unsqueeze(2).broadcast_to([HA, imgs, SEQ]), ALU.mult).then_inc(dv_anchored, 1)

            def own_blocks(g, m):
                t0, n, imgs = group(g)
                if g >= 2:
                    ve.wait_ge(pe_heads, g - 1)
                ve.wait_ge(pe_keys_values, 4 * g + m + 1)
                i, kind = m // 2, m % 2
                ve.tensor_tensor(kvb[:, g % 2, i, kind * PER:kind * PER + imgs, :],
                                 ps[5][0:HALF, 0:imgs * HALF].rearrange("p (b c) -> p b c", c=HALF),
                                 blk.unsqueeze(1).broadcast_to([HALF, imgs, HALF]), ALU.mult).then_inc(dv_keys_values, 1)

            def windows(g, m):
                t0, n, _ = group(g)
                ve.wait_ge(pe_scores, 4 * g + m + 1)
                ve.tensor_tensor(at[0:n, g % 2, 3 * m:3 * m + 3, 0:n],
                                 ps[6][0:n, 0:3 * n].rearrange("p (a s) -> p a s", a=3),
                                 band[0:n, 0:n].unsqueeze(1).broadcast_to([n, 3, n]), ALU.mult).then_inc(dv_windows, 1)

            def residual(g):
                t0, n, _ = group(g)
                ve.wait_ge(pe_projected, g + 1)
                ve.tensor_tensor(h[0:n, g, :], ps[0][0:n, 0:D], h[0:n, g, :], ALU.add).then_inc(dv_h2, 1)
                ve.wait_ge(dv_h2, g + 1)
                moments(g, n, h[0:n, g, :])

            def tokens_out(g):
                n = group(g)[1]
                normalise(g, n, h[0:n, g, :], row[0:n, g, 0, 0:D], 1).then_inc(dv_x2, 1)

            def take_logits(g):
                n = group(g)[1]
                ve.wait_ge(pe_logits, g + 1)
                ve.tensor_copy(pair[0:n, g, 0, :], ps[1][0:n, 256:256 + E]).then_inc(dv_logits, 1)

            def take_places(g):
                n = group(g)[1]
                ve.wait_ge(pe_places, g + 1)
                ve.tensor_tensor(pair[0:n, g, 1, :], ps[4][0:n, 0:E], const("region")[0:n, :], ALU.add).then_inc(dv_places, 1)

            def route(g):
                ve.wait_ge(dv_logits, g + 1)
                t0, n, _ = group(g)
                mine = pair[0:n, g, 0, :].unsqueeze(2).broadcast_to([n, E, E])
                other = pair[0:n, g, 0, :].unsqueeze(1).broadcast_to([n, E, E])
                link(ve.tensor_tensor(cmpa[0:n], other, mine, ALU.is_equal))
                link(ve.tensor_tensor(cmpb[0:n], cmpa[0:n], tri[0:n].rearrange("p (a b) -> p a b", a=E), ALU.mult))
                link(ve.tensor_tensor(cmpa[0:n], other, mine, ALU.is_gt))
                link(ve.tensor_tensor(cmpb[0:n], cmpb[0:n], cmpa[0:n], ALU.add))
                link(ve.tensor_reduce(rank[0:n], cmpb[0:n], AX.X, ALU.add))
                ve.tensor_scalar(both[0:n, g, :], rank[0:n], float(TOP), None, ALU.is_lt).then_inc(dv_both, 1)
                for k in range(TOP):
                    link(ve.tensor_scalar(sel[0:n, g, k, :], rank[0:n], float(k), None, ALU.is_equal))
                ve.wait_ge(dv_both, 2 * g + 1)
                ve.tensor_tensor(run[:, g + 1, :], run[:, g, :], both[:, g, :], ALU.add).then_inc(dv_both, 1)
                ve.wait_ge(dv_both, 2 * g + 2)
                link(ve.tensor_tensor(pick[0:n], sel[0:n, g], pair[0:n, g, 0:1, :].broadcast_to([n, TOP, E]), ALU.mult))
                link(ve.tensor_reduce(best[0:n, g, :], pick[0:n], AX.X, ALU.add))
                ve.tensor_tensor(diff[0:n, g, 0:1], best[0:n, g, 1:2], best[0:n, g, 0:1], ALU.subtract).then_inc(dv_diff, 1)
                ve.wait_ge(dv_diff, g + 1)

            def send(g):
                t0, n, _ = group(g)
                ve.wait_ge(dv_places, g + 1)
                link(ve.tensor_tensor(pick[0:n], sel[0:n, g], pair[0:n, g, 1:2, :].broadcast_to([n, TOP, E]), ALU.mult))
                link(ve.tensor_reduce(place[0:n, :], pick[0:n], AX.X, ALU.add))
                link(ve.tensor_copy(index[0:n, g, :], place[0:n, :]))
                ve.wait_ge(ac_weight_exp, g + 1)
                link(ve.tensor_scalar(diff[0:n, g, 2:3], diff[0:n, g, 1:2], 1.0, None, ALU.add))
                link(ve.reciprocal(row[0:n, g, 0, D:D + 1], diff[0:n, g, 2:3]))
                ve.wait_ge(gp_row, g + 1)
                link(ve.tensor_tensor(row[0:n, g, 1, D:D + 1], row[0:n, g, 0, D:D + 1], diff[0:n, g, 1:2], ALU.mult))
                ve.tensor_copy(row[0:n, g, :, D + 1].bitcast(U32),
                               const("number")[0:n, g:g + 1].broadcast_to([n, TOP])).then_inc(dv_row, 1)
                ve.wait_ge(dv_row, g + 1)
                link(ve.tensor_scalar(pick[0:n, 0, :], sel[0:n, g, 0, :], row[0:n, g, 0, D:D + 1], None, ALU.mult))
                ve.scalar_tensor_tensor(comb[0:n, g, :], sel[0:n, g, 1, :], row[0:n, g, 1, D:D + 1], pick[0:n, 0, :],
                                        ALU.mult, ALU.add).then_inc(dv_combine, 1)
                ve.wait_ge(dv_combine, g + 1)

            ve.wait_ge(gp_route_zero, 2)
            ve.wait_ge(consts_in, 16)
            ve.wait_ge(gp_ktok_one, 1)
            turning_over(ve)
            ve.wait_ge(ac_anchor_sum, 1)
            for t in range(GROUPS + 5):
                if t == 3:
                    embedding_over(ve)
                for m in range(4):
                    if 0 <= t - 3 < GROUPS:
                        own_blocks(t - 3, m)
                        windows(t - 3, m)
                    if m == 0:
                        if 0 <= t - 3 < GROUPS:
                            over_anchors(t - 3)
                        if t == 3:
                            xhat(5)
                        if 0 <= t - 5 < GROUPS - 2:
                            tokens_out(t - 5)
                    if m == (1 if t == 3 else 0) and 0 <= t - 1 < GROUPS:
                        scaled_queries(t - 1)
                        image_key_sums(t - 1)
                    if m == 1 and 0 <= t - 6 < GROUPS - 3:
                        route(t - 6)
                    if m == 1 and 0 <= t - 7 < GROUPS - 4:
                        send(t - 7)
                if t == GROUPS + 3:
                    take_places(GROUPS - 3)
                    send(GROUPS - 3)
                    take_logits(GROUPS - 2)
                if 0 <= t - 4 < GROUPS:
                    residual(t - 4)
                if t == GROUPS + 3:
                    tokens_out(GROUPS - 1)
                    route(GROUPS - 2)
                if 0 <= t - 5 < GROUPS - 2:
                    take_logits(t - 5)
                if 0 <= t - 6 < GROUPS - 3:
                    take_places(t - 6)
                if t == GROUPS + 2:
                    tokens_out(GROUPS - 2)
                    route(GROUPS - 3)
                    send(GROUPS - 4)
                if t < GROUPS:
                    features(t)
                if 1 <= t < GROUPS - 3:
                    embedded(t + 3)
                if t < 3:
                    xhat(t + 2)
                if t == 0:
                    embedded(3)
            take_logits(GROUPS - 1)
            route(GROUPS - 1)
            take_places(GROUPS - 2)
            send(GROUPS - 2)
            take_places(GROUPS - 1)
            send(GROUPS - 1)
            attention_over(ve)
            for s in range(2):
                link(ve.tensor_copy(xhi[HALF:HALF + 1, s, 1, :], ones[HALF:HALF + 1, :]))
                link(ve.tensor_scalar(xlo[HALF:HALF + 1, s, 1, :], ones[HALF:HALF + 1, :], 0.0, None, ALU.mult))

            def weights_low(e):
                ve.wait_ge(ac_w1_high, e + 1)
                ve.tensor_tensor(w1lo[:, e], w1s[:, e], w1hi[:, e].bitcast(F32), ALU.subtract).then_inc(dv_w1_low, 1)

            ve.wait_ge(pe_counts, 1)
            ve.tensor_copy(counts[:], ps[0][0:1, 0:E]).then_inc(dv_count, 1)
            weights_low(DV_SPLITS[0])
            ve.wait_ge(dv_count, 1)
            count, start, end, rest = (tiles[:, k, :] for k in range(4))
            link(ve.tensor_tensor(full[:], counts[:].unsqueeze(2).broadcast_to([1, E, REGION - 1]),
                                  const("full").rearrange("p (e r) -> p e r", e=E), ALU.is_gt))
            link(ve.tensor_reduce(count, full[:], AX.X, ALU.add))
            link(ve.tensor_tensor(ge[:, 0, 0:E, :], count.unsqueeze(1).broadcast_to([1, E, E]),
                                  tri[0:1].rearrange("p (a b) -> p a b", a=E), ALU.mult))
            link(ve.tensor_reduce(start, ge[:, 0, 0:E, :], AX.X, ALU.add))
            link(ve.tensor_tensor(end, start, count, ALU.add))
            link(ve.tensor_scalar(rest, count, -1.0, float(REGION), ALU.mult, ALU.add))
            number = const("tile").rearrange("p (j e) -> p j e", e=E)
            link(ve.tensor_tensor(ge[:, 0], number, end.unsqueeze(1).broadcast_to([1, EXTRA, E]), ALU.is_ge))
            link(ve.tensor_tensor(ge[:, 1], ge[:, 0], rest.unsqueeze(1).broadcast_to([1, EXTRA, E]), ALU.mult))
            link(ve.tensor_reduce(tabf[:], ge[:], AX.X, ALU.add))
            link(ve.tensor_tensor(tabf[:, 1, :], tabf[:, 1, :], number[:, :, 0], ALU.add))
            link(ve.tensor_scalar(tabf[:, 0, :], tabf[:, 0, :], float(E - 1), None, ALU.min))
            link(ve.tensor_scalar(tabf[:, 1, :], tabf[:, 1, :], 1.0, float(EMPTY), ALU.add, ALU.min))
            ve.tensor_copy(tab[:], tabf[:]).then_inc(dv_tab, 1)

            def tokens_low(j):
                ve.wait_ge(ac_x_high, j + 1)
                if j >= 2:
                    ve.wait_ge(pe_hidden, 2 * (j - 1))
                ve.tensor_tensor(xlo[0:HALF, j % 2], ps[j % 2][0:HALF, 0:2 * SLOTS].rearrange("p (i t) -> p i t", i=2),
                                 xhi[0:HALF, j % 2].bitcast(F32), ALU.subtract).then_inc(dv_x_low, 1)

            tokens_low(0)
            tokens_low(1)
            for g in range(GROUPS):
                t0, n, _ = group(g)
                ve.wait_ge(pe_out_bias, 2 * (g // 2) + 2)
                ve.tensor_tensor(first[0:n, g, :], ps[(6, 7, 4)[g // 2]][0:n, (g % 2) * 256:(g % 2) * 256 + D],
                                 h[0:n, g, :], ALU.add).then_inc(dv_first, 1)
            for j in range(TILES):
                ve.wait_ge(pe_hidden, 2 * j + 2)
                if j >= 1:
                    ve.wait_ge(pe_hidden_turned, 2 * j)
                ve.tensor_scalar(hid[:, PASS:DF], ps[3][:, 0:PASS], 0.0, None, ALU.max).then_inc(dv_hidden, 1)
                if j + 2 < TILES:
                    tokens_low(j + 2)
                ve.wait_ge(pe_hidden_turned, 2 * j + 2)
                if j >= 1:
                    ve.wait_ge(pe_answers, j)
                ve.tensor_copy(hidT[:, 3:6, :].rearrange("p k t -> p (k t)"), ps[5][:, 0:PASS]).then_inc(dv_hidden_turned, 1)
                if j + 1 < len(DV_SPLITS):
                    weights_low(DV_SPLITS[j + 1])

        @block.scalar
        def _(ac):
            ac.dma_start(cst[:, 0:128], consts[:, 0:128]).then_inc(ident_in, 16)
            ac.wait_ge(gp_class_zero, 1)
            for c in range(CH):
                ac.wait_ge(x_in[c], 16 * GRID)
                ac.activation(patch_rows(c, 1), image_rows(c, 1), ACT.Copy).then_inc(ac_patch_rows, 1)
                for k in (2 * c, 2 * c + 1):
                    ac.wait_ge(pe_patch_turned, 2 * k + 2)
                    ac.activation(patches_of(1, k), turned(2 * k + 1), ACT.Copy).then_inc(ac_patches, 1)
            ac.wait_ge(dv_band_diff, 1)
            ac.activation(wv[:, 0:3], wvn[:, 0:3], ACT.Exp).then_inc(ac_band_exp, 1)
            ac.wait_ge(dv_anchors, 1)
            ac.activation(anc[2][:], anc[1][:], ACT.Exp).then_inc(ac_anchor_exp, 1)
            ac.wait_ge(pe_base, 1)
            ac.activation(hbase[:], ps[5][0:GTOK, 0:D], ACT.Copy).then_inc(ac_base, 1)
            ac.wait_ge(gp_eps, 1)

            def root(g, layer):
                t0, n, _ = group(g)
                ac.wait_ge(dv_moments, GROUPS * layer + g + 1)
                ac.activation(rstd[0:n, g:g + 1], mv[0:n, g, 1:2], ACT.Sqrt, bias=epsv[0:n, :]).then_inc(ac_root, 1)

            def xhat_out(g):
                t0, n, _ = group(g)
                ac.wait_ge(pe_xhat_turned, g + 1)
                ac.activation(xhT[:, :, t0:t0 + n],
                              xhat_bank(g)[0:HALF, 0:2 * GTOK].rearrange("p (i t) -> p i t", i=2)[:, :, 0:n],
                              ACT.Copy).then_inc(ac_xhat_turned, 1)

            root(0, 0)
            root(1, 0)
            for m in range(4):
                i, r3 = m // 2, m % 2
                ac.wait_ge(pe_weights_turned, m + 1)
                ac.activation(wT[:, i, 288 * r3:288 * (r3 + 1)], ps[2 + m][0:HALF, 0:288], ACT.Copy).then_inc(ac_weights, 1)
            xhat_out(0)
            root(2, 0)
            ac.wait_ge(pe_weights_turned, 5)
            ac.activation(woT[:].rearrange("p i c -> p (i c)"), ps[4][0:HALF, 0:2 * D], ACT.Copy).then_inc(ac_weights, 1)
            ac.wait_ge(pe_weights_turned, 6)
            ac.activation(aqs[:], ps[5][0:GTOK, 160:160 + D], ACT.Copy).then_inc(ac_anchor_sum, 1)
            ac.activation(aq[:].rearrange("p i c -> p (i c)"), ps[5][0:HALF, 0:2 * HA], ACT.Copy).then_inc(ac_weights, 1)
            xhat_out(1)

            def heads_out(g):
                t0, n, _ = group(g)
                ac.wait_ge(pe_heads, g + 1)
                if g >= 2:
                    ac.wait_ge(pe_projected, g - 1)
                ac.activation(oT[:, g % 2, :, 0:n],
                              ps[7][0:HALF, 0:2 * GTOK].rearrange("p (i t) -> p i t", i=2)[:, :, 0:n], ACT.Copy).then_inc(ac_heads, 1)

            def spread(g):
                t0, n, imgs = group(g)
                ac.wait_ge(pe_queries_turned, 2 * g + 1)
                if g >= 2:
                    ac.wait_ge(pe_scores, 4 * (g - 1))
                turned_q = ps[2][0:HALF, 0:2 * GTOK].rearrange("p (i t) -> p i t", i=2)[:, :, 0:n]
                for hh in range(HH):
                    ins = ac.activation(qlb[:, g % 2, :, hh, 0:n], turned_q, ACT.Copy, scale=blk[:, hh * HD:hh * HD + 1])
                ins.then_inc(ac_local_queries, 1)
                if g >= 2:
                    ac.wait_ge(pe_heads, g - 1)
                ac.activation(own_columns(g, 0, imgs), by_image(ps[2][0:HALF, 2 * GTOK:4 * GTOK], n, imgs), ACT.Copy).then_inc(ac_strided_queries, 1)
                ac.wait_ge(pe_queries_turned, 2 * g + 2)
                if g >= 2:
                    ac.wait_ge(pe_on_anchors, g - 1)
                ac.activation(qgT[:, g % 2, :, 0:n],
                              ps[1][0:HALF, 0:2 * GTOK].rearrange("p (i t) -> p i t", i=2)[:, :, 0:n], ACT.Copy).then_inc(ac_global_queries, 1)

            def weight(g):
                t0, n, _ = group(g)
                ac.wait_ge(dv_diff, g + 1)
                ac.activation(diff[0:n, g, 1:2], diff[0:n, g, 0:1], ACT.Exp).then_inc(ac_weight_exp, 1)

            def x2_out(g):
                t0, n, _ = group(g)
                ac.wait_ge(pe_x2_turned, g + 1)
                if g >= 2:
                    ac.wait_ge(pe_logits, g - 1)
                ac.activation(x2T[:, g % 2, :, 0:n],
                              ps[1][0:HALF, 0:2 * GTOK].rearrange("p (i t) -> p i t", i=2)[:, :, 0:n],
                              ACT.Copy).then_inc(ac_x2_turned, 1)

            ac.wait_ge(gp_qx_zero, 1)
            turning_over(ac)

            def combine_out(c):
                lo, hi = 4 * c * GTOK, (4 * GTOK, TOK)[c]
                ac.wait_ge(pe_combine_turned, c + 1)
                ac.activation(cT[:, lo:hi], ps[5][0:E, 0:hi - lo], ACT.Copy).then_inc(ac_combine_turned, 1)

            def weights_high(e):
                ac.activation(w1hi[:, e], w1s[:, e], ACT.Copy).then_inc(ac_w1_high, 1)

            for t in range(GROUPS + 5):
                if 0 <= t - 1 < GROUPS:
                    t0, n, _ = group(t - 1)
                    ac.wait_ge(pe_keys_turned, t)
                    if t - 1 >= 3:
                        ac.wait_ge(pe_scores, 4 * (t - 3))
                    ac.activation(kT[:, (t - 1) % 3, :, 0:n],
                                  ps[3][0:HALF, 0:2 * GTOK].rearrange("p (i t) -> p i t", i=2)[:, :, 0:n], ACT.Copy).then_inc(ac_keys_turned, 1)
                if 1 <= t < 4:
                    xhat_out(t + 1)
                if 0 <= t - 2 < GROUPS:
                    spread(t - 2)
                if t == 3:
                    xhat_out(5)
                if t == GROUPS + 3:
                    weight(GROUPS - 3)
                    x2_out(GROUPS - 2)
                if 0 <= t - 4 < GROUPS:
                    heads_out(t - 4)
                if t == GROUPS + 3:
                    attention_over(ac)
                    ac.wait_ge(w1_in, 16 * (E + 1))
                    ac.wait_ge(gp_bias_zero, 1)
                    weights_high(0)
                    root(GROUPS - 1, 1)
                    x2_out(GROUPS - 1)
                    weight(GROUPS - 2)
                    combine_out(0)
                if 0 <= t - 5 < GROUPS - 2:
                    x2_out(t - 5)
                if 0 <= t - 3 < GROUPS:
                    g = t - 3
                    t0, n, imgs = group(g)
                    ac.wait_ge(pe_from_anchors, g + 1)
                    if g >= 2:
                        ac.wait_ge(pe_heads, g - 1)
                    ac.activation(own_columns(g, 1, imgs), by_image(ps[0][0:HALF, 0:2 * GTOK], n, imgs), ACT.Copy).then_inc(ac_from_anchors, 1)
                if 0 <= t - 6 < GROUPS - 3:
                    weight(t - 6)
                if t < GROUPS:
                    t0, n, _ = group(t)
                    ac.wait_ge(dv_min, t + 1)
                    if t >= 1:
                        ac.wait_ge(dv_features, t)
                    ac.activation(qkexp[0:n, :], qkmin[0:n, :], ACT.Exp).then_inc(ac_exp, 1)
                    ac.wait_ge(pe_v, t + 1)
                    if t >= 3:
                        ac.wait_ge(gp_head_values, HH * (t - 2))
                    ac.activation(vtok[0:n, t % 3, :], ps[3][0:n, 0:D], ACT.Copy).then_inc(ac_v, 1)
                if t + 3 < GROUPS:
                    root(t + 3, 0)
                if 0 <= t - 4 < GROUPS - 1:
                    root(t - 4, 1)
                if t >= GROUPS + 3:
                    weights_high(t - GROUPS - 2)
            weight(GROUPS - 1)
            weights_high(3)
            weights_high(4)
            combine_out(1)

            def tokens_high(j):
                ac.wait_ge(pe_tile_turned, j + 1)
                if j >= 2:
                    ac.wait_ge(pe_hidden, 2 * (j - 1))
                ac.activation(xhi[0:HALF, j % 2], ps[j % 2][0:HALF, 0:2 * SLOTS].rearrange("p (i t) -> p i t", i=2),
                              ACT.Copy).then_inc(ac_x_high, 1)

            def weigh(j):
                ac.wait_ge(pe_answers, j + 1)
                if j >= 2:
                    ac.wait_ge(added, 16 * (j - 1))
                ac.activation(ys[:, j % 2, :], ps[6 + j % 2][:, 0:D], ACT.Copy,
                              scale=xs[:, j % NS, D:D + 1]).then_inc(ac_answers, 1)

            weights_high(5)
            tokens_high(0)
            tokens_high(1)
            weights_high(6)
            weights_high(7)
            for j in range(TILES):
                ac.wait_ge(pe_hidden, 2 * j + 1)
                if j >= 1:
                    ac.wait_ge(pe_hidden_turned, 2 * j - 1)
                ac.activation(hid[:, 0:PASS], ps[2][:, 0:PASS], ACT.Relu).then_inc(ac_hidden, 1)
                if j >= 1:
                    weigh(j - 1)
                if j + 2 < TILES:
                    tokens_high(j + 2)
                ac.wait_ge(pe_hidden_turned, 2 * j + 1)
                if j >= 1:
                    ac.wait_ge(pe_answers, j)
                ac.activation(hidT[:, 0:3, :].rearrange("p k t -> p (k t)"), ps[4][:, 0:PASS], ACT.Copy).then_inc(ac_hidden_turned, 1)
            weigh(TILES - 1)

        @block.gpsimd
        def _(po):
            linked = {}
            for k, w in enumerate((w_loc, w_str, w_glo)):
                po.dma_start(wv[:, k:k + 1], w.partition_broadcast(GTOK)).then_inc(wv_in, 16)
            for i in range(2):
                po.dma_start(anc[0][:, i, :], anchor_q.rearrange("o a (b d) -> (o a b) d", d=HD)[i * HA:(i + 1) * HA, :]).then_inc(anc_in, 16)

            def link(ins, signal=gp):
                linked[id(signal)] = linked.get(id(signal), 0) + 1
                ins.then_inc(signal, 1)
                po.wait_ge(signal, linked[id(signal)])

            link(po.memset(ones[:], 1.0), gp_one)
            link(po.memset(xT[:].rearrange("p k (b s) -> p k b s", s=SEQ)[:, :, :, 0:2], 0.0), gp_class_zero)
            link(po.memset(posb[0:1, :], 0.0), gp_posb_zero)
            link(po.memset(epsv[:], EPS_LN), gp_eps)
            po.wait_ge(dv_anchors, 2)
            po.wait_ge(consts_in, 16)
            for i in range(2):
                link(po.tensor_tensor(aqT[:, i], anc[3][:, i, :].unsqueeze(1).broadcast_to([HA, HH, HD]),
                                      ablk.rearrange("p (a d) -> p a d", d=HD), ALU.mult), gp_anchors)
            link(po.memset(ktok[96:GTOK + 1], 1.0), gp_ktok_one)
            link(po.memset(blank[:, 0:D + 1], 0.0))
            link(po.tensor_copy(blank[:, D + 1:ROW].bitcast(U32), const("number")[:, GROUPS:GROUPS + 1]), gp_blank)
            link(po.memset(qx[:], 0.0), gp_qx_zero)
            link(po.tensor_copy(own[:], const("expert")), gp_own)
            link(po.memset(both[:], 0.0), gp_route_zero)
            link(po.memset(run[:, 0, :], 0.0), gp_route_zero)
            link(po.memset(w1s[HALF:HALF + 1, :, 0, :], 0.0), gp_bias_zero)

            def copy_row(g):
                n = group(g)[1]
                po.wait_ge(dv_x2, g + 1)
                link(po.tensor_copy(row[0:n, g, 1, 0:D], row[0:n, g, 0, 0:D]), gp_row)

            def weights_low(e):
                po.wait_ge(ac_w1_high, e + 1)
                link(po.tensor_tensor(w1lo[:, e], w1s[:, e], w1hi[:, e].bitcast(F32), ALU.subtract), gp_w1_low)

            def scatter(g):
                n = group(g)[1]
                po.wait_ge(dv_row, g + 1)
                for k in range(TOP):
                    po.indirect_dma_start(sent.rearrange("r p c -> (r p) c"),
                                          bass.IndirectOffsetOnAxis(ap=index[0:n, g, k:k + 1], axis=0),
                                          row[0:n, g, k, :], None).then_inc(sent_in, 16)

            turning_over(po)
            for g in range(GROUPS):
                t0, n, imgs = group(g)
                if g >= 4:
                    copy_row(g - 4)
                po.wait_ge(ac_v, g + 1)
                if g >= 2:
                    po.wait_ge(pe_keys_values, 4 * (g - 1))
                for i in range(2):
                    v = vtok[0:n, g % 3, i * HALF:(i + 1) * HALF]
                    link(po.tensor_tensor(vm[0:n, g % 2, i], v.unsqueeze(1).broadcast_to([n, 2 * PER, HALF]),
                                          vmask[0:n, :].unsqueeze(2).broadcast_to([n, 2 * PER, HALF]), ALU.mult), gp_masked_values)
                if g == 0:
                    embedding_over(po)
                    link(po.memset(vexp[:], 0.0), gp_vexp_zero)
                if g >= 2:
                    po.wait_ge(pe_heads, g - 1)
                for hh in range(HH):
                    link(po.tensor_copy(
                        vexp[0:n, g % 2].rearrange("p (i a) c -> p i a c", i=2)[:, :, hh, hh * HD:(hh + 1) * HD],
                        vtok[0:n, g % 3].rearrange("p (i c) -> p i c", i=2)[:, :, hh * HD:(hh + 1) * HD]), gp_head_values)
            po.wait_ge(sent_blank, 16)
            for g in range(GROUPS - 4, GROUPS + 2):
                if g == GROUPS - 1:
                    weights_low(GP_SPLITS[0])
                if g < GROUPS:
                    copy_row(g)
                scatter(g - 2)
            for e in GP_SPLITS[1:]:
                weights_low(e)
            po.wait_ge(sums_in, 16 * (GROUPS + 1))
            for j in range(TILES):
                po.wait_ge(ac_answers, j + 1)
                if j >= 1:
                    po.wait_ge(added, 16 * j)
                po.indirect_dma_start(sums, bass.IndirectOffsetOnAxis(ap=xs[:, j % NS, D + 1:ROW].bitcast(U32), axis=0),
                                      ys[:, j % 2, :], None, compute_op=ALU.add).then_inc(added, 16)
            po.wait_ge(added, 16 * TILES)


_INS = ["x", "cls_tok", "L0_tok_W_emb", "L0_tok_b_emb", "L0_tok_pos_embedding", "L0_tok_cls_token",
        "L0_attn_qkv_w", "L0_attn_out_w", "L0_attn_anchor_q", "L0_attn_w_local", "L0_attn_w_stride",
        "L0_attn_w_global", "L0_ffn_Wg", "L0_ffn_W1", "L0_ffn_b1", "L0_ffn_W2", "L0_ffn_b2"]


def kernel(**inputs):
    import concourse.bacc as bacc
    from concourse.bass_utils import run_bass_kernel_spmd

    nc = bacc.Bacc("TRN2", target_bir_lowering=False, num_devices=1)
    arrays, args = {}, []
    for name in _INS:
        a = np.ascontiguousarray(inputs[name])
        arrays[f"in_{name}"] = a
        args.append(nc.dram_tensor(f"in_{name}", a.shape, mybir.dt.from_np(a.dtype), kind="ExternalInput").ap())
    arrays["in_constants"] = constants()
    args.append(nc.dram_tensor("in_constants", (128, CONST_COLS), F32, kind="ExternalInput").ap())
    args.append(nc.dram_tensor("out", (IMAGES, SEQ, D), F32, kind="ExternalOutput").ap())
    build(nc, *args)
    r = run_bass_kernel_spmd(nc, [arrays], core_ids=[0])
    return r.results[0]["out"]
```
